# Optimizing a Trainium2 kernel written in Bass

```python
import numpy as np
import jax
import jax.numpy as jnp

def _softmax(x, axis=-1):
    return jax.nn.softmax(x, axis=axis)

def _gelu(x):
    return jax.nn.gelu(x, approximate=True)

def _silu(x):
    return jax.nn.silu(x)

def _sigmoid(x):
    return jax.nn.sigmoid(x)

def _layernorm(x, axis=-1, eps=1e-05):
    m = jnp.mean(x, axis=axis, keepdims=True)
    v = jnp.var(x, axis=axis, keepdims=True)
    return (x - m) / jnp.sqrt(v + eps)

def _scatter_add(tgt, idx, src, axis=0):
    return tgt.at[idx].add(src)

def _segment_sum(src, seg, n):
    return jax.ops.segment_sum(src, seg, n)
kernel_name = 'mk_gnn_preln_d4_gnn_r8_f90d67'

def setup_inputs(seed: int=0):
    np.random.seed(seed)
    _w = jnp.asarray

    def _rec_inputs():
        import jax
        import jax.numpy as jnp
        _gk = jax.random.key(seed)
        x = -0.000202 + 1 * jax.random.normal(jax.random.fold_in(_gk, 1), (6250, 128), jnp.float32)
        src = jax.random.randint(jax.random.fold_in(_gk, 2), (100000,), 0, 6250, jnp.int32)
        dst = jax.random.randint(jax.random.fold_in(_gk, 3), (100000,), 0, 6250, jnp.int32)
        _o = jnp.argsort(dst, stable=True)
        src = src[_o]
        dst = dst[_o]
        edge_type_32 = jax.random.randint(jax.random.fold_in(_gk, 13), (100000,), 0, 32, jnp.int32)
        edge_weight1 = jax.random.uniform(jax.random.fold_in(_gk, 14), (100000, 1), jnp.float32, 0.0, 0.999998)
        return (x, src, dst, edge_type_32, edge_weight1)
    x, src, dst, edge_type_32, edge_weight1 = _rec_inputs()

    def _L0_gnn_setup():
        import jax, jax.numpy as jnp
        import numpy as np
        N_NODES = 6250
        N_EDGES = 100000
        IN_FEATS = 128
        OUT_FEATS = 128
        FREQ_DIM = OUT_FEATS // 2 + 1
        BN_EPS = 1e-05
        key = jax.random.key(seed)
        ks = jax.random.split(key, 8)
        x = jax.random.normal(ks[0], (N_NODES, IN_FEATS), dtype=jnp.float32)
        edge_index = jax.random.randint(ks[1], (2, N_EDGES), 0, N_NODES, dtype=jnp.int64)
        W_fuse = jax.random.normal(ks[2], (OUT_FEATS, 2 * IN_FEATS), dtype=jnp.float32) * (1.0 / np.sqrt(2 * IN_FEATS))
        b_fuse = jnp.zeros((OUT_FEATS,), dtype=jnp.float32)
        W_in = jax.random.normal(ks[3], (OUT_FEATS, IN_FEATS), dtype=jnp.float32) * (1.0 / np.sqrt(IN_FEATS))
        b_in = jnp.zeros((OUT_FEATS,), dtype=jnp.float32)
        complex_weight = jax.random.normal(ks[4], (FREQ_DIM, 2), dtype=jnp.float32) * 0.02
        alpha = jnp.float32(0.5)
        gamma = jnp.ones((OUT_FEATS,), dtype=jnp.float32)
        beta = jnp.zeros((OUT_FEATS,), dtype=jnp.float32)
        return {'x': x, 'edge_index': edge_index, 'W_fuse': W_fuse, 'b_fuse': b_fuse, 'W_in': W_in, 'b_in': b_in, 'complex_weight': complex_weight, 'alpha': alpha, 'gamma': gamma, 'beta': beta}
    _L0_gnn_all = _L0_gnn_setup()
    _L0_gnn_in = {k: v for k, v in _L0_gnn_all.items() if k in ('W_fuse', 'b_fuse', 'W_in', 'b_in', 'complex_weight', 'alpha', 'gamma', 'beta')}
    del _L0_gnn_all

    def _L1_gnn_setup():
        import jax, jax.numpy as jnp
        import numpy as np
        N_NODES = 6250
        N_EDGES = 62500
        IN_FEAT = 128
        OUT_FEAT = 128
        NUM_RELS = 32
        NUM_BASES = 8
        key = jax.random.key(seed)
        ks = jax.random.split(key, 8)
        h = jax.random.normal(ks[0], (N_NODES, IN_FEAT), dtype=jnp.float32)
        src = jax.random.randint(ks[1], (N_EDGES,), 0, N_NODES, dtype=jnp.int32)
        dst = jax.random.randint(ks[2], (N_EDGES,), 0, N_NODES, dtype=jnp.int32)
        etype = jax.random.randint(ks[3], (N_EDGES,), 0, NUM_RELS, dtype=jnp.int32)
        norm = jax.random.uniform(ks[4], (N_EDGES, 1), dtype=jnp.float32)
        weight = jax.random.normal(ks[5], (NUM_BASES, IN_FEAT, OUT_FEAT), dtype=jnp.float32) * 0.05
        w_comp = jax.random.normal(ks[6], (NUM_RELS, NUM_BASES), dtype=jnp.float32) * 0.3
        bias_param = jax.random.normal(ks[7], (OUT_FEAT,), dtype=jnp.float32) * 0.05
        return {'h': h, 'src': src, 'dst': dst, 'etype': etype, 'norm': norm, 'weight': weight, 'w_comp': w_comp, 'bias_param': bias_param}
    _L1_gnn_all = _L1_gnn_setup()
    _L1_gnn_in = {k: v for k, v in _L1_gnn_all.items() if k in ('weight', 'w_comp', 'bias_param')}
    del _L1_gnn_all

    def _L2_gnn_setup():
        import jax, jax.numpy as jnp
        import numpy as np
        N = 12500
        E = 100000
        D = 128
        H = 8
        C = D // H
        FF = 512
        EPS = 1e-05
        NEG_SLOPE = 0.2

        def _layernorm(x, g, b):
            mu = jnp.mean(x, axis=-1, keepdims=True)
            var = jnp.mean(jnp.square(x - mu), axis=-1, keepdims=True)
            return (x - mu) * jax.lax.rsqrt(var + EPS) * g + b
        key = jax.random.key(seed)
        ks = jax.random.split(key, 10)
        x = jax.random.normal(ks[0], (N, D), dtype=jnp.float32)
        virtual_edge_index = jax.random.randint(ks[1], (2, E), 0, N, dtype=jnp.int64)
        s = 1.0 / np.sqrt(D)
        W_gat = jax.random.normal(ks[2], (D, H * C), dtype=jnp.float32) * s
        att_src = jax.random.normal(ks[3], (H, C), dtype=jnp.float32) * s
        att_dst = jax.random.normal(ks[4], (H, C), dtype=jnp.float32) * s
        b_gat = jnp.zeros((H * C,), dtype=jnp.float32)
        W1 = jax.random.normal(ks[5], (D, FF), dtype=jnp.float32) * s
        b1 = jnp.zeros((FF,), dtype=jnp.float32)
        W2 = jax.random.normal(ks[6], (FF, D), dtype=jnp.float32) * (1.0 / np.sqrt(FF))
        b2 = jnp.zeros((D,), dtype=jnp.float32)
        ln1_g = jnp.ones((D,), dtype=jnp.float32)
        ln1_b = jnp.zeros((D,), dtype=jnp.float32)
        ln2_g = jnp.ones((D,), dtype=jnp.float32)
        ln2_b = jnp.zeros((D,), dtype=jnp.float32)
        return {'x': x, 'virtual_edge_index': virtual_edge_index, 'W_gat': W_gat, 'att_src': att_src, 'att_dst': att_dst, 'b_gat': b_gat, 'W1': W1, 'b1': b1, 'W2': W2, 'b2': b2, 'ln1_g': ln1_g, 'ln1_b': ln1_b, 'ln2_g': ln2_g, 'ln2_b': ln2_b}
    _L2_gnn_all = _L2_gnn_setup()
    _L2_gnn_in = {k: v for k, v in _L2_gnn_all.items() if k in ('W_gat', 'att_src', 'att_dst', 'b_gat', 'W1', 'b1', 'W2', 'b2', 'ln1_g', 'ln1_b', 'ln2_g', 'ln2_b')}
    del _L2_gnn_all

    def _L3_gnn_setup():
        import jax, jax.numpy as jnp
        import numpy as np
        N_NODES = 12500
        N_EDGES = 400000
        D_FEAT = 128
        K = 10
        ALPHA = 0.1

        def _appnp(x, src, dst, norm, n_nodes):
            h = x

            def step(xk, _):
                msg = norm[:, None] * xk[src]
                agg = jax.ops.segment_sum(msg, dst, num_segments=n_nodes)
                return ((1.0 - ALPHA) * agg + ALPHA * h, None)
            xK, _ = jax.lax.scan(step, x, None, length=K)
            return xK
        key = jax.random.key(seed)
        k1, k2 = jax.random.split(key)
        x = jax.random.normal(k1, (N_NODES, D_FEAT), dtype=jnp.float32)
        edge_index = jax.random.randint(k2, (2, N_EDGES), 0, N_NODES, dtype=jnp.int64)
        return {'x': x, 'edge_index': edge_index}
    _L3_gnn_all = _L3_gnn_setup()
    _L3_gnn_in = {k: v for k, v in _L3_gnn_all.items() if k in ()}
    del _L3_gnn_all
    return {'x': x, 'src': src, 'dst': dst, 'edge_type_32': edge_type_32, 'edge_weight1': edge_weight1, 'L0_gnn_W_fuse': _L0_gnn_in['W_fuse'], 'L0_gnn_b_fuse': _L0_gnn_in['b_fuse'], 'L0_gnn_W_in': _L0_gnn_in['W_in'], 'L0_gnn_b_in': _L0_gnn_in['b_in'], 'L0_gnn_complex_weight': _L0_gnn_in['complex_weight'], 'L0_gnn_alpha': _L0_gnn_in['alpha'], 'L0_gnn_gamma': _L0_gnn_in['gamma'], 'L0_gnn_beta': _L0_gnn_in['beta'], 'L1_gnn_weight': _L1_gnn_in['weight'], 'L1_gnn_w_comp': _L1_gnn_in['w_comp'], 'L1_gnn_bias_param': _L1_gnn_in['bias_param'], 'L2_gnn_W_gat': _L2_gnn_in['W_gat'], 'L2_gnn_att_src': _L2_gnn_in['att_src'], 'L2_gnn_att_dst': _L2_gnn_in['att_dst'], 'L2_gnn_b_gat': _L2_gnn_in['b_gat'], 'L2_gnn_W1': _L2_gnn_in['W1'], 'L2_gnn_b1': _L2_gnn_in['b1'], 'L2_gnn_W2': _L2_gnn_in['W2'], 'L2_gnn_b2': _L2_gnn_in['b2'], 'L2_gnn_ln1_g': _L2_gnn_in['ln1_g'], 'L2_gnn_ln1_b': _L2_gnn_in['ln1_b'], 'L2_gnn_ln2_g': _L2_gnn_in['ln2_g'], 'L2_gnn_ln2_b': _L2_gnn_in['ln2_b']}

def reference(x, src, dst, edge_type_32, edge_weight1, L0_gnn_W_fuse, L0_gnn_b_fuse, L0_gnn_W_in, L0_gnn_b_in, L0_gnn_complex_weight, L0_gnn_alpha, L0_gnn_gamma, L0_gnn_beta, L1_gnn_weight, L1_gnn_w_comp, L1_gnn_bias_param, L2_gnn_W_gat, L2_gnn_att_src, L2_gnn_att_dst, L2_gnn_b_gat, L2_gnn_W1, L2_gnn_b1, L2_gnn_W2, L2_gnn_b2, L2_gnn_ln1_g, L2_gnn_ln1_b, L2_gnn_ln2_g, L2_gnn_ln2_b):
    import jax
    import jax.numpy as jnp

    def _L0_gnn_ref(x, edge_index, W_fuse, b_fuse, W_in, b_in, complex_weight, alpha, gamma, beta):
        import jax, jax.numpy as jnp
        import numpy as np
        N_NODES = 6250
        N_EDGES = 100000
        IN_FEATS = 128
        OUT_FEATS = 128
        FREQ_DIM = OUT_FEATS // 2 + 1
        BN_EPS = 1e-05
        N = x.shape[0]
        src, dst = (edge_index[0], edge_index[1])
        msgs = x[src]
        agg_sum = jax.ops.segment_sum(msgs, dst, num_segments=N)
        cnt = jax.ops.segment_sum(jnp.ones((src.shape[0],), dtype=x.dtype), dst, num_segments=N)
        aggs = agg_sum / jnp.maximum(cnt, 1.0)[:, None]
        combined = jnp.concatenate([x, aggs], axis=1)
        x_spatial = combined @ W_fuse.T + b_fuse
        h = x @ W_in.T + b_in
        hf = jnp.fft.rfft(h, axis=-1)
        w = complex_weight[:, 0] + 1j * complex_weight[:, 1]
        x_spectral = jnp.fft.irfft(hf * w, n=h.shape[-1], axis=-1).astype(x.dtype)
        out = x_spatial + alpha * x_spectral
        mean = jnp.mean(out, axis=0)
        var = jnp.mean(jnp.square(out - mean), axis=0)
        out = (out - mean) / jnp.sqrt(var + BN_EPS) * gamma + beta
        return jax.nn.gelu(out, approximate=False)

    def _L1_gnn_ref(h, src, dst, etype, norm, weight, w_comp, bias_param):
        import jax, jax.numpy as jnp
        import numpy as np
        N_NODES = 6250
        N_EDGES = 62500
        IN_FEAT = 128
        OUT_FEAT = 128
        NUM_RELS = 32
        NUM_BASES = 8
        hsrc = h[src]
        coef = w_comp[etype]
        msg = jnp.zeros((hsrc.shape[0], weight.shape[2]), dtype=h.dtype)
        for b in range(weight.shape[0]):
            msg = msg + hsrc @ weight[b] * coef[:, b][:, None]
        msg = msg * norm
        node_repr = jax.ops.segment_sum(msg, dst, num_segments=h.shape[0])
        node_repr = node_repr + bias_param
        return jax.nn.relu(node_repr)

    def _L2_gnn_ref(x, virtual_edge_index, W_gat, att_src, att_dst, b_gat, W1, b1, W2, b2, ln1_g, ln1_b, ln2_g, ln2_b):
        import jax, jax.numpy as jnp
        import numpy as np
        N = 12500
        E = 100000
        D = 128
        H = 8
        C = D // H
        FF = 512
        EPS = 1e-05
        NEG_SLOPE = 0.2

        def _layernorm(x, g, b):
            mu = jnp.mean(x, axis=-1, keepdims=True)
            var = jnp.mean(jnp.square(x - mu), axis=-1, keepdims=True)
            return (x - mu) * jax.lax.rsqrt(var + EPS) * g + b
        n = x.shape[0]
        loop = jnp.arange(n, dtype=virtual_edge_index.dtype)
        src = jnp.concatenate([virtual_edge_index[0], loop])
        dst = jnp.concatenate([virtual_edge_index[1], loop])
        h = (x @ W_gat).reshape(n, H, C)
        a_s = jnp.sum(h * att_src, axis=-1)
        a_d = jnp.sum(h * att_dst, axis=-1)
        e = a_s[src] + a_d[dst]
        e = jnp.where(e >= 0, e, NEG_SLOPE * e)
        m = jax.ops.segment_max(e, dst, num_segments=n)
        alpha = jnp.exp(e - m[dst])
        den = jax.ops.segment_sum(alpha, dst, num_segments=n)
        alpha = alpha / den[dst]
        msg = h[src] * alpha[..., None]
        agg = jax.ops.segment_sum(msg, dst, num_segments=n)
        gat_out = agg.reshape(n, H * C) + b_gat
        h1 = _layernorm(x + gat_out, ln1_g, ln1_b)
        ff = jax.nn.relu(h1 @ W1 + b1) @ W2 + b2
        return _layernorm(h1 + ff, ln2_g, ln2_b)

    def _L3_gnn_ref(x, edge_index):
        import jax, jax.numpy as jnp
        import numpy as np
        N_NODES = 12500
        N_EDGES = 400000
        D_FEAT = 128
        K = 10
        ALPHA = 0.1

        def _appnp(x, src, dst, norm, n_nodes):
            h = x

            def step(xk, _):
                msg = norm[:, None] * xk[src]
                agg = jax.ops.segment_sum(msg, dst, num_segments=n_nodes)
                return ((1.0 - ALPHA) * agg + ALPHA * h, None)
            xK, _ = jax.lax.scan(step, x, None, length=K)
            return xK
        n = x.shape[0]
        src = edge_index[0]
        dst = edge_index[1]
        loop = jnp.arange(n, dtype=src.dtype)
        src = jnp.concatenate([src, loop])
        dst = jnp.concatenate([dst, loop])
        ones = jnp.ones(src.shape[0], dtype=x.dtype)
        deg = jax.ops.segment_sum(ones, dst, num_segments=n)
        deg_inv_sqrt = jnp.where(deg > 0, jax.lax.rsqrt(deg), 0.0)
        norm = deg_inv_sqrt[src] * deg_inv_sqrt[dst]
        out = _appnp(x, src, dst, norm, n)
        return jax.nn.relu(out)
    edge_index = jnp.stack([src, dst])
    h = jnp.maximum(_layernorm(x, axis=-1), 0.0)
    x = x + _L0_gnn_ref(h, edge_index, L0_gnn_W_fuse, L0_gnn_b_fuse, L0_gnn_W_in, L0_gnn_b_in, L0_gnn_complex_weight, L0_gnn_alpha, L0_gnn_gamma, L0_gnn_beta)
    h = jnp.maximum(_layernorm(x, axis=-1), 0.0)
    x = x + _L1_gnn_ref(h, src, dst, edge_type_32, edge_weight1, L1_gnn_weight, L1_gnn_w_comp, L1_gnn_bias_param)
    h = jnp.maximum(_layernorm(x, axis=-1), 0.0)
    x = x + _L2_gnn_ref(h, edge_index, L2_gnn_W_gat, L2_gnn_att_src, L2_gnn_att_dst, L2_gnn_b_gat, L2_gnn_W1, L2_gnn_b1, L2_gnn_W2, L2_gnn_b2, L2_gnn_ln1_g, L2_gnn_ln1_b, L2_gnn_ln2_g, L2_gnn_ln2_b)
    h = jnp.maximum(_layernorm(x, axis=-1), 0.0)
    x = x + _L3_gnn_ref(h, edge_index)
    return x

_drawn_inputs = setup_inputs


def setup_inputs(seed=0):
    import zlib

    import numpy as np

    out = dict(_drawn_inputs(seed))
    spreads = {'L0_gnn_b_fuse': (0.0, 0.8),
     'L0_gnn_b_in': (0.0, 0.8),
     'L0_gnn_gamma': (1.0, 0.2),
     'L0_gnn_beta': (0.0, 0.1),
     'L2_gnn_b_gat': (0.0, 0.1),
     'L2_gnn_b1': (0.0, 0.308),
     'L2_gnn_b2': (0.0, 0.1),
     'L2_gnn_ln1_g': (1.0, 0.2),
     'L2_gnn_ln1_b': (0.0, 0.1),
     'L2_gnn_ln2_g': (1.0, 0.2),
     'L2_gnn_ln2_b': (0.0, 0.1)}
    factors = {'L0_gnn_W_in': 5.146, 'L0_gnn_complex_weight': 5.646, 'L2_gnn_att_dst': 8.0}
    for name, (base, spread) in spreads.items():
        noise = np.random.default_rng([zlib.crc32(name.encode()), seed]).standard_normal(out[name].shape)
        drawn = base * np.exp(spread * noise) if base else spread * noise
        out[name] = jnp.asarray(drawn.astype(out[name].dtype))
    for name, factor in factors.items():
        out[name] = (out[name] * factor).astype(out[name].dtype)
    return out
```

```python
from contextlib import ExitStack

import numpy as np

import concourse.bass as bass
from concourse import mybir

P = 128
N_NODES, N_EDGES, D = 6250, 100000, 128
NT = (N_NODES + P - 1) // P
NP = NT * P
GT = 4
SLOTS = 4
NG = 196
ET = NG * GT
EP = ET * P
GE_ROWS = GT * P
FULL = N_EDGES // P
REST = N_EDGES - FULL * P
FRONT = 2 * GE_ROWS
RELS, BASES, HEADS, HC, FF = 32, 8, 8, 16, 512
CH = 16
CE = EP // CH
CT = ET // CH
FREQ = D // 2 + 1
BIG = 1.0e30
EPS = 1e-5
STEPS, TELEPORT, SLOPE = 10, 0.1, 0.2
WL2 = D + 2 * HEADS

F32, I32, BF16 = mybir.dt.float32, mybir.dt.int32, mybir.dt.bfloat16
ALU, ACT, AX = mybir.AluOpType, mybir.ActivationFunctionType, mybir.AxisListType
ADD, SUB, MUL, MAX, MIN = ALU.add, ALU.subtract, ALU.mult, ALU.max, ALU.min


def build(nc, t, out):
    ctx = ExitStack()
    with ctx:
        def sb(name, shape, dt=F32):
            return ctx.enter_context(nc.sbuf_tensor(name, shape, dt))

        def dram(name, shape, dt=F32):
            return nc.dram_tensor(name, shape, dt).ap()

        names = {}

        def sem(name):
            if name not in names:
                names[name] = ctx.enter_context(nc.semaphore(name))
            return names[name]

        dst_pad = dram("dst_pad", (FRONT + EP + 8,), I32)
        table = dram("table", (NP, D))
        rel_table = dram("rel_table", (NP * RELS, D))
        gat_table = dram("gat_table", (NP, D + HEADS))
        x_spill = dram("x_spill", (NP, D))
        runs = dram("runs", (EP, D))
        runs2 = dram("runs2", (EP, WL2))
        edge_rows = dram("edge_rows", (EP, D))
        seeds = dram("seeds", (EP, 2 * HEADS))

        X, A, B, C, E = (sb(n, [P, NP]) for n in ("X", "A", "B", "C", "E"))
        Dw = sb("Dw", [P, NT * WL2])
        Db = Dw[:, 0:NP]

        def nodes(v):
            return v[:, 0:NP].rearrange("p (t f) -> p t f", f=D)

        def bc(v, n):
            return v.unsqueeze(2).to_broadcast([v.shape[0], v.shape[1], n])

        def row_bc(v, n):
            return v.unsqueeze(1).to_broadcast([v.shape[0], n, v.shape[1]])

        src_i = sb("src_i", [P, ET], I32)
        rel_i = sb("rel_i", [P, ET], I32)
        dst_f = sb("dst_f", [P, ET + 1])
        weight_e = sb("weight_e", [P, ET])
        G = sb("G", [P, SLOTS, GT, D + HEADS])
        idx = sb("idx", [P, SLOTS, GT], I32)
        O = sb("O", [P, 2, GT, WL2])
        S = sb("S", [P, 2, GT, P])
        carry_mask = sb("carry_mask", [1, 2, GT, P])
        dst_b = sb("dst_b", [P, 2, GE_ROWS], I32)
        ident, tri = (sb(n, [P, P]) for n in ("ident", "tri"))
        ones, iota_f = Dw[:, NP:NP + P], Dw[:, NP + P:NP + 2 * P]
        iota_i = A[:, 0:P].bitcast(I32)
        hot_lo = C[:, 0:GT * P].bitcast(BF16).rearrange("p (a k n) -> p a k n", a=2, k=GT)
        hot_hi = C[:, 1024:1024 + GT * NT].bitcast(BF16).rearrange("p (a k n) -> p a k n", a=2, k=GT)
        (cnt, mask, rcnt, dinv, row_f, stat_a, stat_b, sc_a, sc_b) = (
            sb(n, [P, NT]) for n in ("cnt", "mask", "rcnt", "dinv", "row_f", "stat_a", "stat_b", "sc_a", "sc_b"))
        row_i, seed_i = sb("row_i", [P, NT], I32), sb("seed_i", [P, NT], I32)
        scores = sb("scores", [P, NT, 2 * HEADS])
        self_w = sb("self_w", [P, NT * HEADS])
        wf = sb("wf", [P, 2, D])
        w_tot = sb("w_tot", [P, D])
        w_in, c_mat = Dw[:, 0:D], Dw[:, D:2 * D]
        cs = Dw[0:FREQ, 2 * D:6 * D].rearrange("p (a f) -> p a f", f=D)
        cs_w = Dw[0:FREQ, 6 * D:9 * D].rearrange("p (a f) -> p a f", f=D)
        cols = sb("cols", [P, 8])
        cw = sb("cw", [FREQ, 2])
        w_base = Dw[:, RELS * D:(RELS + BASES) * D].rearrange("p (b o) -> p b o", o=D)
        comp = Dw[:, (RELS + BASES) * D:(RELS + BASES) * D + RELS * BASES].rearrange("p (r b) -> p r b", b=BASES)
        rows = sb("rows", [P, 9, D])
        w_gat, w1, w2, b1 = sb("w_gat", [P, D]), sb("w1", [P, FF]), sb("w2", [P, 4, D]), sb("b1", [P, 4])
        bn_st, bn = sb("bn_st", [P, 14, 6]), sb("bn", [P, 4])
        end_col, in_col = sb("end_col", [P, 2]), sb("in_col", [P, 1])
        chain_row = S[0:1, :, :, :].rearrange("p a k e -> p (a k) e")
        (BIAS1, ATT_S, ATT_D, B_GAT, G1, BB1, G2, BB2, B2) = range(9)

        ps = [ctx.enter_context(nc.psum_tensor(f"ps{k}", [P, 512], F32)) for k in range(4)]
        pt = [ctx.enter_context(nc.psum_tensor(f"pt{k}", [P, 1024], F32)) for k in range(2)]
        T7 = 7
        PTN = NT // T7

        gathered = [sem(f"gathered{k}") for k in range(SLOTS)]
        reloaded = [sem(f"reloaded{k}") for k in range(SLOTS)]
        dst_in = [sem(f"dst_in{k}") for k in range(2)]
        stored = [sem(f"stored{k}") for k in range(2)]
        kept = [sem(f"kept{k}") for k in range(SLOTS)]
        idx_set, summed, evacuated, selected = sem("idx_set"), sem("summed"), sem("evacuated"), sem("selected")
        scaled, hist_ready, hist_used, as_kept, max_kept = (
            sem(n) for n in ("scaled", "hist_ready", "hist_used", "as_kept", "max_kept"))
        CREDIT_SUM, CREDIT_EV, CREDIT_SEL = SLOTS * GT, 4, 2

        def settle(eng):
            eng.sem_inc(sem("settled"), 1)

        table_v = table.rearrange("(t p) f -> p t f", p=P)
        spill_v = x_spill.rearrange("(t p) f -> p t f", p=P)
        gat_v = gat_table.rearrange("(t p) f -> p t f", p=P)
        out_full = (N_NODES // P) * P

        LOADS = []
        for k, n in enumerate(("b_fuse", "b_in", "gamma", "beta")):
            LOADS.append((cols[:, k:k + 1], t[n].rearrange("(p a) -> p a", a=1)))
        LOADS.append((cols[:, 4:5], t["alpha"].rearrange("(a b) -> a b", a=1).to_broadcast([P, 1])))
        LOADS.append((wf[:, :, :], t["w_fuse_t"].rearrange("(a p) o -> p a o", p=P)))
        LOADS.append((w_in[:, :], t["w_in"]))
        LOADS.append((cs[:, :, :], t["fourier"]))
        LOADS.append((cw[:, :], t["complex_weight"]))
        for k, n in enumerate(("bias_param", "att_src", "att_dst", "b_gat", "ln1_g", "ln1_b", "ln2_g", "ln2_b", "b2")):
            v = t[n] if len(t[n].shape) == 1 else t[n].rearrange("h c -> (h c)")
            LOADS.append((rows[:, k, :], v.rearrange("(a f) -> a f", a=1).to_broadcast([P, D])))
        LOADS.append((w_gat[:, :], t["w_gat"]))
        LOADS.append((w1[:, :], t["w1"]))
        LOADS.append((w2[:, :, :], t["w2"].rearrange("(c p) o -> p c o", p=P)))
        LOADS.append((b1[:, :], t["b1"]))
        EDGES = []
        for v, n in ((src_i, "src"), (rel_i, "etype"), (weight_e, "norm"), (B[:, :].bitcast(I32), "dst")):
            EDGES.append((v[:, 0:FULL], t[n + "_cols"]))
            EDGES.append((v[0:REST, FULL:FULL + 1], t[n][FULL * P:N_EDGES].rearrange("(p a) -> p a", a=1)))
        Bi, Ci, Ei = (v[:, :].bitcast(I32) for v in (B, C, E))

        block = ctx.enter_context(nc.Block())

        @block.sync
        def _(sp):
            def group_of(i):
                return NG - 1 - i

            def load_dst(slot, q):
                sp.dma_start(dst_b[:, slot, :],
                             dst_pad[bass.ds(q * GE_ROWS + FRONT, GE_ROWS)].rearrange("(a e) -> a e", a=1)
                             .to_broadcast([P, GE_ROWS])).then_inc(dst_in[slot], 16)

            def sweep(base, base_pairs, to, width, reload=False):
                def load_rows(slot, q):
                    sp.dma_start(G[:, slot, :, 0:D],
                                 edge_rows[bass.ds(q * GE_ROWS, GE_ROWS), :].rearrange("(t p) f -> p t f", p=P)
                                 ).then_inc(reloaded[slot], 16)
                to_v = to.rearrange("(t p) f -> p t f", p=P)

                def groups(j, last=False):
                    for u in range(SLOTS):
                        i = j * SLOTS + u
                        sp.wait_ge(evacuated, (i + base) * GT + GT + CREDIT_EV)
                        if width == WL2:
                            settle(sp)
                            sp.wait_ge(max_kept, i + 1)
                        settle(sp)
                        sp.dma_start(to_v[:, bass.ds(group_of(i) * GT, GT), :],
                                     O[:, u % 2, :, 0:width]).then_inc(stored[u % 2], 16)
                        if reload and not last:
                            load_rows(u, group_of(i) - SLOTS)
                        sp.wait_ge(selected, i + base + 1 + CREDIT_SEL)
                        settle(sp)
                        load_dst(u % 2, group_of(i) - 2)

                if not reload:
                    with sp.Fori(0, NG // SLOTS) as j:
                        groups(j)
                    return
                for u in range(SLOTS):
                    load_rows(u, group_of(u))
                with sp.Fori(0, NG // SLOTS - 1) as j:
                    groups(j)
                groups(NG // SLOTS - 1, last=True)

            sp.wait_ge(sem("padded"), 4)
            for dst_ap, src_ap in EDGES:
                sp.dma_start(dst_ap, src_ap).then_inc(sem("edges_in"), 16)
            full = N_NODES // P
            sp.dma_start(nodes(X)[:, 0:full, :], t["x"][0:full * P, :].rearrange("(t p) f -> p t f", p=P)
                         ).then_inc(sem("x_in"), 16)
            sp.dma_start(nodes(X)[0:N_NODES - full * P, full, :], t["x"][full * P:N_NODES, :]).then_inc(sem("x_in"), 16)
            tail = EP - N_EDGES
            sp.dma_start(dst_pad[FRONT:FRONT + N_EDGES], t["dst"]).then_inc(sem("dst_padded"), 16)
            sp.dma_start(dst_pad[0:FRONT - tail], t["dst"][EP - FRONT:N_EDGES]).then_inc(sem("dst_padded"), 16)
            pad = Ei[0:1, 0:tail + 8]
            sp.dma_start(dst_pad[FRONT - tail:FRONT], pad[:, 0:tail]).then_inc(sem("dst_padded"), 16)
            sp.dma_start(dst_pad[FRONT + N_EDGES:FRONT + EP + 8], pad).then_inc(sem("dst_padded"), 16)
            for dst_ap, src_ap in LOADS:
                sp.dma_start(dst_ap, src_ap).then_inc(sem("weights_in"), 16)
            sz = 2 * HEADS * EP // P
            seeds_z = seeds.rearrange("(p a) f -> p (a f)", p=P)
            for k in range(2):
                sp.dma_start(seeds_z[:, k * (sz // 2):(k + 1) * (sz // 2)], C[:, 0:sz // 2]
                             ).then_inc(sem("seeds_zero"), 16)
            for k in range(2):
                sp.dma_start(runs[k * P:(k + 1) * P, :], C[:, 0:D]).then_inc(stored[k], 16)
            for k in range(SLOTS):
                sp.dma_start(edge_rows[k * P:(k + 1) * P, :], C[:, 0:D]).then_inc(kept[k], 16)
            sp.wait_ge(sem("dst_padded"), 64)
            load_dst(0, NG - 1)
            load_dst(1, NG - 2)
            sp.wait_ge(sem("ln0"), 1)
            sp.dma_start(table_v, nodes(A)).then_inc(sem("table0"), 16)
            sweep(0, 0, runs, D)
            sp.wait_ge(sem("ln1"), 1)
            sp.dma_start(w_base, t["weight"].rearrange("b i o -> i b o")).then_inc(sem("bases_in"), 16)
            sp.dma_start(comp.rearrange("p r b -> p (r b)"),
                         t["w_comp"].rearrange("(a r) b -> a (r b)", a=1).to_broadcast([P, RELS * BASES])
                         ).then_inc(sem("bases_in"), 16)
            rel_v = rel_table.rearrange("(t p r) o -> t p (r o)", p=P, r=RELS)
            for n in range(NT):
                sp.wait_ge(sem("rel_act"), 4 * (n + 1))
                sp.wait_ge(sem("rel_dve"), 4 * (n + 1))
                sp.dma_start(rel_v[n], (C, E)[n % 2][:, 0:RELS * D]).then_inc(sem(f"rel_stored{n % 2}"), 16)
            sweep(NG, 0, runs, D)
            sp.wait_ge(sem("ln2"), 1)
            sp.dma_start(table_v, nodes(A)).then_inc(sem("spilled"), 16)
            sp.dma_start(spill_v, nodes(X)).then_inc(sem("spilled"), 16)
            sp.wait_ge(sem("gat_rows"), PTN)
            sp.dma_start(gat_v[:, :, 0:D], nodes(C)).then_inc(sem("gat_stored"), 16)
            sp.wait_ge(sem("scores_ready"), 2)
            sp.dma_start(gat_v[:, :, D:D + HEADS], scores[:, :, HEADS:]).then_inc(sem("gat_stored"), 16)
            rows_v = edge_rows.rearrange("(t p) f -> p t f", p=P)
            with sp.Fori(0, NG // SLOTS) as j:
                for u in range(SLOTS):
                    sp.wait_ge(gathered[u], (j + 1 + 2 * (NG // SLOTS)) * (16 * GT))
                    sp.dma_start(rows_v[:, bass.ds((j * SLOTS + u) * GT, GT), :],
                                 G[:, u, :, 0:D]).then_inc(kept[u], 16)
            for k in range(SLOTS):
                sp.wait_ge(kept[k], 16 * (NG // SLOTS) + 16)
            sp.wait_ge(sem("seeded"), 16 * NT)
            sp.wait_ge(sem("spilled"), 32)
            sp.wait_ge(sem("gat_stored"), 32)
            seeds_v = seeds.rearrange("(t p) f -> p t f", p=P)
            with nc.allow_non_contiguous_dma(reason="32-byte rows"):
                sp.dma_start(B[:, :].rearrange("p (t h) -> p t h", h=HEADS), seeds_v[:, :, 0:HEADS]
                             ).then_inc(sem("seeds_in"), 16)
                sp.dma_start(C[:, :].rearrange("p (t h) -> p t h", h=HEADS), seeds_v[:, :, HEADS:]
                             ).then_inc(sem("seeds_in"), 16)

            def load_head_major(v, shift, name):
                for h in range(HEADS):
                    sp.dma_start(v[h * CH:(h + 1) * CH, :],
                                 dst_pad[FRONT + shift:FRONT + shift + EP].rearrange("(c e) -> c e", c=CH)
                                 ).then_inc(sem(name), 16)
            sp.wait_ge(sem("to_heads"), 3 * PTN)
            load_head_major(Bi, 0, "dst_heads")
            load_head_major(Ci, -1, "dst_heads")
            sp.wait_ge(sem("fwd_done"), 1)
            load_head_major(Bi, 0, "dst_heads2")
            load_head_major(Ci, 1, "dst_heads2")
            sp.wait_ge(sem("from_heads"), 2 * PTN)
            sp.dma_start(nodes(A), table_v).then_inc(sem("h2_back"), 16)
            sp.dma_start(nodes(X), spill_v).then_inc(sem("x_back"), 16)
            sweep(2 * NG, 0, runs2, WL2, reload=True)
            sp.dma_start(nodes(C), gat_v[:, :, 0:D]).then_inc(sem("gat_back"), 16)
            with sp.Fori(0, STEPS) as s:
                sp.wait_ge(sem("y_ready"), s + 1)
                sp.dma_start(table_v, nodes(C)).then_inc(sem("y_stored"), 16)
                sweep((s + 3) * NG, 0, runs, D)
            sp.wait_ge(sem("out_ready"), 1)
            sp.dma_start(out[0:full * P, :].rearrange("(t p) f -> p t f", p=P), nodes(X)[:, 0:full, :]
                         ).then_inc(sem("out_stored"), 16)
            sp.dma_start(out[full * P:N_NODES, :], nodes(X)[0:N_NODES - full * P, full, :]
                         ).then_inc(sem("out_stored"), 16)
            sp.wait_ge(sem("out_stored"), 32)
            for k in range(2):
                sp.wait_ge(stored[k], 16 * (NG // 2) * (3 + STEPS) + 16)
                sp.wait_ge(dst_in[k], 16 * (NG // 2) * (3 + STEPS) + 16)
            sp.wait_ge(sem("y_stored"), 16 * STEPS)

        @block.gpsimd
        def _(pool):
            pool.memset(nodes(X)[:, NT - 1, :], 0.0).then_inc(sem("padded"), 1)
            pool.memset(ident[:, :], 0.0).then_inc(sem("made"), 1)
            pool.memset(tri[:, :], 1.0).then_inc(sem("made"), 1)
            pool.memset(ones[:, :], 1.0).then_inc(sem("made"), 1)
            pool.iota(iota_i[:, :], pattern=[[1, P]], base=0, channel_multiplier=0).then_inc(sem("made"), 1)
            pool.wait_ge(sem("made"), 4)
            pool.affine_select(out=ident[:, :], in_=ident[:, :], compare_op=ALU.not_equal, fill=1.0, base=0,
                               pattern=[[-1, P]], channel_multiplier=1).then_inc(sem("made"), 1)
            pool.affine_select(out=tri[:, :], in_=tri[:, :], compare_op=ALU.is_ge, fill=0.0, base=0,
                               pattern=[[-1, P]], channel_multiplier=1).then_inc(sem("made"), 1)

            def sweep(p, rows_ap, indices, keep=False):
                with pool.Fori(0, NG // SLOTS) as j:
                    for u in range(SLOTS):
                        i = j * SLOTS + u
                        if keep:
                            pool.wait_ge(kept[u], j * 16 + 16)
                            settle(pool)
                            pool.wait_ge(as_kept, i + 1)
                        else:
                            pool.wait_ge(summed, (p * NG + i) * GT + GT)
                        settle(pool)
                        q = i if keep else NG - 1 - i
                        pool.tensor_copy(idx[:, u, :], indices[:, bass.ds(q * GT, GT)]).then_inc(idx_set, 1)
                        pool.wait_ge(idx_set, p * NG + i + 1)
                        settle(pool)
                        for k in range(GT):
                            w = rows_ap.shape[1]
                            pool.indirect_dma_start(
                                out=G[:, u, k, 0:w], out_offset=None, in_=rows_ap,
                                in_offset=bass.IndirectOffsetOnAxis(ap=idx[:, u, k:k + 1], axis=0)
                            ).then_inc(gathered[u], 16)

            def node_rows(rows_ap, to_v, done):
                for n in range(NT):
                    pool.indirect_dma_start(
                        out=to_v[:, n, :], out_offset=None, in_=rows_ap,
                        in_offset=bass.IndirectOffsetOnAxis(ap=row_i[:, n:n + 1], axis=0)).then_inc(done, 16)

            def wait_runs(passes):
                for k in range(2):
                    pool.wait_ge(stored[k], passes * (16 * (NG // 2)) + 16)
                    settle(pool)

            pool.wait_ge(sem("edge_numbers"), 1)
            pool.wait_ge(sem("table0"), 16)
            sweep(0, table, src_i)
            wait_runs(1)
            pool.wait_ge(sem("row_starts"), 1)
            node_rows(runs, nodes(C), sem("nodes0"))
            for k in range(2):
                pool.wait_ge(sem(f"rel_stored{k}"), 16 * ((NT + 1 - k) // 2))
            sweep(1, rel_table, rel_i)
            wait_runs(2)
            node_rows(runs, nodes(C), sem("nodes1"))
            pool.wait_ge(sem("seeds_zero"), 32)
            pool.wait_ge(sem("scores_ready"), 2)
            for n in range(NT):
                pool.indirect_dma_start(
                    out=seeds, out_offset=bass.IndirectOffsetOnAxis(ap=seed_i[:, n:n + 1], axis=0),
                    in_=scores[:, n, :], in_offset=None, bounds_check=EP - 1, oob_is_err=False
                ).then_inc(sem("seeded"), 16)
            pool.wait_ge(sem("gat_stored"), 32)
            pool.wait_ge(summed, 2 * NG * GT + CREDIT_SUM)
            sweep(2, gat_table, src_i, keep=True)
            wait_runs(3)
            node_rows(runs2, Dw[:, :].rearrange("p (t f) -> p t f", f=WL2), sem("nodes2"))
            with pool.Fori(0, STEPS) as s:
                pool.wait_ge(sem("y_stored"), s * 16 + 16)
                settle(pool)
                sweep(s + 3, table, src_i)
                wait_runs(s + 4)
                node_rows(runs, nodes(Db), sem("nodes3"))

        @block.scalar
        def _(act):
            def sweep(base, width=D, scale=False, keep_max=False):
                act_to = width
                with act.Fori(0, NG // SLOTS) as j:
                    for u in range(SLOTS):
                        i = j * SLOTS + u
                        gi = i + base
                        if scale:
                            act.wait_ge(gathered[u], (j + 1 + base // SLOTS) * (16 * GT))
                            for k in range(GT - 1, -1, -1):
                                act.activation(G[:, u, k, 0:D], G[:, u, k, 0:D], ACT.Copy,
                                               scale=weight_e[:, bass.ds((NG - 1 - i) * GT + k, 1)]
                                               ).then_inc(scaled, 1)
                        act.wait_ge(stored[u % 2], (gi - u % 2) * 8 + 16)
                        if keep_max:
                            act.activation(O[:, u % 2, :, D + HEADS:WL2].rearrange("p k h -> p k h"),
                                           C[:, bass.ds((NG - 1 - i) * (GT * HEADS), GT * HEADS)]
                                           .rearrange("p (k h) -> p k h", h=HEADS), ACT.Copy).then_inc(max_kept, 1)
                        for m in range(GT):
                            k = GT - 1 - m
                            act.wait_ge(summed, gi * GT + m + 1 + CREDIT_SUM)
                            act.activation(O[:, u % 2, k, 0:act_to], ps[m % 4][:, 0:act_to], ACT.Copy
                                           ).then_inc(evacuated, 1)

            def copy_pt(n, ready, done, to, before=0):
                for r in range(PTN):
                    act.wait_ge(ready, before + r + 1)
                    act.activation(to[:, r * T7 * P:(r + 1) * T7 * P], pt[r % 2][:, 0:T7 * P], ACT.Copy
                                   ).then_inc(done, 1)

            roots = [0]

            def root(v):
                roots[0] += 1
                act.wait_ge(sem("to_root"), roots[0])
                act.activation(v, v, ACT.Sqrt).then_inc(sem("rooted"), 1)

            root(stat_b[:, :])
            copy_pt(0, sem("hT_ps"), sem("hT"), B)
            sweep(0)
            root(dinv[:, :])
            copy_pt(0, sem("aggT_ps"), sem("aggT"), Dw)
            act.wait_ge(sem("w_tot"), 2)
            for n in range(14):
                act.wait_ge(sem("mix_ps"), n + 1)
                act.activation(E[:, n * 448:(n + 1) * 448], ps[n % 4][:, 0:448], ACT.Identity, bias=cols[:, 5:6]
                               ).then_inc(sem("mix_out"), 1)
            root(bn[:, 2:3])
            for n in range(2):
                act.wait_ge(sem("bn_ready"), n + 1)
                half = slice(n * NP // 2, (n + 1) * NP // 2)
                act.activation(E[:, half], E[:, half], ACT.Gelu, bias=cols[:, 3:4]).then_inc(sem("gelu"), 1)
            root(stat_b[:, :])
            copy_pt(0, sem("h1T_ps"), sem("h1T"), B)
            act.wait_ge(sem("x1_done"), 1)
            for n in range(NT):
                if n >= 2:
                    act.wait_ge(sem(f"rel_stored{n % 2}"), 16 * (n // 2))
                for k in range(0, 8, 2):
                    act.wait_ge(sem("rel_ps"), 8 * n + k + 1)
                    act.activation((C, E)[n % 2][:, k * 512:(k + 1) * 512], ps[k % 4][:, :], ACT.Copy
                                   ).then_inc(sem("rel_act"), 1)
            sweep(NG, scale=True)
            root(stat_b[:, :])
            copy_pt(0, sem("h2T_ps"), sem("h2T"), B)
            copy_pt(0, sem("gat_ps"), sem("gat_rows"), C)
            with act.Fori(0, NG // SLOTS) as j:
                for u in range(SLOTS):
                    i = j * SLOTS + u
                    act.wait_ge(gathered[u], (j + 1 + 2 * (NG // SLOTS)) * (16 * GT))
                    act.activation(E[:, bass.ds(i * (GT * HEADS), GT * HEADS)].rearrange("p (k h) -> p k h", h=HEADS),
                                   G[:, u, :, D:D + HEADS], ACT.Copy).then_inc(as_kept, 1)
            for r in range(3 * PTN):
                to = (A, Dw, X)[r // PTN]
                act.wait_ge(sem("heads_ps"), r + 1)
                act.activation(to[:, (r % PTN) * T7 * P:(r % PTN + 1) * T7 * P], pt[r % 2][:, 0:T7 * P], ACT.Copy
                               ).then_inc(sem("to_heads"), 1)
            act.wait_ge(sem("exponents"), 1)
            act.activation(A[:, :], A[:, :], ACT.Exp).then_inc(sem("edge_w"), 1)
            for r in range(2 * PTN):
                to = (B, C)[r // PTN][:, :].rearrange("p (c j h) -> p j h c", c=CH, h=HEADS)
                act.wait_ge(sem("edges_ps"), r + 1)
                for n in range(T7):
                    a = act.activation(to[:, (r % PTN) * T7 + n, :, :],
                                       pt[r % 2][:, n * P:(n + 1) * P].rearrange("p (h c) -> p h c", c=CH),
                                       ACT.Copy)
                a.then_inc(sem("from_heads"), 1)
            act.wait_ge(sem("from_heads"), 2 * PTN)
            sweep(2 * NG, width=D + HEADS, keep_max=True)
            act.wait_ge(sem("self_exponents"), 1)
            act.activation(self_w[:, :], self_w[:, :], ACT.Exp).then_inc(sem("self_w"), 1)
            root(stat_b[:, :])
            copy_pt(0, sem("h3T_ps"), sem("h3T"), B)
            for n in range(14):
                for c in range(4):
                    act.wait_ge(sem("ff1_ps"), 4 * n + c + 1)
                    if n >= 2:
                        act.wait_ge(sem("ff2_ps"), n - 1)
                    act.activation(E[:, (n % 2) * 1792 + c * 448:(n % 2) * 1792 + (c + 1) * 448], ps[c % 2][:, 0:448],
                                   ACT.Relu, bias=b1[:, c:c + 1]).then_inc(sem("ff1"), 1)
            root(stat_b[:, :])
            root(stat_b[:, :])
            with act.Fori(0, STEPS) as s:
                sweep((s + 3) * NG)

        @block.tensor
        def _(pe):
            def sweep(base, ready, width=D, hist=False):
                with pe.Fori(0, NG // SLOTS) as j:
                    for u in range(SLOTS):
                        i = j * SLOTS + u
                        gi = i + base
                        pe.wait_ge(selected, gi + 1 + CREDIT_SEL)
                        for m in range(GT):
                            k = GT - 1 - m
                            ready(j, u, i, m)
                            pe.wait_ge(evacuated, gi * GT + m + 1)
                            pe.matmul(ps[m % 4][:, 0:width], S[:, u % 2, k, :], G[:, u, k, 0:width],
                                      start=True, stop=False)
                            pe.wait_ge(evacuated, gi * GT + m + CREDIT_EV)
                            prev = O[0:1, u % 2, k + 1, 0:width] if m else O[0:1, 1 - u % 2, 0, 0:width]
                            pe.matmul(ps[m % 4][:, 0:width], carry_mask[0:1, u % 2, k, :], prev,
                                      start=False, stop=True).then_inc(summed, 1)
                        if hist:
                            pe.wait_ge(hist_ready, i + 1)
                            for k in range(GT):
                                mm = pe.matmul(pt[0][:, 0:NT], hot_lo[:, u % 2, k, :], hot_hi[:, u % 2, k, :],
                                               start=False, stop=False, skip_group_check=True)
                            mm.then_inc(hist_used, 1)

            def transposes(src, done, free, before=0):
                for r in range(PTN):
                    if r >= 2:
                        pe.wait_ge(free, before + r - 1)
                    for n in range(T7):
                        mm = pe.transpose(pt[r % 2][:, n * P:(n + 1) * P], src(r * T7 + n), ident[:, :])
                    mm.then_inc(done, 1)

            def tiles(v):
                return lambda n: v[:, n * P:(n + 1) * P]

            pe.sem_inc(summed, CREDIT_SUM)
            pe.wait_ge(sem("made"), 6)
            pe.wait_ge(sem("weights_in"), 16 * len(LOADS))
            pe.wait_ge(sem("filter"), 2)
            pe.matmul(ps[0][:, 0:D], cs[:, 0, :], cs_w[:, 0, :], start=True, stop=False)
            pe.matmul(ps[0][:, 0:D], cs[:, 1, :], cs_w[:, 1, :], start=False, stop=True).then_inc(sem("filter_ps"), 1)
            pe.wait_ge(sem("filter_c"), 1)
            pe.matmul(ps[1][:, 0:D], w_in[:, :], c_mat[:, :], start=True, stop=True).then_inc(sem("filter_ps"), 1)
            pe.matmul(ps[2][:, 0:1], c_mat[:, :], cols[:, 1:2], start=True, stop=True).then_inc(sem("filter_ps"), 1)
            pe.wait_ge(sem("ln0"), 1)
            transposes(tiles(A), sem("hT_ps"), sem("hT"))
            pe.wait_ge(sem("hT"), PTN)
            pe.wait_ge(sem("w_tot"), 2)
            pe.wait_ge(sem("hist_zero"), 1)
            pe.matmul(pt[0][:, 0:NT], hot_lo[:, 0, 0, :], hot_hi[:, 0, 0, :], start=True, stop=False,
                      skip_group_check=True).then_inc(sem("hist_started"), 1)

            def rows_in(base):
                def ready(j, u, i, m):
                    if m == 0:
                        pe.wait_ge(gathered[u], (j + 1 + base) * (16 * GT))
                return ready
            per = NG // SLOTS
            sweep(0, rows_in(0), hist=True)
            pe.wait_ge(sem("counts"), 1)
            pe.wait_ge(evacuated, NG * GT + CREDIT_EV)
            pe.matmul(ps[0][:, 0:NT], iota_f[:, :], cnt[:, :], start=True, stop=True)
            pe.matmul(ps[1][:, 0:NT], ones[:, :], cnt[:, :], start=True, stop=True).then_inc(sem("starts_ps"), 1)
            pe.wait_ge(sem("agg"), 1)
            transposes(tiles(C), sem("aggT_ps"), sem("aggT"))
            pe.wait_ge(sem("aggT"), PTN)
            for n in range(14):
                if n >= 4:
                    pe.wait_ge(sem("mix_out"), n - 3)
                c = slice(n * 448, (n + 1) * 448)
                pe.matmul(ps[n % 4][:, 0:448], w_tot[:, :], B[:, c], start=True, stop=False)
                pe.matmul(ps[n % 4][:, 0:448], wf[:, 1, :], Dw[:, c], start=False, stop=True
                          ).then_inc(sem("mix_ps"), 1)
            pe.wait_ge(sem("gelu"), 2)
            transposes(tiles(E), sem("x1_ps"), sem("x1"))
            pe.wait_ge(sem("ln1"), 1)
            transposes(tiles(A), sem("h1T_ps"), sem("h1T"))
            pe.wait_ge(sem("h1T"), PTN)
            pe.wait_ge(sem("rel_w"), 1)
            for n in range(NT):
                for k in range(8):
                    g = 8 * n + k
                    if g >= 4:
                        pe.wait_ge(sem("rel_dve" if k % 2 else "rel_act"), (g - 4) // 2 + 1)
                    pe.matmul(ps[k % 4][:, :], B[:, n * P:(n + 1) * P], Db[:, k * 512:(k + 1) * 512],
                              start=True, stop=True).then_inc(sem("rel_ps"), 1)
            pe.wait_ge(sem("rel_act"), 4 * NT)
            pe.wait_ge(sem("rel_dve"), 4 * NT)

            def scaled_in(j, u, i, m):
                pe.wait_ge(scaled, i * GT + m + 1)
            sweep(NG, scaled_in)
            pe.wait_ge(sem("ln2"), 1)
            transposes(tiles(A), sem("h2T_ps"), sem("h2T"))
            pe.wait_ge(sem("h2T"), PTN)
            for r in range(PTN):
                if r >= 2:
                    pe.wait_ge(sem("gat_rows"), r - 1)
                for n in range(T7):
                    mm = pe.matmul(pt[r % 2][:, n * P:(n + 1) * P], B[:, (r * T7 + n) * P:(r * T7 + n + 1) * P],
                                   w_gat[:, :], start=True, stop=True)
                mm.then_inc(sem("gat_ps"), 1)
            pe.wait_ge(sem("gat_rows"), PTN)

            for k, v in enumerate((A, Dw, X)):
                pe.wait_ge(sem("permuted"), k + 1)
                for r in range(PTN):
                    g = k * PTN + r
                    if g >= 2:
                        pe.wait_ge(sem("to_heads"), g - 1)
                    for n in range(T7):
                        mm = pe.transpose(pt[g % 2][:, n * P:(n + 1) * P], tiles(v)(r * T7 + n), ident[:, :])
                    mm.then_inc(sem("heads_ps"), 1)
            pe.wait_ge(sem("to_heads"), 3 * PTN)
            chains = 0
            for n, back in enumerate((False, True, True, False, True)):
                pe.wait_ge(sem("ends"), n + 1)
                pe.transpose(ps[0][0:1, 0:P], end_col[:, 0:1], ident[:, :]).then_inc(sem("ends_ps"), 1)
                if back:
                    chains += 1
                    pe.wait_ge(sem("starts"), chains)
                    pe.matmul(ps[1][:, 0:1], chain_row[0:1, 5, :], ones[0:1, 0:1], start=True, stop=True
                              ).then_inc(sem("starts_c"), 1)
            pe.wait_ge(sem("edge_w"), 1)
            for k, v in enumerate((A, X)):
                for r in range(PTN):
                    g = k * PTN + r
                    if g >= 2:
                        pe.wait_ge(sem("from_heads"), g - 1)
                    for n in range(T7):
                        mm = pe.transpose(pt[g % 2][:, n * P:(n + 1) * P], v[:, (r * T7 + n) * P:(r * T7 + n + 1) * P],
                                          ident[:, :])
                    mm.then_inc(sem("edges_ps"), 1)
            pe.wait_ge(sem("from_heads"), 2 * PTN)
            sweep(2 * NG, lambda j, u, i, m: pe.wait_ge(sem("weighted"), i + 1) if m == 0 else None, width=D + HEADS)
            pe.wait_ge(sem("ln_a"), 1)
            transposes(tiles(A), sem("h3T_ps"), sem("h3T"))
            pe.wait_ge(sem("h3T"), PTN)
            for n in range(14 + 1):
                if n < 14:
                    for c in range(4):
                        g = 4 * n + c
                        if g >= 2:
                            pe.wait_ge(sem("ff1"), g - 1)
                        pe.matmul(ps[c % 2][:, 0:448], w1[:, c * P:(c + 1) * P], B[:, n * 448:(n + 1) * 448],
                                  start=True, stop=True).then_inc(sem("ff1_ps"), 1)
                if n >= 1:
                    pe.wait_ge(sem("ff1"), 4 * n)
                    if n >= 3:
                        pe.wait_ge(sem("ff2"), n - 2)
                    base = ((n - 1) % 2) * 1792
                    for c in range(4):
                        mm = pe.matmul(ps[2 + (n - 1) % 2][:, 0:448], w2[:, c, :],
                                       E[:, base + c * 448:base + (c + 1) * 448], start=(c == 0), stop=(c == 3))
                    mm.then_inc(sem("ff2_ps"), 1)
            pe.wait_ge(sem("ff2"), 14)
            transposes(tiles(Dw), sem("ffb_ps"), sem("ffb"))
            pe.wait_ge(sem("ffb"), PTN)
            with pe.Fori(0, STEPS) as s:
                sweep((s + 3) * NG, rows_in((s + 3) * per))

        @block.vector
        def _(dve):
            links = [0]

            def link(ins):
                links[0] += 1
                ins.then_inc(sem("dve_link"), 1)
                dve.wait_ge(sem("dve_link"), links[0])

            def sweep(base, hist=False, weights=False):
                with dve.Fori(0, NG // SLOTS) as j:
                    for u in range(SLOTS):
                        i = j * SLOTS + u
                        gi = i + base
                        t0 = (NG - 1 - i) * GT
                        if weights:
                            dve.wait_ge(reloaded[u], j * 16 + 16)
                            w = B[:, bass.ds(t0 * HEADS, GT * HEADS)].rearrange("p (k h) -> p k h", h=HEADS)
                            for k in range(GT):
                                g = G[:, u, k, 0:D].rearrange("p (h c) -> p h c", c=HC)
                                dve.tensor_tensor(g, g, bc(B[:, bass.ds((t0 + k) * HEADS, HEADS)], HC), MUL)
                            dve.tensor_copy(G[:, u, :, D:D + HEADS], w).then_inc(sem("weighted"), 1)
                        dve.wait_ge(dst_in[u % 2], (gi - u % 2) * 8 + 16)
                        dve.wait_ge(summed, gi * GT + (CREDIT_SUM - GT))
                        settle(dve)
                        for k in range(GT):
                            dve.scalar_tensor_tensor(S[:, u % 2, k, :], dst_b[:, u % 2, k * P:(k + 1) * P],
                                                     dst_f[:, bass.ds(t0 + k, 1)], tri[:, :], ALU.is_equal, MUL)
                        dve.tensor_tensor(carry_mask[0:1, u % 2, :, :],
                                          dst_b[0:1, u % 2, :].rearrange("p (k e) -> p k e", e=P),
                                          bc(dst_f[0:1, bass.ds(t0 + 1, GT)], P), ALU.is_equal
                                          ).then_inc(selected, 1)
                        if hist:
                            dve.wait_ge(hist_used, i + 1)
                            for k in range(GT):
                                dve.tensor_scalar(hot_lo[:, u % 2, k, :], iota_f[:, :],
                                                  E[:, bass.ds(t0 + k, 1)], None, ALU.is_equal)
                                a = dve.tensor_scalar(hot_hi[:, u % 2, k, :], iota_f[:, 0:NT],
                                                      E[:, bass.ds(t0 + k + ET, 1)], None, ALU.is_equal)
                            a.then_inc(hist_ready, 1)

            roots = [0]

            def inv_sqrt(v):
                roots[0] += 1
                dve.sem_inc(sem("to_root"), 1)
                dve.wait_ge(sem("rooted"), roots[0])
                link(dve.reciprocal(v, v))

            def layernorm(x, h, done=None, relu=True, gain=None, shift=None, tmp=None):
                xn, hn = nodes(x), nodes(h)
                link(dve.tensor_reduce(stat_a[:, :], xn, AX.X, ADD))
                link(dve.tensor_scalar(stat_a[:, :], stat_a[:, :], 1.0 / D, None, MUL))
                link(dve.tensor_tensor(hn, xn, bc(stat_a[:, :], D), SUB))
                link(dve.tensor_tensor(nodes(tmp), hn, hn, MUL))
                link(dve.tensor_reduce(stat_b[:, :], nodes(tmp), AX.X, ADD))
                link(dve.tensor_scalar(stat_b[:, :], stat_b[:, :], 1.0 / D, EPS, MUL, ADD))
                inv_sqrt(stat_b[:, :])
                a = dve.tensor_tensor(hn, hn, bc(stat_b[:, :], D), MUL)
                if relu:
                    link(a)
                    a = dve.tensor_scalar(h[:, 0:NP], h[:, 0:NP], 0.0, None, MAX)
                if gain is not None:
                    link(a)
                    link(dve.tensor_tensor(hn, hn, row_bc(rows[:, gain, :], NT), MUL))
                    a = dve.tensor_tensor(hn, hn, row_bc(rows[:, shift, :], NT), ADD)
                if done is None:
                    link(a)
                else:
                    a.then_inc(done, 1)
                    dve.wait_ge(done, 1)

            dve.memset(src_i[:, FULL:ET], 0)
            dve.memset(rel_i[:, FULL:ET], 0)
            dve.memset(weight_e[:, FULL:ET], 0.0)
            dve.memset(C[:, :], 0.0).then_inc(sem("padded"), 1)
            dve.memset(Ei[0:1, 0:EP - N_EDGES + 8], NP).then_inc(sem("padded"), 1)
            dve.memset(Bi[:, FULL:ET], NP).then_inc(sem("padded"), 1)
            dve.memset(O[:, :, :, :], 0.0)
            dve.sem_inc(selected, CREDIT_SEL)
            dve.sem_inc(evacuated, CREDIT_EV)
            dve.sem_inc(as_kept, 4)
            dve.sem_inc(hist_used, 2)
            dve.memset(dst_f[:, ET:ET + 1], -1.0)
            dve.wait_ge(sem("edges_in"), 16 * len(EDGES))
            dve.wait_ge(sem("dst_padded"), 64)
            dve.tensor_copy(dst_f[:, 0:ET], Bi[:, 0:ET])
            dve.tensor_scalar(Bi[:, ET:2 * ET], Bi[:, 0:ET], 127, None, ALU.bitwise_and)
            link(dve.tensor_scalar(Bi[:, 2 * ET:3 * ET], Bi[:, 0:ET], 7, None, ALU.logical_shift_right))
            dve.tensor_copy(E[:, 0:2 * ET], Bi[:, ET:3 * ET])
            dve.scalar_tensor_tensor(rel_i[:, :], src_i[:, :], float(RELS), rel_i[:, :], MUL, ADD
                                     ).then_inc(sem("edge_numbers"), 1)
            dve.wait_ge(sem("made"), 6)
            link(dve.tensor_copy(iota_f[:, :], iota_i[:, :]))
            dve.wait_ge(sem("weights_in"), 16 * len(LOADS))
            link(dve.tensor_scalar(cs_w[:, 2, :], cs[:, 3, :], cw[:, 1:2], None, MUL))
            dve.scalar_tensor_tensor(cs_w[:, 0, :], cs[:, 2, :], cw[:, 0:1], cs_w[:, 2, :], MUL, SUB
                                     ).then_inc(sem("filter"), 1)
            dve.wait_ge(sem("filter"), 1)
            link(dve.tensor_scalar(cs_w[:, 2, :], cs[:, 2, :], cw[:, 1:2], None, MUL))
            dve.scalar_tensor_tensor(cs_w[:, 1, :], cs[:, 3, :], cw[:, 0:1], cs_w[:, 2, :], MUL, ADD
                                     ).then_inc(sem("filter"), 1)
            dve.wait_ge(sem("filter_ps"), 1)
            dve.tensor_copy(c_mat[:, :], ps[0][:, 0:D]).then_inc(sem("filter_c"), 1)
            dve.wait_ge(sem("filter_ps"), 3)
            dve.scalar_tensor_tensor(w_tot[:, :], ps[1][:, 0:D], cols[:, 4:5], wf[:, 0, :], MUL, ADD
                                     ).then_inc(sem("w_tot"), 1)
            dve.scalar_tensor_tensor(cols[:, 5:6], ps[2][:, 0:1], cols[:, 4:5], cols[:, 0:1], MUL, ADD
                                     ).then_inc(sem("w_tot"), 1)
            dve.wait_ge(sem("x_in"), 32)
            dve.wait_ge(sem("seeds_zero"), 32)
            for k in range(SLOTS):
                dve.wait_ge(kept[k], 16)
            for k in range(2):
                dve.wait_ge(stored[k], 16)
            layernorm(X, A, sem("ln0"), tmp=C)
            dve.memset(hot_lo[:, 0, 0, :], 0.0)
            dve.memset(hot_hi[:, 0, 0, :], 0.0).then_inc(sem("hist_zero"), 1)
            dve.wait_ge(sem("hist_started"), 1)
            sweep(0, hist=True)
            dve.wait_ge(hist_used, NG + 2)
            dve.tensor_scalar(iota_f[:, :], tri[:, :], -1.0, 1.0, MUL, ADD)
            dve.tensor_copy(cnt[:, :], pt[0][:, 0:NT]).then_inc(sem("counts"), 1)
            dve.wait_ge(sem("counts"), 1)
            link(dve.tensor_scalar(mask[:, :], cnt[:, :], 1.0, None, MIN))
            link(dve.tensor_scalar(rcnt[:, :], cnt[:, :], 1.0, None, MAX))
            link(dve.reciprocal(rcnt[:, :], rcnt[:, :]))
            link(dve.tensor_tensor(rcnt[:, :], rcnt[:, :], mask[:, :], MUL))
            link(dve.tensor_scalar(dinv[:, :], cnt[:, :], 1.0, None, ADD))
            inv_sqrt(dinv[:, :])
            dve.wait_ge(sem("starts_ps"), 1)
            link(dve.tensor_copy(stat_a[:, :], ps[1][:, 0:NT]))
            link(dve.tensor_tensor_scan(stat_b[:, :], ones[:, 0:NT], stat_a[:, :], 0.0, MUL, ADD))
            link(dve.tensor_tensor(stat_b[:, :], stat_b[:, :], stat_a[:, :], SUB))
            link(dve.tensor_tensor(row_f[:, :], stat_b[:, :], ps[0][:, 0:NT], ADD))
            dve.tensor_copy(row_i[:, :], row_f[:, :]).then_inc(sem("row_starts"), 1)
            link(dve.tensor_scalar(stat_a[:, :], mask[:, :], -2.0 * EP, 2.0 * EP, MUL, ADD))
            link(dve.tensor_tensor(stat_a[:, :], stat_a[:, :], row_f[:, :], ADD))
            link(dve.tensor_copy(seed_i[:, :], stat_a[:, :]))
            dve.wait_ge(sem("nodes0"), 16 * NT)
            dve.tensor_tensor(nodes(C), nodes(C), bc(rcnt[:, :], D), MUL).then_inc(sem("agg"), 1)
            for n in range(14):
                dve.wait_ge(sem("mix_out"), n + 1)
                last = dve.bn_stats(bn_st[:, n, :], E[:, n * 448:min((n + 1) * 448, N_NODES)])
            link(last)
            link(dve.bn_aggr(bn[:, 0:2], bn_st[:, :, :].rearrange("p a b -> p (a b)")))
            link(dve.tensor_scalar(bn[:, 2:3], bn[:, 1:2], EPS, None, ADD))
            inv_sqrt(bn[:, 2:3])
            link(dve.tensor_scalar(bn[:, 2:3], bn[:, 2:3], cols[:, 2:3], None, MUL))
            for n in range(2):
                half = slice(n * NP // 2, (n + 1) * NP // 2)
                dve.tensor_scalar(E[:, half], E[:, half], bn[:, 0:1], bn[:, 2:3], SUB, MUL).then_inc(sem("bn_ready"), 1)
            for r in range(PTN):
                c = slice(r * T7 * P, (r + 1) * T7 * P)
                dve.wait_ge(sem("x1_ps"), r + 1)
                dve.tensor_tensor(X[:, c], X[:, c], pt[r % 2][:, 0:T7 * P], ADD).then_inc(sem("x1"), 1)
            dve.wait_ge(sem("x1"), PTN)
            dve.sem_inc(sem("x1_done"), 1)
            layernorm(X, A, sem("ln1"), tmp=C)
            w_rel = Db[:, 0:RELS * D].rearrange("p (r o) -> p r o", o=D)
            tmp = C[:, 0:RELS * D].rearrange("p (r o) -> p r o", o=D)
            dve.wait_ge(sem("bases_in"), 32)
            for b in range(BASES):
                link(dve.tensor_tensor(w_rel if b == 0 else tmp, bc(comp[:, :, b], D), row_bc(w_base[:, b, :], RELS), MUL))
                if b:
                    link(dve.tensor_tensor(w_rel, w_rel, tmp, ADD))
            dve.sem_inc(sem("rel_w"), 1)
            for n in range(NT):
                if n >= 2:
                    dve.wait_ge(sem(f"rel_stored{n % 2}"), 16 * (n // 2))
                for k in range(1, 8, 2):
                    dve.wait_ge(sem("rel_ps"), 8 * n + k + 1)
                    dve.tensor_copy((C, E)[n % 2][:, k * 512:(k + 1) * 512], ps[k % 4][:, :]).then_inc(sem("rel_dve"), 1)
            sweep(NG)
            dve.wait_ge(sem("nodes1"), 16 * NT)
            link(dve.tensor_tensor(nodes(C), nodes(C), bc(mask[:, :], D), MUL))
            link(dve.tensor_tensor(nodes(C), nodes(C), row_bc(rows[:, BIAS1, :], NT), ADD))
            link(dve.scalar_tensor_tensor(X[:, :], C[:, :], 0.0, X[:, :], MAX, ADD))
            layernorm(X, A, sem("ln2"), tmp=C)
            dve.wait_ge(sem("gat_rows"), PTN)
            for k, att in ((0, ATT_D), (1, ATT_S)):
                link(dve.tensor_tensor(nodes(Db), nodes(C), row_bc(rows[:, att, :], NT), MUL))
                link(dve.tensor_reduce(E[:, 0:NT * HEADS], Db.rearrange("p (t c) -> p t c", c=HC), AX.X, ADD))
                dve.tensor_copy(scores[:, :, k * HEADS:(k + 1) * HEADS],
                                E[:, 0:NT * HEADS].rearrange("p (t h) -> p t h", h=HEADS)
                                ).then_inc(sem("scores_ready"), 1)
                dve.wait_ge(sem("scores_ready"), k + 1)
            dve.wait_ge(as_kept, NG + 4)
            dve.wait_ge(sem("spilled"), 32)
            by_place = lambda v: v[:, 0:NP].rearrange("p (j h c) -> p j h c", h=HEADS, c=CH)
            by_tile = lambda v: v[:, 0:NP].rearrange("p (c j h) -> p j h c", c=CH, h=HEADS)
            for k, (to, of) in enumerate(((A, E), (Dw, B), (X, C))):
                if k == 1:
                    dve.wait_ge(sem("seeds_in"), 32)
                dve.tensor_copy(by_place(to), by_tile(of)).then_inc(sem("permuted"), 1)
            dve.wait_ge(sem("to_heads"), 3 * PTN)
            dve.wait_ge(sem("dst_heads"), 16 * 2 * HEADS)
            link(dve.tensor_tensor(E[:, :], Bi, Ci, ALU.not_equal))
            link(dve.tensor_scalar(B[:, :], E[:, :], BIG, -BIG, MUL, ADD))
            link(dve.tensor_tensor(X[:, :], X[:, :], B[:, :], ADD))
            link(dve.tensor_tensor(B[:, :], A[:, :], X[:, :], MAX))
            link(dve.tensor_scalar(C[:, :], E[:, :], -BIG, None, MUL))
            link(dve.tensor_scalar(X[:, :], E[:, :], -1.0, 1.0, MUL, ADD))

            hc = lambda v: v.rearrange("p (h c) -> p h c", c=CH)
            state, through, through_01, result, starts = (chain_row[0:1, k, :] for k in (0, 1, 2, 3, 5))
            events = [0, 0]

            def flags(first_edges):
                link(dve.tensor_reduce(end_col[:, 0:1], first_edges[:, 0:NP], AX.X, MAX))
                dve.sem_inc(sem("ends"), 1)
                events[0] += 1
                dve.wait_ge(sem("ends_ps"), events[0])
                link(dve.tensor_scalar(through_01, ps[0][0:1, 0:P], -1.0, 1.0, MUL, ADD))

            def chain(scan, data, rev, largest):
                zero = -BIG if largest else 0.0
                if largest:
                    link(dve.tensor_scalar(through, through_01, BIG, -BIG, MUL, ADD))
                else:
                    link(dve.tensor_copy(through, through_01))
                at = slice(CH - 1, CH) if rev else slice(0, 1)
                link(dve.memset(hc(through)[:, :, at], zero))
                link(scan(zero))
                at = slice(0, 1) if rev else slice(CE - 1, CE)
                link(dve.tensor_copy(end_col[:, 0:1], data[:, at]))
                dve.sem_inc(sem("ends"), 1)
                events[0] += 1
                events[1] += 1
                dve.wait_ge(sem("ends_ps"), events[0])
                link(dve.tensor_copy(state, ps[0][0:1, 0:P]))
                way = (lambda v: v[:, ::-1]) if rev else (lambda v: v)
                link(dve.tensor_tensor_scan(way(result), way(through), way(state), zero,
                                            ADD if largest else MUL, MAX if largest else ADD))
                link(dve.memset(starts, zero))
                if rev:
                    link(dve.tensor_copy(hc(starts)[:, :, 0:CH - 1], hc(result)[:, :, 1:CH]))
                else:
                    link(dve.tensor_copy(hc(starts)[:, :, 1:CH], hc(result)[:, :, 0:CH - 1]))
                dve.sem_inc(sem("starts"), 1)
                dve.wait_ge(sem("starts_c"), events[1])
                link(dve.tensor_copy(in_col[:, :], ps[1][:, 0:1]))
                link(scan(in_col[:, 0:1]))

            flags(E)
            chain(lambda z: dve.tensor_tensor_scan(E[:, :], X[:, :], Db, z, MUL, ADD), E, False, False)
            chain(lambda z: dve.tensor_tensor_scan(Db, C[:, :], B[:, :], z, ADD, MAX), Db, False, True)
            dve.sem_inc(sem("fwd_done"), 1)
            dve.wait_ge(sem("dst_heads2"), 16 * 2 * HEADS)
            link(dve.tensor_tensor(B[:, :], Bi, Ci, ALU.not_equal))
            link(dve.tensor_scalar(C[:, :], B[:, :], -BIG, None, MUL))
            flags(B)
            chain(lambda z: dve.tensor_tensor_scan(X[:, ::-1], C[:, ::-1], Db[:, ::-1], z, ADD, MAX), X, True, True)
            link(dve.tensor_tensor(A[:, :], A[:, :], E[:, :], ADD))
            link(dve.scalar_tensor_tensor(A[:, :], A[:, :], SLOPE, A[:, :], MUL, MAX))
            link(dve.tensor_tensor(B[:, :], X[:, :], E[:, :], ADD))
            link(dve.scalar_tensor_tensor(B[:, :], B[:, :], SLOPE, B[:, :], MUL, MAX))
            dve.tensor_tensor(A[:, :], A[:, :], B[:, :], SUB).then_inc(sem("exponents"), 1)
            dve.wait_ge(sem("from_heads"), 2 * PTN)
            sweep(2 * NG, weights=True)
            dve.wait_ge(sem("nodes2"), 16 * NT)
            dve.wait_ge(sem("h2_back"), 16)
            dve.wait_ge(sem("gat_back"), 16)
            dve.wait_ge(sem("x_back"), 16)
            agg = Dw[:, :].rearrange("p (t f) -> p t f", f=WL2)
            K = NT * HEADS
            e0, e1, e2, e3 = (E[:, k * K:(k + 1) * K] for k in range(4))
            th = lambda v: v.rearrange("p (t h) -> p t h", h=HEADS)
            a_d, a_s = scores[:, :, 0:HEADS], scores[:, :, HEADS:]
            link(dve.tensor_scalar(stat_a[:, :], mask[:, :], BIG, -BIG, MUL, ADD))
            link(dve.tensor_tensor(th(e0), agg[:, :, D + HEADS:], bc(mask[:, :], HEADS), MUL))
            link(dve.tensor_tensor(th(e0), th(e0), bc(stat_a[:, :], HEADS), ADD))
            link(dve.tensor_tensor(th(e0), th(e0), a_s, MAX))
            link(dve.tensor_tensor(th(e1), th(e0), a_d, ADD))
            link(dve.scalar_tensor_tensor(e1, e1, SLOPE, e1, MUL, MAX))
            link(dve.tensor_tensor(th(e2), a_s, a_d, ADD))
            link(dve.scalar_tensor_tensor(e2, e2, SLOPE, e2, MUL, MAX))
            dve.tensor_tensor(self_w[:, :], e2, e1, SUB).then_inc(sem("self_exponents"), 1)
            dve.wait_ge(sem("self_w"), 1)
            link(dve.tensor_tensor(th(e3), agg[:, :, D:D + HEADS], bc(mask[:, :], HEADS), MUL))
            link(dve.tensor_tensor(e3, e3, self_w[:, :], ADD))
            link(dve.reciprocal(e3, e3))
            heads = lambda v: v[:, 0:NP].rearrange("p (k c) -> p k c", c=HC)
            link(dve.tensor_tensor(heads(B), heads(C), bc(self_w[:, :], HC), MUL))
            link(dve.tensor_tensor(nodes(C), agg[:, :, 0:D], bc(mask[:, :], D), MUL))
            link(dve.tensor_tensor(B[:, :], B[:, :], C[:, :], ADD))
            link(dve.tensor_tensor(heads(B), heads(B), bc(e3, HC), MUL))
            link(dve.tensor_tensor(nodes(B), nodes(B), row_bc(rows[:, B_GAT, :], NT), ADD))
            link(dve.tensor_tensor(B[:, :], B[:, :], A[:, :], ADD))
            layernorm(B, A, sem("ln_a"), relu=False, gain=G1, shift=BB1, tmp=C)
            for n in range(14):
                dve.wait_ge(sem("ff2_ps"), n + 1)
                dve.tensor_copy(Dw[:, n * 448:(n + 1) * 448], ps[2 + n % 2][:, 0:448]).then_inc(sem("ff2"), 1)
            for r in range(PTN):
                c = slice(r * T7 * P, (r + 1) * T7 * P)
                dve.wait_ge(sem("ffb_ps"), r + 1)
                dve.tensor_tensor(C[:, c], A[:, c], pt[r % 2][:, 0:T7 * P], ADD).then_inc(sem("ffb"), 1)
            dve.wait_ge(sem("ffb"), PTN)
            link(dve.tensor_tensor(nodes(C), nodes(C), row_bc(rows[:, B2, :], NT), ADD))
            layernorm(C, B, relu=False, gain=G2, shift=BB2, tmp=E)
            link(dve.tensor_tensor(X[:, :], X[:, :], B[:, :], ADD))
            layernorm(X, A, tmp=C)
            link(dve.tensor_scalar(stat_a[:, :], dinv[:, :], TELEPORT, None, MUL))
            link(dve.tensor_tensor(nodes(B), nodes(A), bc(stat_a[:, :], D), MUL))
            link(dve.tensor_tensor(sc_a[:, :], dinv[:, :], dinv[:, :], MUL))
            link(dve.tensor_scalar(sc_a[:, :], sc_a[:, :], 1.0 - TELEPORT, None, MUL))
            link(dve.tensor_tensor(sc_b[:, :], sc_a[:, :], mask[:, :], MUL))
            dve.tensor_tensor(nodes(C), nodes(A), bc(dinv[:, :], D), MUL).then_inc(sem("y_ready"), 1)
            dve.wait_ge(sem("y_ready"), 1)
            with dve.Fori(0, STEPS) as s:
                sweep((s + 3) * NG)
                step = sem("step_link")
                dve.tensor_tensor(nodes(E), nodes(C), bc(sc_a[:, :], D), MUL).then_inc(step, 1)
                dve.wait_ge(step, s * 3 + 1)
                dve.tensor_tensor(E[:, :], E[:, :], B[:, :], ADD).then_inc(step, 1)
                dve.wait_ge(sem("nodes3"), s * (16 * NT) + 16 * NT)
                dve.tensor_tensor(nodes(Db), nodes(Db), bc(sc_b[:, :], D), MUL).then_inc(step, 1)
                dve.wait_ge(step, s * 3 + 3)
                dve.wait_ge(sem("y_stored"), s * 16 + 16)
                dve.tensor_tensor(C[:, :], E[:, :], Db, ADD).then_inc(sem("y_ready"), 1)
                dve.wait_ge(sem("y_ready"), s + 2)
            link(dve.reciprocal(dinv[:, :], dinv[:, :]))
            link(dve.tensor_tensor(nodes(C), nodes(C), bc(dinv[:, :], D), MUL))
            dve.scalar_tensor_tensor(X[:, :], C[:, :], 0.0, X[:, :], MAX, ADD).then_inc(sem("out_ready"), 1)


def kernel(**inputs):
    import concourse.bacc as bacc
    from concourse.bass_utils import run_bass_kernel_spmd as run

    full = FULL * P
    k, n = np.arange(FREQ)[:, None], np.arange(D)[None, :]
    share = np.where((k == 0) | (k == D // 2), 1.0, 2.0) / D
    turn = 2 * np.pi * ((k * n) % D) / D
    cos, sin = np.cos(turn), np.where((k * n) % (D // 2) == 0, 0.0, np.sin(turn))
    fourier = np.stack([cos, sin, share * cos, share * sin], axis=1).astype(np.float32)

    def cols(a):
        return np.ascontiguousarray(np.asarray(a).reshape(-1)[:full].reshape(FULL, P).T)

    flat = {name: np.asarray(v) for name, v in inputs.items()}
    arrays = {
        "x": flat["x"], "src": flat["src"], "dst": flat["dst"], "etype": flat["edge_type_32"],
        "norm": flat["edge_weight1"].reshape(-1), "src_cols": cols(flat["src"]), "dst_cols": cols(flat["dst"]),
        "etype_cols": cols(flat["edge_type_32"]), "norm_cols": cols(flat["edge_weight1"]), "fourier": fourier,
        "w_fuse_t": np.ascontiguousarray(flat["L0_gnn_W_fuse"].T), "alpha": flat["L0_gnn_alpha"].reshape(1),
        "w_in": flat["L0_gnn_W_in"], "b_fuse": flat["L0_gnn_b_fuse"], "b_in": flat["L0_gnn_b_in"],
        "complex_weight": flat["L0_gnn_complex_weight"], "gamma": flat["L0_gnn_gamma"], "beta": flat["L0_gnn_beta"],
        "weight": flat["L1_gnn_weight"], "w_comp": flat["L1_gnn_w_comp"], "bias_param": flat["L1_gnn_bias_param"],
        "w_gat": flat["L2_gnn_W_gat"], "att_src": flat["L2_gnn_att_src"], "att_dst": flat["L2_gnn_att_dst"],
        "b_gat": flat["L2_gnn_b_gat"], "w1": flat["L2_gnn_W1"], "b1": np.ascontiguousarray(flat["L2_gnn_b1"].reshape(4, P).T),
        "w2": flat["L2_gnn_W2"], "b2": flat["L2_gnn_b2"], "ln1_g": flat["L2_gnn_ln1_g"], "ln1_b": flat["L2_gnn_ln1_b"],
        "ln2_g": flat["L2_gnn_ln2_g"], "ln2_b": flat["L2_gnn_ln2_b"],
    }
    nc = bacc.Bacc("TRN2", target_bir_lowering=False, num_devices=1)
    aps = {name: nc.dram_tensor(f"in_{name}", a.shape, mybir.dt.from_np(a.dtype), kind="ExternalInput").ap()
           for name, a in arrays.items()}
    out = nc.dram_tensor("out_x", (N_NODES, D), F32, kind="ExternalOutput").ap()
    build(nc, aps, out)
    r = run(nc, [{f"in_{name}": a for name, a in arrays.items()}], core_ids=[0])
    return r.results[0]["out_x"]
```

```python
from contextlib import ExitStack

import numpy as np

import concourse.bass as bass
from concourse import mybir

P = 128
N_NODES, N_EDGES, D = 6250, 100000, 128
NT = (N_NODES + P - 1) // P
NP = NT * P
GT = 4
SLOTS = 4
NG = 196
ET = NG * GT
EP = ET * P
GE_ROWS = GT * P
FULL = N_EDGES // P
REST = N_EDGES - FULL * P
FRONT = 2 * GE_ROWS
RELS, BASES, HEADS, HC, FF = 32, 8, 8, 16, 512
CH = 16
CE = EP // CH
CT = ET // CH
FREQ = D // 2 + 1
BIG = 1.0e30
EPS = 1e-5
STEPS, TELEPORT, SLOPE = 10, 0.1, 0.2
WL2 = D + 2 * HEADS

ADJ_SLOTS = 7
ADJ_PITCH = 1 << 13
MOST = 16
MOST_DEGREE = P
EARLIER = 1024
WIN = (GT + 2) * P
SCALE = 1024.0

F32, I32, BF16 = mybir.dt.float32, mybir.dt.int32, mybir.dt.bfloat16
F16, F8, U8 = mybir.dt.float16, mybir.dt.float8e4, mybir.dt.uint8
ALU, ACT, AX = mybir.AluOpType, mybir.ActivationFunctionType, mybir.AxisListType
ADD, SUB, MUL, MAX, MIN = ALU.add, ALU.subtract, ALU.mult, ALU.max, ALU.min


def build(nc, t, out):
    ctx = ExitStack()
    with ctx:
        def sb(name, shape, dt=F32):
            return ctx.enter_context(nc.sbuf_tensor(name, shape, dt))

        def dram(name, shape, dt=F32):
            return nc.dram_tensor(name, shape, dt).ap()

        names = {}

        def sem(name):
            if name not in names:
                names[name] = ctx.enter_context(nc.semaphore(name))
            return names[name]

        dst_pad = dram("dst_pad", (FRONT + EP + P,), I32)
        src_pad = dram("src_pad", (P + EP + P,), I32)
        adj = dram("adj", (NP, ADJ_PITCH), U8)
        table = dram("table", (NP, D))
        rel_table = dram("rel_table", (NP * RELS, D))
        gat_table = dram("gat_table", (NP, D + HEADS))
        x_spill = dram("x_spill", (NP, D))
        runs = dram("runs", (EP, D))
        runs2 = dram("runs2", (EP, WL2))
        edge_rows = dram("edge_rows", (EP, D))
        seeds = dram("seeds", (EP, 2 * HEADS))

        X, A, B, C, E = (sb(n, [P, NP]) for n in ("X", "A", "B", "C", "E"))
        arena = sb("arena", [P, NT * WL2 + SLOTS * GT * (D + HEADS) + 4 * GT * P + 2 * GE_ROWS])
        at = [0]

        def part(n):
            at[0] += n
            return arena[:, at[0] - n:at[0]]

        Dw = part(NT * WL2)
        Db = Dw[:, 0:NP]

        def nodes(v):
            return v[:, 0:NP].rearrange("p (t f) -> p t f", f=D)

        def halves(v):
            return v[:, 0:NP].bitcast(F16).rearrange("p (t f) -> p t f", f=2 * D)

        def bc(v, n):
            return v.unsqueeze(2).to_broadcast([v.shape[0], v.shape[1], n])

        def row_bc(v, n):
            return v.unsqueeze(1).to_broadcast([v.shape[0], n, v.shape[1]])

        src_i = sb("src_i", [P, ET], I32)
        rel_i = sb("rel_i", [P, ET], I32)
        dst_f = sb("dst_f", [P, ET + 1])
        weight_e = sb("weight_e", [P, ET])
        G = part(SLOTS * GT * (D + HEADS)).rearrange("p (s k f) -> p s k f", s=SLOTS, k=GT)
        idx = sb("idx", [P, SLOTS, GT], I32)
        O = sb("O", [P, 2, GT, WL2])
        S = part(2 * GT * P).rearrange("p (s k e) -> p s k e", s=2, k=GT)
        carry_mask = part(2 * GT * P)[0:1, :].rearrange("p (s k e) -> p s k e", s=2, k=GT)
        dst_b = part(2 * GE_ROWS).bitcast(I32).rearrange("p (s e) -> p s e", s=2)
        adj_ring = arena[:, 0:ADJ_SLOTS * NP // 4].bitcast(F8).rearrange("p (s f) -> p s f", s=ADJ_SLOTS)
        vals = sb("vals", [P, SLOTS, GT], U8)
        verdict = sb("verdict", [1, 1], I32)
        win = Dw[:, 0:4 * WIN].bitcast(I32).rearrange("p (a s e) -> p a s e", a=2, s=2)
        codes = Dw[:, 4 * WIN:4 * WIN + ET]
        window_w = Dw[:, 4 * WIN + ET:4 * WIN + ET + 3 * P]
        same = Dw[:, 4 * WIN + ET + 3 * P:4 * WIN + ET + 12 * P].rearrange("p (a e) -> p a e", a=3)
        ident, tri = (sb(n, [P, P]) for n in ("ident", "tri"))
        ones, iota_f = Dw[:, NP:NP + P], Dw[:, NP + P:NP + 2 * P]
        iota_i = A[:, 0:P].bitcast(I32)
        hot_lo = C[:, 0:GT * P].bitcast(BF16).rearrange("p (a k n) -> p a k n", a=2, k=GT)
        hot_hi = C[:, 1024:1024 + GT * NT].bitcast(BF16).rearrange("p (a k n) -> p a k n", a=2, k=GT)
        (cnt, mask, rcnt, dinv, row_f, stat_a, stat_b, sc_a, sc_b) = (
            sb(n, [P, NT]) for n in ("cnt", "mask", "rcnt", "dinv", "row_f", "stat_a", "stat_b", "sc_a", "sc_b"))
        row_i, seed_i = sb("row_i", [P, NT], I32), sb("seed_i", [P, NT], I32)
        scores = sb("scores", [P, NT, 2 * HEADS])
        self_w = sb("self_w", [P, NT * HEADS])
        wf = sb("wf", [P, 2, D])
        w_tot = sb("w_tot", [P, D])
        w_in, c_mat = Dw[:, 0:D], Dw[:, D:2 * D]
        cs = Dw[0:FREQ, 2 * D:6 * D].rearrange("p (a f) -> p a f", f=D)
        cs_w = Dw[0:FREQ, 6 * D:9 * D].rearrange("p (a f) -> p a f", f=D)
        cols = sb("cols", [P, 8])
        cw = sb("cw", [FREQ, 2])
        w_base = Dw[:, RELS * D:(RELS + BASES) * D].rearrange("p (b o) -> p b o", o=D)
        comp = Dw[:, (RELS + BASES) * D:(RELS + BASES) * D + RELS * BASES].rearrange("p (r b) -> p r b", b=BASES)
        rows = sb("rows", [P, 9, D])
        w_gat, w1, w2, b1 = sb("w_gat", [P, D]), sb("w1", [P, FF]), sb("w2", [P, 4, D]), sb("b1", [P, 4])
        bn_st, bn = sb("bn_st", [P, 14, 6]), sb("bn", [P, 4])
        end_col, in_col = sb("end_col", [P, 2]), sb("in_col", [P, 1])
        chain_row = S[0:1, :, :, :].rearrange("p a k e -> p (a k) e")
        (BIAS1, ATT_S, ATT_D, B_GAT, G1, BB1, G2, BB2, B2) = range(9)

        ps = [ctx.enter_context(nc.psum_tensor(f"ps{k}", [P, 512], F32)) for k in range(4)]
        pt = [ctx.enter_context(nc.psum_tensor(f"pt{k}", [P, 1024], F32)) for k in range(2)]
        T7 = 7
        PTN = NT // T7

        gathered = [sem(f"gathered{k}") for k in range(SLOTS)]
        reloaded = [sem(f"reloaded{k}") for k in range(SLOTS)]
        dst_in = [sem(f"dst_in{k}") for k in range(2)]
        stored = [sem(f"stored{k}") for k in range(2)]
        kept = [sem(f"kept{k}") for k in range(SLOTS)]
        idx_set, summed, evacuated, selected = sem("idx_set"), sem("summed"), sem("evacuated"), sem("selected")
        scaled, hist_ready, hist_used, as_kept, max_kept = (
            sem(n) for n in ("scaled", "hist_ready", "hist_used", "as_kept", "max_kept"))
        CREDIT_SUM, CREDIT_EV, CREDIT_SEL = SLOTS * GT, 4, 2

        def settle(eng):
            eng.sem_inc(sem("settled"), 1)

        table_v = table.rearrange("(t p) f -> p t f", p=P)
        spill_v = x_spill.rearrange("(t p) f -> p t f", p=P)
        gat_v = gat_table.rearrange("(t p) f -> p t f", p=P)
        out_full = (N_NODES // P) * P

        LOADS = []
        for k, n in enumerate(("b_fuse", "b_in", "gamma", "beta")):
            LOADS.append((cols[:, k:k + 1], t[n].rearrange("(p a) -> p a", a=1)))
        LOADS.append((cols[:, 4:5], t["alpha"].rearrange("(a b) -> a b", a=1).to_broadcast([P, 1])))
        LOADS.append((wf[:, :, :], t["w_fuse_t"].rearrange("(a p) o -> p a o", p=P)))
        LOADS.append((w_in[:, :], t["w_in"]))
        LOADS.append((cs[:, :, :], t["fourier"]))
        LOADS.append((cw[:, :], t["complex_weight"]))
        for k, n in enumerate(("bias_param", "att_src", "att_dst", "b_gat", "ln1_g", "ln1_b", "ln2_g", "ln2_b", "b2")):
            v = t[n] if len(t[n].shape) == 1 else t[n].rearrange("h c -> (h c)")
            LOADS.append((rows[:, k, :], v.rearrange("(a f) -> a f", a=1).to_broadcast([P, D])))
        LOADS.append((w_gat[:, :], t["w_gat"]))
        LOADS.append((w1[:, :], t["w1"]))
        LOADS.append((w2[:, :, :], t["w2"].rearrange("(c p) o -> p c o", p=P)))
        LOADS.append((b1[:, :], t["b1"]))
        EDGES = []
        for v, n in ((src_i, "src"), (rel_i, "etype"), (weight_e, "norm"), (B[:, :].bitcast(I32), "dst")):
            EDGES.append((v[:, 0:FULL], t[n + "_cols"]))
            EDGES.append((v[0:REST, FULL:FULL + 1], t[n][FULL * P:N_EDGES].rearrange("(p a) -> p a", a=1)))
        Bi, Ci, Ei = (v[:, :].bitcast(I32) for v in (B, C, E))

        block = ctx.enter_context(nc.Block())

        @block.sync
        def _(sp):
            def group_of(i):
                return NG - 1 - i

            def load_dst(slot, q):
                sp.dma_start(dst_b[:, slot, :],
                             dst_pad[bass.ds(q * GE_ROWS + FRONT, GE_ROWS)].rearrange("(a e) -> a e", a=1)
                             .to_broadcast([P, GE_ROWS])).then_inc(dst_in[slot], 16)

            def sweep(base, base_pairs, to, width, reload=False):
                def load_rows(slot, q):
                    sp.dma_start(G[:, slot, :, 0:D],
                                 edge_rows[bass.ds(q * GE_ROWS, GE_ROWS), :].rearrange("(t p) f -> p t f", p=P)
                                 ).then_inc(reloaded[slot], 16)
                to_v = to.rearrange("(t p) f -> p t f", p=P)

                def groups(j, last=False):
                    for u in range(SLOTS):
                        i = j * SLOTS + u
                        sp.wait_ge(evacuated, (i + base) * GT + GT + CREDIT_EV)
                        if width == WL2:
                            settle(sp)
                            sp.wait_ge(max_kept, i + 1)
                        settle(sp)
                        sp.dma_start(to_v[:, bass.ds(group_of(i) * GT, GT), :],
                                     O[:, u % 2, :, 0:width]).then_inc(stored[u % 2], 16)
                        if reload and not last:
                            load_rows(u, group_of(i) - SLOTS)
                        sp.wait_ge(selected, i + base + 1 + CREDIT_SEL)
                        settle(sp)
                        load_dst(u % 2, group_of(i) - 2)

                if not reload:
                    with sp.Fori(0, NG // SLOTS) as j:
                        groups(j)
                    return
                for u in range(SLOTS):
                    load_rows(u, group_of(u))
                with sp.Fori(0, NG // SLOTS - 1) as j:
                    groups(j)
                groups(NG // SLOTS - 1, last=True)

            sp.wait_ge(sem("padded"), 4)
            for dst_ap, src_ap in EDGES:
                sp.dma_start(dst_ap, src_ap).then_inc(sem("edges_in"), 16)
            full = N_NODES // P
            sp.dma_start(nodes(X)[:, 0:full, :], t["x"][0:full * P, :].rearrange("(t p) f -> p t f", p=P)
                         ).then_inc(sem("x_in"), 16)
            sp.dma_start(nodes(X)[0:N_NODES - full * P, full, :], t["x"][full * P:N_NODES, :]).then_inc(sem("x_in"), 16)
            tail = EP - N_EDGES
            sp.dma_start(dst_pad[FRONT:FRONT + N_EDGES], t["dst"]).then_inc(sem("dst_padded"), 16)
            sp.dma_start(dst_pad[0:FRONT - tail], t["dst"][EP - FRONT:N_EDGES]).then_inc(sem("dst_padded"), 16)
            pad = Ei[0:1, 0:tail + P]
            sp.dma_start(dst_pad[FRONT - tail:FRONT], pad[:, 0:tail]).then_inc(sem("dst_padded"), 16)
            sp.dma_start(dst_pad[FRONT + N_EDGES:FRONT + EP + P], pad).then_inc(sem("dst_padded"), 16)
            sp.dma_start(src_pad[P:P + N_EDGES], t["src"]).then_inc(sem("dst_padded"), 16)
            sp.dma_start(src_pad[0:P], pad[:, 0:P]).then_inc(sem("dst_padded"), 16)
            sp.dma_start(src_pad[P + N_EDGES:P + EP + P], pad).then_inc(sem("dst_padded"), 16)
            for dst_ap, src_ap in LOADS:
                sp.dma_start(dst_ap, src_ap).then_inc(sem("weights_in"), 16)
            sz = 2 * HEADS * EP // P
            seeds_z = seeds.rearrange("(p a) f -> p (a f)", p=P)
            for k in range(2):
                sp.dma_start(seeds_z[:, k * (sz // 2):(k + 1) * (sz // 2)], C[:, 0:sz // 2]
                             ).then_inc(sem("seeds_zero"), 16)
            for k in range(2):
                sp.dma_start(runs[k * P:(k + 1) * P, :], C[:, 0:D]).then_inc(stored[k], 16)
            for k in range(SLOTS):
                sp.dma_start(edge_rows[k * P:(k + 1) * P, :], C[:, 0:D]).then_inc(kept[k], 16)
            sp.wait_ge(sem("dst_padded"), 112)
            load_dst(0, NG - 1)
            load_dst(1, NG - 2)
            sp.wait_ge(sem("ln0"), 1)
            sp.dma_start(table_v, nodes(A)).then_inc(sem("table0"), 16)
            sp.wait_ge(sem("zeros"), 1)
            adj_v = adj.rearrange("(j p) b -> p j b", p=P)
            for j in range(0, NT, 4):
                n = min(4, NT - j)
                sp.dma_start(adj_v[:, j:j + n, 0:NP],
                             A[:, 0:n * NP // 4].bitcast(U8).rearrange("p (j b) -> p j b", j=n)
                             ).then_inc(sem("adj_zero"), 16)
            sweep(0, 0, runs, D)
            sp.wait_ge(sem("ln1"), 1)
            sp.dma_start(w_base, t["weight"].rearrange("b i o -> i b o")).then_inc(sem("bases_in"), 16)
            sp.dma_start(comp.rearrange("p r b -> p (r b)"),
                         t["w_comp"].rearrange("(a r) b -> a (r b)", a=1).to_broadcast([P, RELS * BASES])
                         ).then_inc(sem("bases_in"), 16)
            rel_v = rel_table.rearrange("(t p r) o -> t p (r o)", p=P, r=RELS)
            for n in range(NT):
                sp.wait_ge(sem("rel_act"), 4 * (n + 1))
                sp.wait_ge(sem("rel_dve"), 4 * (n + 1))
                sp.dma_start(rel_v[n], (C, E)[n % 2][:, 0:RELS * D]).then_inc(sem(f"rel_stored{n % 2}"), 16)
            sweep(NG, 0, runs, D)
            sp.wait_ge(sem("ln2"), 1)
            sp.dma_start(table_v, nodes(A)).then_inc(sem("spilled"), 16)
            sp.dma_start(spill_v, nodes(X)).then_inc(sem("spilled"), 16)
            sp.wait_ge(sem("gat_rows"), PTN)
            sp.dma_start(gat_v[:, :, 0:D], nodes(C)).then_inc(sem("gat_stored"), 16)
            sp.wait_ge(sem("scores_ready"), 2)
            sp.dma_start(gat_v[:, :, D:D + HEADS], scores[:, :, HEADS:]).then_inc(sem("gat_stored"), 16)
            rows_v = edge_rows.rearrange("(t p) f -> p t f", p=P)

            def load_window(slot, q):
                for k, (of, front) in enumerate(((dst_pad, FRONT), (src_pad, P))):
                    sp.dma_start(win[:, k, slot, :], of[bass.ds(q * GE_ROWS + front - P, WIN)]
                                 .rearrange("(a e) -> a e", a=1).to_broadcast([P, WIN])
                                 ).then_inc(sem(f"window_in{slot}"), 16)

            def keep_groups(j, last=False):
                for u in range(SLOTS):
                    i = j * SLOTS + u
                    sp.wait_ge(gathered[u], (j + 1 + 2 * (NG // SLOTS)) * (16 * GT))
                    if not last:
                        settle(sp)
                    sp.dma_start(rows_v[:, bass.ds(i * GT, GT), :], G[:, u, :, 0:D]).then_inc(kept[u], 16)
                    if not last or u < SLOTS - 2:
                        sp.wait_ge(sem("searched"), i + 1)
                        if not last:
                            settle(sp)
                        load_window(u % 2, i + 2)

            sp.wait_ge(sem("scores_ready"), 2)
            for k in range(2):
                load_window(k, k)
            with sp.Fori(0, NG // SLOTS - 1) as j:
                keep_groups(j)
            keep_groups(NG // SLOTS - 1, last=True)
            for k in range(SLOTS):
                sp.wait_ge(kept[k], 16 * (NG // SLOTS) + 16)
            sp.wait_ge(sem("seeded"), 16 * NT)
            sp.wait_ge(sem("spilled"), 32)
            sp.wait_ge(sem("gat_stored"), 32)
            seeds_v = seeds.rearrange("(t p) f -> p t f", p=P)
            with nc.allow_non_contiguous_dma(reason="32-byte rows"):
                sp.dma_start(B[:, :].rearrange("p (t h) -> p t h", h=HEADS), seeds_v[:, :, 0:HEADS]
                             ).then_inc(sem("seeds_in"), 16)
                sp.dma_start(C[:, :].rearrange("p (t h) -> p t h", h=HEADS), seeds_v[:, :, HEADS:]
                             ).then_inc(sem("seeds_in"), 16)

            def load_head_major(v, shift, name):
                for h in range(HEADS):
                    sp.dma_start(v[h * CH:(h + 1) * CH, :],
                                 dst_pad[FRONT + shift:FRONT + shift + EP].rearrange("(c e) -> c e", c=CH)
                                 ).then_inc(sem(name), 16)
            sp.wait_ge(sem("to_heads"), 3 * PTN)
            load_head_major(Bi, 0, "dst_heads")
            load_head_major(Ci, -1, "dst_heads")
            sp.wait_ge(sem("fwd_done"), 1)
            load_head_major(Bi, 0, "dst_heads2")
            load_head_major(Ci, 1, "dst_heads2")
            sp.wait_ge(sem("from_heads"), 2 * PTN)
            sp.dma_start(nodes(A), table_v).then_inc(sem("h2_back"), 16)
            sp.dma_start(nodes(X), spill_v).then_inc(sem("x_back"), 16)
            sweep(2 * NG, 0, runs2, WL2, reload=True)
            sp.dma_start(nodes(C), gat_v[:, :, 0:D]).then_inc(sem("gat_back"), 16)
            sp.wait_ge(sem("judged"), 1)
            dense = sp.value_load(verdict[0:1, 0:1], min_val=0, max_val=1)
            adj_r = adj.rearrange("(j p) b -> p j b", p=P)
            ring_u8 = arena[:, 0:ADJ_SLOTS * NP // 4].bitcast(U8).rearrange("p (s f) -> p s f", s=ADJ_SLOTS)
            for k in range(2):
                sp.wait_ge(dst_in[k], 16 * (NG // 2) * 3 + 16)
                sp.wait_ge(stored[k], 16 * (NG // 2) * 3 + 16)
            with sp.If(dense == 1):
                def load_adj(u, j):
                    sp.dma_start(ring_u8[:, u:u + 1, :], adj_r[:, bass.ds(j, 1), 0:NP]).then_inc(sem(f"adj_in{u}"), 16)
                sp.wait_ge(sem("scattered_all"), 1)
                sp.wait_ge(sem("ffb"), PTN)
                for u in range(ADJ_SLOTS):
                    load_adj(u, u)
                with sp.Fori(0, STEPS) as s:
                    with sp.Fori(0, NT // ADJ_SLOTS - 1) as a:
                        for u in range(ADJ_SLOTS):
                            sp.wait_ge(sem("multiplied"), s * NT + a * ADJ_SLOTS + u + 1)
                            settle(sp)
                            load_adj(u, a * ADJ_SLOTS + (u + ADJ_SLOTS))
                    for u in range(ADJ_SLOTS):
                        sp.wait_ge(sem("multiplied"), s * NT + (NT - ADJ_SLOTS + u + 1))
                        settle(sp)
                        load_adj(u, u)
                for u in range(ADJ_SLOTS):
                    sp.wait_ge(sem(f"adj_in{u}"), 16 * (STEPS * NT // ADJ_SLOTS + 1))
            with sp.Else():
                with sp.Fori(0, STEPS) as s:
                    sp.wait_ge(sem("y_ready"), s + 1)
                    sp.dma_start(table_v, nodes(C)).then_inc(sem("y_stored"), 16)
                    sweep((s + 3) * NG, 0, runs, D)
                for k in range(2):
                    sp.wait_ge(stored[k], 16 * (NG // 2) * (3 + STEPS) + 16)
                    sp.wait_ge(dst_in[k], 16 * (NG // 2) * (3 + STEPS) + 16)
                sp.wait_ge(sem("y_stored"), 16 * STEPS)
            sp.wait_ge(sem("out_ready"), 1)
            sp.dma_start(out[0:full * P, :].rearrange("(t p) f -> p t f", p=P), nodes(X)[:, 0:full, :]
                         ).then_inc(sem("out_stored"), 16)
            sp.dma_start(out[full * P:N_NODES, :], nodes(X)[0:N_NODES - full * P, full, :]
                         ).then_inc(sem("out_stored"), 16)
            sp.wait_ge(sem("out_stored"), 32)

        @block.gpsimd
        def _(pool):
            pool.memset(nodes(X)[:, NT - 1, :], 0.0).then_inc(sem("padded"), 1)
            pool.memset(ident[:, :], 0.0).then_inc(sem("made"), 1)
            pool.memset(tri[:, :], 1.0).then_inc(sem("made"), 1)
            pool.memset(ones[:, :], 1.0).then_inc(sem("made"), 1)
            pool.iota(iota_i[:, :], pattern=[[1, P]], base=0, channel_multiplier=0).then_inc(sem("made"), 1)
            pool.wait_ge(sem("made"), 4)
            pool.affine_select(out=ident[:, :], in_=ident[:, :], compare_op=ALU.not_equal, fill=1.0, base=0,
                               pattern=[[-1, P]], channel_multiplier=1).then_inc(sem("made"), 1)
            pool.affine_select(out=tri[:, :], in_=tri[:, :], compare_op=ALU.is_ge, fill=0.0, base=0,
                               pattern=[[-1, P]], channel_multiplier=1).then_inc(sem("made"), 1)

            def sweep(p, rows_ap, indices, keep=False):
                with pool.Fori(0, NG // SLOTS) as j:
                    for u in range(SLOTS):
                        i = j * SLOTS + u
                        if keep:
                            pool.wait_ge(kept[u], j * 16 + 16)
                            settle(pool)
                            pool.wait_ge(as_kept, i + 1)
                        else:
                            pool.wait_ge(summed, (p * NG + i) * GT + GT)
                        settle(pool)
                        q = i if keep else NG - 1 - i
                        pool.tensor_copy(idx[:, u, :], indices[:, bass.ds(q * GT, GT)]).then_inc(idx_set, 1)
                        pool.wait_ge(idx_set, p * NG + i + 1)
                        settle(pool)
                        for k in range(GT):
                            w = rows_ap.shape[1]
                            pool.indirect_dma_start(
                                out=G[:, u, k, 0:w], out_offset=None, in_=rows_ap,
                                in_offset=bass.IndirectOffsetOnAxis(ap=idx[:, u, k:k + 1], axis=0)
                            ).then_inc(gathered[u], 16)

            def node_rows(rows_ap, to_v, done):
                for n in range(NT):
                    pool.indirect_dma_start(
                        out=to_v[:, n, :], out_offset=None, in_=rows_ap,
                        in_offset=bass.IndirectOffsetOnAxis(ap=row_i[:, n:n + 1], axis=0)).then_inc(done, 16)

            def wait_runs(passes):
                for k in range(2):
                    pool.wait_ge(stored[k], passes * (16 * (NG // 2)) + 16)
                    settle(pool)

            pool.wait_ge(sem("edge_numbers"), 1)
            pool.wait_ge(sem("table0"), 16)
            sweep(0, table, src_i)
            wait_runs(1)
            pool.wait_ge(sem("row_starts"), 1)
            node_rows(runs, nodes(C), sem("nodes0"))
            for k in range(2):
                pool.wait_ge(sem(f"rel_stored{k}"), 16 * ((NT + 1 - k) // 2))
            sweep(1, rel_table, rel_i)
            wait_runs(2)
            node_rows(runs, nodes(C), sem("nodes1"))
            pool.wait_ge(sem("seeds_zero"), 32)
            pool.wait_ge(sem("scores_ready"), 2)
            for n in range(NT):
                pool.indirect_dma_start(
                    out=seeds, out_offset=bass.IndirectOffsetOnAxis(ap=seed_i[:, n:n + 1], axis=0),
                    in_=scores[:, n, :], in_offset=None, bounds_check=EP - 1, oob_is_err=False
                ).then_inc(sem("seeded"), 16)
            pool.wait_ge(sem("gat_stored"), 32)
            pool.wait_ge(summed, 2 * NG * GT + CREDIT_SUM)
            sweep(2, gat_table, src_i, keep=True)
            pool.wait_ge(sem("judged"), 1)
            pool.wait_ge(sem("adj_zero"), 16 * 13)
            cells = adj.rearrange("r (b a) -> (r b) a", a=1)
            counts = weight_e[:, 0:ET // 4].bitcast(U8)

            def scatter_groups(j, first=False):
                for u in range(SLOTS):
                    if not first:
                        pool.wait_ge(sem(f"scattered{u}"), j * (16 * GT))
                        settle(pool)
                    q = j * SLOTS + u
                    pool.tensor_copy(idx[:, u, :], rel_i[:, bass.ds(q * GT, GT)]).then_inc(sem("cells_set"), 1)
                    pool.tensor_copy(vals[:, u, :], counts[:, bass.ds(q * GT, GT)]).then_inc(sem("cells_set"), 1)
                    pool.wait_ge(sem("cells_set"), q * 2 + 2)
                    if not first:
                        settle(pool)
                    for k in range(GT):
                        pool.indirect_dma_start(
                            out=cells, out_offset=bass.IndirectOffsetOnAxis(ap=idx[:, u, k:k + 1], axis=0),
                            in_=vals[:, u, k:k + 1], in_offset=None, bounds_check=NP * ADJ_PITCH - 1,
                            oob_is_err=False).then_inc(sem(f"scattered{u}"), 16)

            for u in range(SLOTS):
                pool.wait_ge(gathered[u], 3 * (NG // SLOTS) * 16 * GT)
            scatter_groups(0, first=True)
            with pool.Fori(1, NG // SLOTS) as j:
                scatter_groups(j)
            for u in range(SLOTS):
                pool.wait_ge(sem(f"scattered{u}"), 16 * GT * (NG // SLOTS))
            pool.sem_inc(sem("scattered_all"), 1)
            wait_runs(3)
            node_rows(runs2, Dw[:, :].rearrange("p (t f) -> p t f", f=WL2), sem("nodes2"))
            dense = pool.value_load(verdict[0:1, 0:1], min_val=0, max_val=1)
            with pool.If(dense == 0):
                with pool.Fori(0, STEPS) as s:
                    pool.wait_ge(sem("y_stored"), s * 16 + 16)
                    settle(pool)
                    sweep(s + 3, table, src_i)
                    wait_runs(s + 4)
                    node_rows(runs, nodes(Db), sem("nodes3"))

        @block.scalar
        def _(act):
            def sweep(base, width=D, scale=False, keep_max=False):
                act_to = width
                with act.Fori(0, NG // SLOTS) as j:
                    for u in range(SLOTS):
                        i = j * SLOTS + u
                        gi = i + base
                        if scale:
                            act.wait_ge(gathered[u], (j + 1 + base // SLOTS) * (16 * GT))
                            for k in range(GT - 1, -1, -1):
                                act.activation(G[:, u, k, 0:D], G[:, u, k, 0:D], ACT.Copy,
                                               scale=weight_e[:, bass.ds((NG - 1 - i) * GT + k, 1)]
                                               ).then_inc(scaled, 1)
                        act.wait_ge(stored[u % 2], (gi - u % 2) * 8 + 16)
                        if keep_max:
                            act.activation(O[:, u % 2, :, D + HEADS:WL2].rearrange("p k h -> p k h"),
                                           C[:, bass.ds((NG - 1 - i) * (GT * HEADS), GT * HEADS)]
                                           .rearrange("p (k h) -> p k h", h=HEADS), ACT.Copy).then_inc(max_kept, 1)
                        for m in range(GT):
                            k = GT - 1 - m
                            act.wait_ge(summed, gi * GT + m + 1 + CREDIT_SUM)
                            act.activation(O[:, u % 2, k, 0:act_to], ps[m % 4][:, 0:act_to], ACT.Copy
                                           ).then_inc(evacuated, 1)

            def copy_pt(n, ready, done, to, before=0):
                for r in range(PTN):
                    act.wait_ge(ready, before + r + 1)
                    act.activation(to[:, r * T7 * P:(r + 1) * T7 * P], pt[r % 2][:, 0:T7 * P], ACT.Copy
                                   ).then_inc(done, 1)

            roots = [0]

            def root(v):
                roots[0] += 1
                act.wait_ge(sem("to_root"), roots[0])
                act.activation(v, v, ACT.Sqrt).then_inc(sem("rooted"), 1)

            root(stat_b[:, :])
            copy_pt(0, sem("hT_ps"), sem("hT"), B)
            sweep(0)
            root(dinv[:, :])
            copy_pt(0, sem("aggT_ps"), sem("aggT"), Dw)
            act.wait_ge(sem("w_tot"), 2)
            for n in range(14):
                act.wait_ge(sem("mix_ps"), n + 1)
                act.activation(E[:, n * 448:(n + 1) * 448], ps[n % 4][:, 0:448], ACT.Identity, bias=cols[:, 5:6]
                               ).then_inc(sem("mix_out"), 1)
            root(bn[:, 2:3])
            for n in range(2):
                act.wait_ge(sem("bn_ready"), n + 1)
                half = slice(n * NP // 2, (n + 1) * NP // 2)
                act.activation(E[:, half], E[:, half], ACT.Gelu, bias=cols[:, 3:4]).then_inc(sem("gelu"), 1)
            root(stat_b[:, :])
            copy_pt(0, sem("h1T_ps"), sem("h1T"), B)
            act.wait_ge(sem("x1_done"), 1)
            for n in range(NT):
                if n >= 2:
                    act.wait_ge(sem(f"rel_stored{n % 2}"), 16 * (n // 2))
                for k in range(0, 8, 2):
                    act.wait_ge(sem("rel_ps"), 8 * n + k + 1)
                    act.activation((C, E)[n % 2][:, k * 512:(k + 1) * 512], ps[k % 4][:, :], ACT.Copy
                                   ).then_inc(sem("rel_act"), 1)
            sweep(NG, scale=True)
            root(stat_b[:, :])
            copy_pt(0, sem("h2T_ps"), sem("h2T"), B)
            copy_pt(0, sem("gat_ps"), sem("gat_rows"), C)
            with act.Fori(0, NG // SLOTS) as j:
                for u in range(SLOTS):
                    i = j * SLOTS + u
                    act.wait_ge(gathered[u], (j + 1 + 2 * (NG // SLOTS)) * (16 * GT))
                    act.activation(E[:, bass.ds(i * (GT * HEADS), GT * HEADS)].rearrange("p (k h) -> p k h", h=HEADS),
                                   G[:, u, :, D:D + HEADS], ACT.Copy).then_inc(as_kept, 1)
            for r in range(3 * PTN):
                to = (A, Dw, X)[r // PTN]
                act.wait_ge(sem("heads_ps"), r + 1)
                act.activation(to[:, (r % PTN) * T7 * P:(r % PTN + 1) * T7 * P], pt[r % 2][:, 0:T7 * P], ACT.Copy
                               ).then_inc(sem("to_heads"), 1)
            act.wait_ge(sem("exponents"), 1)
            act.activation(A[:, :], A[:, :], ACT.Exp).then_inc(sem("edge_w"), 1)
            for r in range(2 * PTN):
                to = (B, C)[r // PTN][:, :].rearrange("p (c j h) -> p j h c", c=CH, h=HEADS)
                act.wait_ge(sem("edges_ps"), r + 1)
                for n in range(T7):
                    a = act.activation(to[:, (r % PTN) * T7 + n, :, :],
                                       pt[r % 2][:, n * P:(n + 1) * P].rearrange("p (h c) -> p h c", c=CH),
                                       ACT.Copy)
                a.then_inc(sem("from_heads"), 1)
            act.wait_ge(sem("from_heads"), 2 * PTN)
            sweep(2 * NG, width=D + HEADS, keep_max=True)
            act.wait_ge(sem("self_exponents"), 1)
            act.activation(self_w[:, :], self_w[:, :], ACT.Exp).then_inc(sem("self_w"), 1)
            root(stat_b[:, :])
            copy_pt(0, sem("h3T_ps"), sem("h3T"), B)
            for n in range(14):
                for c in range(4):
                    act.wait_ge(sem("ff1_ps"), 4 * n + c + 1)
                    if n >= 2:
                        act.wait_ge(sem("ff2_ps"), n - 1)
                    act.activation(E[:, (n % 2) * 1792 + c * 448:(n % 2) * 1792 + (c + 1) * 448], ps[c % 2][:, 0:448],
                                   ACT.Relu, bias=b1[:, c:c + 1]).then_inc(sem("ff1"), 1)
            root(stat_b[:, :])
            root(stat_b[:, :])
            act.wait_ge(sem("judged"), 1)
            dense = act.value_load(verdict[0:1, 0:1], min_val=0, max_val=1)
            with act.If(dense == 1):
                act.wait_ge(sem("y_ready"), 1)
                act.activation(halves(E)[:, :, 0:D], nodes(C), ACT.Copy, scale=SCALE).then_inc(sem("upper"), 1)
                with act.Fori(0, STEPS // 2) as s2:
                    for half in range(2):
                        with act.Fori(0, NT // ADJ_SLOTS) as a:
                            for u in range(ADJ_SLOTS):
                                n = s2 * (2 * NT) + a * ADJ_SLOTS + (half * NT + u)
                                act.wait_ge(sem("y_tiles"), n + 1 + ADJ_SLOTS)
                                act.activation(halves((A, E)[half])[:, bass.ds(a * ADJ_SLOTS + u, 1), 0:D],
                                               nodes(C)[:, bass.ds(a * ADJ_SLOTS + u, 1), :],
                                               ACT.Copy, scale=SCALE).then_inc(sem("upper"), 1)
            with act.Else():
                with act.Fori(0, STEPS) as s:
                    sweep((s + 3) * NG)

        @block.tensor
        def _(pe):
            def sweep(base, ready, width=D, hist=False):
                with pe.Fori(0, NG // SLOTS) as j:
                    for u in range(SLOTS):
                        i = j * SLOTS + u
                        gi = i + base
                        pe.wait_ge(selected, gi + 1 + CREDIT_SEL)
                        for m in range(GT):
                            k = GT - 1 - m
                            ready(j, u, i, m)
                            pe.wait_ge(evacuated, gi * GT + m + 1)
                            pe.matmul(ps[m % 4][:, 0:width], S[:, u % 2, k, :], G[:, u, k, 0:width],
                                      start=True, stop=False)
                            pe.wait_ge(evacuated, gi * GT + m + CREDIT_EV)
                            prev = O[0:1, u % 2, k + 1, 0:width] if m else O[0:1, 1 - u % 2, 0, 0:width]
                            pe.matmul(ps[m % 4][:, 0:width], carry_mask[0:1, u % 2, k, :], prev,
                                      start=False, stop=True).then_inc(summed, 1)
                        if hist:
                            pe.wait_ge(hist_ready, i + 1)
                            for k in range(GT):
                                mm = pe.matmul(pt[0][:, 0:NT], hot_lo[:, u % 2, k, :], hot_hi[:, u % 2, k, :],
                                               start=False, stop=False, skip_group_check=True)
                            mm.then_inc(hist_used, 1)

            def transposes(src, done, free, before=0):
                for r in range(PTN):
                    if r >= 2:
                        pe.wait_ge(free, before + r - 1)
                    for n in range(T7):
                        mm = pe.transpose(pt[r % 2][:, n * P:(n + 1) * P], src(r * T7 + n), ident[:, :])
                    mm.then_inc(done, 1)

            def tiles(v):
                return lambda n: v[:, n * P:(n + 1) * P]

            pe.sem_inc(summed, CREDIT_SUM)
            pe.wait_ge(sem("made"), 6)
            pe.wait_ge(sem("weights_in"), 16 * len(LOADS))
            pe.wait_ge(sem("filter"), 2)
            pe.matmul(ps[0][:, 0:D], cs[:, 0, :], cs_w[:, 0, :], start=True, stop=False)
            pe.matmul(ps[0][:, 0:D], cs[:, 1, :], cs_w[:, 1, :], start=False, stop=True).then_inc(sem("filter_ps"), 1)
            pe.wait_ge(sem("filter_c"), 1)
            pe.matmul(ps[1][:, 0:D], w_in[:, :], c_mat[:, :], start=True, stop=True).then_inc(sem("filter_ps"), 1)
            pe.matmul(ps[2][:, 0:1], c_mat[:, :], cols[:, 1:2], start=True, stop=True).then_inc(sem("filter_ps"), 1)
            pe.wait_ge(sem("ln0"), 1)
            transposes(tiles(A), sem("hT_ps"), sem("hT"))
            pe.wait_ge(sem("hT"), PTN)
            pe.wait_ge(sem("w_tot"), 2)
            pe.wait_ge(sem("hist_zero"), 1)
            pe.matmul(pt[0][:, 0:NT], hot_lo[:, 0, 0, :], hot_hi[:, 0, 0, :], start=True, stop=False,
                      skip_group_check=True).then_inc(sem("hist_started"), 1)

            def rows_in(base):
                def ready(j, u, i, m):
                    if m == 0:
                        pe.wait_ge(gathered[u], (j + 1 + base) * (16 * GT))
                return ready
            per = NG // SLOTS
            sweep(0, rows_in(0), hist=True)
            pe.wait_ge(sem("counts"), 1)
            pe.wait_ge(evacuated, NG * GT + CREDIT_EV)
            pe.matmul(ps[0][:, 0:NT], iota_f[:, :], cnt[:, :], start=True, stop=True)
            pe.matmul(ps[1][:, 0:NT], ones[:, :], cnt[:, :], start=True, stop=True).then_inc(sem("starts_ps"), 1)
            pe.wait_ge(sem("agg"), 1)
            transposes(tiles(C), sem("aggT_ps"), sem("aggT"))
            pe.wait_ge(sem("aggT"), PTN)
            for n in range(14):
                if n >= 4:
                    pe.wait_ge(sem("mix_out"), n - 3)
                c = slice(n * 448, (n + 1) * 448)
                pe.matmul(ps[n % 4][:, 0:448], w_tot[:, :], B[:, c], start=True, stop=False)
                pe.matmul(ps[n % 4][:, 0:448], wf[:, 1, :], Dw[:, c], start=False, stop=True
                          ).then_inc(sem("mix_ps"), 1)
            pe.wait_ge(sem("gelu"), 2)
            transposes(tiles(E), sem("x1_ps"), sem("x1"))
            pe.wait_ge(sem("ln1"), 1)
            transposes(tiles(A), sem("h1T_ps"), sem("h1T"))
            pe.wait_ge(sem("h1T"), PTN)
            pe.wait_ge(sem("rel_w"), 1)
            for n in range(NT):
                for k in range(8):
                    g = 8 * n + k
                    if g >= 4:
                        pe.wait_ge(sem("rel_dve" if k % 2 else "rel_act"), (g - 4) // 2 + 1)
                    pe.matmul(ps[k % 4][:, :], B[:, n * P:(n + 1) * P], Db[:, k * 512:(k + 1) * 512],
                              start=True, stop=True).then_inc(sem("rel_ps"), 1)
            pe.wait_ge(sem("rel_act"), 4 * NT)
            pe.wait_ge(sem("rel_dve"), 4 * NT)

            def scaled_in(j, u, i, m):
                pe.wait_ge(scaled, i * GT + m + 1)
            sweep(NG, scaled_in)
            pe.wait_ge(sem("ln2"), 1)
            transposes(tiles(A), sem("h2T_ps"), sem("h2T"))
            pe.wait_ge(sem("h2T"), PTN)
            for r in range(PTN):
                if r >= 2:
                    pe.wait_ge(sem("gat_rows"), r - 1)
                for n in range(T7):
                    mm = pe.matmul(pt[r % 2][:, n * P:(n + 1) * P], B[:, (r * T7 + n) * P:(r * T7 + n + 1) * P],
                                   w_gat[:, :], start=True, stop=True)
                mm.then_inc(sem("gat_ps"), 1)
            pe.wait_ge(sem("gat_rows"), PTN)

            pe.wait_ge(sem("worst"), 1)
            pe.transpose(ps[0][0:1, 0:P], end_col[:, 0:1], ident[:, :]).then_inc(sem("worst_ps"), 1)
            for k, v in enumerate((A, Dw, X)):
                pe.wait_ge(sem("permuted"), k + 1)
                for r in range(PTN):
                    g = k * PTN + r
                    if g >= 2:
                        pe.wait_ge(sem("to_heads"), g - 1)
                    for n in range(T7):
                        mm = pe.transpose(pt[g % 2][:, n * P:(n + 1) * P], tiles(v)(r * T7 + n), ident[:, :])
                    mm.then_inc(sem("heads_ps"), 1)
            pe.wait_ge(sem("to_heads"), 3 * PTN)
            chains = 0
            for n, back in enumerate((False, True, True, False, True)):
                pe.wait_ge(sem("ends"), n + 1)
                pe.transpose(ps[0][0:1, 0:P], end_col[:, 0:1], ident[:, :]).then_inc(sem("ends_ps"), 1)
                if back:
                    chains += 1
                    pe.wait_ge(sem("starts"), chains)
                    pe.matmul(ps[1][:, 0:1], chain_row[0:1, 5, :], ones[0:1, 0:1], start=True, stop=True
                              ).then_inc(sem("starts_c"), 1)
            pe.wait_ge(sem("edge_w"), 1)
            for k, v in enumerate((A, X)):
                for r in range(PTN):
                    g = k * PTN + r
                    if g >= 2:
                        pe.wait_ge(sem("from_heads"), g - 1)
                    for n in range(T7):
                        mm = pe.transpose(pt[g % 2][:, n * P:(n + 1) * P], v[:, (r * T7 + n) * P:(r * T7 + n + 1) * P],
                                          ident[:, :])
                    mm.then_inc(sem("edges_ps"), 1)
            pe.wait_ge(sem("from_heads"), 2 * PTN)
            sweep(2 * NG, lambda j, u, i, m: pe.wait_ge(sem("weighted"), i + 1) if m == 0 else None, width=D + HEADS)
            pe.wait_ge(sem("ln_a"), 1)
            transposes(tiles(A), sem("h3T_ps"), sem("h3T"))
            pe.wait_ge(sem("h3T"), PTN)
            for n in range(14 + 1):
                if n < 14:
                    for c in range(4):
                        g = 4 * n + c
                        if g >= 2:
                            pe.wait_ge(sem("ff1"), g - 1)
                        pe.matmul(ps[c % 2][:, 0:448], w1[:, c * P:(c + 1) * P], B[:, n * 448:(n + 1) * 448],
                                  start=True, stop=True).then_inc(sem("ff1_ps"), 1)
                if n >= 1:
                    pe.wait_ge(sem("ff1"), 4 * n)
                    if n >= 3:
                        pe.wait_ge(sem("ff2"), n - 2)
                    base = ((n - 1) % 2) * 1792
                    for c in range(4):
                        mm = pe.matmul(ps[2 + (n - 1) % 2][:, 0:448], w2[:, c, :],
                                       E[:, base + c * 448:base + (c + 1) * 448], start=(c == 0), stop=(c == 3))
                    mm.then_inc(sem("ff2_ps"), 1)
            pe.wait_ge(sem("ff2"), 14)
            transposes(tiles(Dw), sem("ffb_ps"), sem("ffb"))
            pe.wait_ge(sem("ffb"), PTN)
            dense = pe.value_load(verdict[0:1, 0:1], min_val=0, max_val=1)
            banks = [ps[0][:, :], ps[1][:, :], ps[2][:, :], ps[3][:, :],
                     pt[0][:, 0:512], pt[0][:, 512:1024], pt[1][:, 0:512]]
            with pe.If(dense == 1):
                with pe.Fori(0, STEPS // 2) as s2:
                    for half in range(2):
                        y = halves((E, A)[half])
                        pe.wait_ge(sem("lower"), s2 * (2 * NT) + (half + 1) * NT)
                        settle(pe)
                        with pe.Fori(0, NT // ADJ_SLOTS) as a:
                            for u in range(ADJ_SLOTS):
                                n = s2 * (2 * NT) + a * ADJ_SLOTS + (half * NT + u)
                                pe.wait_ge(sem(f"adj_in{u}"), s2 * (2 * 16 * NT // ADJ_SLOTS) + a * 16
                                           + (half * 16 * NT // ADJ_SLOTS + 16))
                                settle(pe)
                                pe.wait_ge(sem("y_tiles"), n + 1)
                                settle(pe)
                                for i in range(NT):
                                    mm = pe.matmul(banks[u][:, 0:2 * D], adj_ring[:, u, i * P:(i + 1) * P],
                                                   y[:, i, :], start=(i == 0), stop=(i == NT - 1))
                                mm.then_inc(sem("multiplied"), 1)
            with pe.Else():
                with pe.Fori(0, STEPS) as s:
                    sweep((s + 3) * NG, rows_in((s + 3) * per))

        @block.vector
        def _(dve):
            links = [0]

            def link(ins):
                links[0] += 1
                ins.then_inc(sem("dve_link"), 1)
                dve.wait_ge(sem("dve_link"), links[0])

            def sweep(base, hist=False, weights=False):
                with dve.Fori(0, NG // SLOTS) as j:
                    for u in range(SLOTS):
                        i = j * SLOTS + u
                        gi = i + base
                        t0 = (NG - 1 - i) * GT
                        if weights:
                            dve.wait_ge(reloaded[u], j * 16 + 16)
                            w = B[:, bass.ds(t0 * HEADS, GT * HEADS)].rearrange("p (k h) -> p k h", h=HEADS)
                            for k in range(GT):
                                g = G[:, u, k, 0:D].rearrange("p (h c) -> p h c", c=HC)
                                dve.tensor_tensor(g, g, bc(B[:, bass.ds((t0 + k) * HEADS, HEADS)], HC), MUL)
                            dve.tensor_copy(G[:, u, :, D:D + HEADS], w).then_inc(sem("weighted"), 1)
                        dve.wait_ge(dst_in[u % 2], (gi - u % 2) * 8 + 16)
                        dve.wait_ge(summed, gi * GT + (CREDIT_SUM - GT))
                        settle(dve)
                        for k in range(GT):
                            dve.scalar_tensor_tensor(S[:, u % 2, k, :], dst_b[:, u % 2, k * P:(k + 1) * P],
                                                     dst_f[:, bass.ds(t0 + k, 1)], tri[:, :], ALU.is_equal, MUL)
                        dve.tensor_tensor(carry_mask[0:1, u % 2, :, :],
                                          dst_b[0:1, u % 2, :].rearrange("p (k e) -> p k e", e=P),
                                          bc(dst_f[0:1, bass.ds(t0 + 1, GT)], P), ALU.is_equal
                                          ).then_inc(selected, 1)
                        if hist:
                            dve.wait_ge(hist_used, i + 1)
                            for k in range(GT):
                                dve.tensor_scalar(hot_lo[:, u % 2, k, :], iota_f[:, :],
                                                  E[:, bass.ds(t0 + k, 1)], None, ALU.is_equal)
                                a = dve.tensor_scalar(hot_hi[:, u % 2, k, :], iota_f[:, 0:NT],
                                                      E[:, bass.ds(t0 + k + ET, 1)], None, ALU.is_equal)
                            a.then_inc(hist_ready, 1)

            roots = [0]

            def inv_sqrt(v):
                roots[0] += 1
                dve.sem_inc(sem("to_root"), 1)
                dve.wait_ge(sem("rooted"), roots[0])
                link(dve.reciprocal(v, v))

            def layernorm(x, h, done=None, relu=True, gain=None, shift=None, tmp=None):
                xn, hn = nodes(x), nodes(h)
                link(dve.tensor_reduce(stat_a[:, :], xn, AX.X, ADD))
                link(dve.tensor_scalar(stat_a[:, :], stat_a[:, :], 1.0 / D, None, MUL))
                link(dve.tensor_tensor(hn, xn, bc(stat_a[:, :], D), SUB))
                link(dve.tensor_tensor(nodes(tmp), hn, hn, MUL))
                link(dve.tensor_reduce(stat_b[:, :], nodes(tmp), AX.X, ADD))
                link(dve.tensor_scalar(stat_b[:, :], stat_b[:, :], 1.0 / D, EPS, MUL, ADD))
                inv_sqrt(stat_b[:, :])
                a = dve.tensor_tensor(hn, hn, bc(stat_b[:, :], D), MUL)
                if relu:
                    link(a)
                    a = dve.tensor_scalar(h[:, 0:NP], h[:, 0:NP], 0.0, None, MAX)
                if gain is not None:
                    link(a)
                    link(dve.tensor_tensor(hn, hn, row_bc(rows[:, gain, :], NT), MUL))
                    a = dve.tensor_tensor(hn, hn, row_bc(rows[:, shift, :], NT), ADD)
                if done is None:
                    link(a)
                else:
                    a.then_inc(done, 1)
                    dve.wait_ge(done, 1)

            dve.memset(src_i[:, FULL:ET], 0)
            dve.memset(rel_i[:, FULL:ET], 0)
            dve.memset(weight_e[:, FULL:ET], 0.0)
            dve.memset(C[:, :], 0.0).then_inc(sem("padded"), 1)
            dve.memset(Ei[0:1, 0:EP - N_EDGES + P], NP).then_inc(sem("padded"), 1)
            dve.memset(Bi[:, FULL:ET], NP).then_inc(sem("padded"), 1)
            dve.memset(O[:, :, :, :], 0.0)
            dve.sem_inc(selected, CREDIT_SEL)
            dve.sem_inc(evacuated, CREDIT_EV)
            dve.sem_inc(as_kept, 4)
            dve.sem_inc(hist_used, 2)
            dve.memset(dst_f[:, ET:ET + 1], -1.0)
            dve.wait_ge(sem("edges_in"), 16 * len(EDGES))
            dve.wait_ge(sem("dst_padded"), 112)
            dve.tensor_copy(dst_f[:, 0:ET], Bi[:, 0:ET])
            dve.tensor_scalar(Bi[:, ET:2 * ET], Bi[:, 0:ET], 127, None, ALU.bitwise_and)
            link(dve.tensor_scalar(Bi[:, 2 * ET:3 * ET], Bi[:, 0:ET], 7, None, ALU.logical_shift_right))
            dve.tensor_copy(E[:, 0:2 * ET], Bi[:, ET:3 * ET])
            dve.scalar_tensor_tensor(rel_i[:, :], src_i[:, :], float(RELS), rel_i[:, :], MUL, ADD
                                     ).then_inc(sem("edge_numbers"), 1)
            dve.wait_ge(sem("made"), 6)
            link(dve.tensor_copy(iota_f[:, :], iota_i[:, :]))
            dve.wait_ge(sem("weights_in"), 16 * len(LOADS))
            link(dve.tensor_scalar(cs_w[:, 2, :], cs[:, 3, :], cw[:, 1:2], None, MUL))
            dve.scalar_tensor_tensor(cs_w[:, 0, :], cs[:, 2, :], cw[:, 0:1], cs_w[:, 2, :], MUL, SUB
                                     ).then_inc(sem("filter"), 1)
            dve.wait_ge(sem("filter"), 1)
            link(dve.tensor_scalar(cs_w[:, 2, :], cs[:, 2, :], cw[:, 1:2], None, MUL))
            dve.scalar_tensor_tensor(cs_w[:, 1, :], cs[:, 3, :], cw[:, 0:1], cs_w[:, 2, :], MUL, ADD
                                     ).then_inc(sem("filter"), 1)
            dve.wait_ge(sem("filter_ps"), 1)
            dve.tensor_copy(c_mat[:, :], ps[0][:, 0:D]).then_inc(sem("filter_c"), 1)
            dve.wait_ge(sem("filter_ps"), 3)
            dve.scalar_tensor_tensor(w_tot[:, :], ps[1][:, 0:D], cols[:, 4:5], wf[:, 0, :], MUL, ADD
                                     ).then_inc(sem("w_tot"), 1)
            dve.scalar_tensor_tensor(cols[:, 5:6], ps[2][:, 0:1], cols[:, 4:5], cols[:, 0:1], MUL, ADD
                                     ).then_inc(sem("w_tot"), 1)
            dve.wait_ge(sem("x_in"), 32)
            dve.wait_ge(sem("seeds_zero"), 32)
            for k in range(SLOTS):
                dve.wait_ge(kept[k], 16)
            for k in range(2):
                dve.wait_ge(stored[k], 16)
            layernorm(X, A, sem("ln0"), tmp=C)
            dve.wait_ge(sem("hT"), PTN)
            dve.wait_ge(sem("table0"), 16)
            dve.memset(A[:, :], 0.0).then_inc(sem("zeros"), 1)
            dve.memset(hot_lo[:, 0, 0, :], 0.0)
            dve.memset(hot_hi[:, 0, 0, :], 0.0).then_inc(sem("hist_zero"), 1)
            dve.wait_ge(sem("hist_started"), 1)
            sweep(0, hist=True)
            dve.wait_ge(hist_used, NG + 2)
            dve.tensor_scalar(iota_f[:, :], tri[:, :], -1.0, 1.0, MUL, ADD)
            dve.tensor_copy(cnt[:, :], pt[0][:, 0:NT]).then_inc(sem("counts"), 1)
            dve.wait_ge(sem("counts"), 1)
            link(dve.tensor_scalar(mask[:, :], cnt[:, :], 1.0, None, MIN))
            link(dve.tensor_scalar(rcnt[:, :], cnt[:, :], 1.0, None, MAX))
            link(dve.reciprocal(rcnt[:, :], rcnt[:, :]))
            link(dve.tensor_tensor(rcnt[:, :], rcnt[:, :], mask[:, :], MUL))
            link(dve.tensor_scalar(dinv[:, :], cnt[:, :], 1.0, None, ADD))
            inv_sqrt(dinv[:, :])
            dve.wait_ge(sem("starts_ps"), 1)
            link(dve.tensor_copy(stat_a[:, :], ps[1][:, 0:NT]))
            link(dve.tensor_tensor_scan(stat_b[:, :], ones[:, 0:NT], stat_a[:, :], 0.0, MUL, ADD))
            link(dve.tensor_tensor(stat_b[:, :], stat_b[:, :], stat_a[:, :], SUB))
            link(dve.tensor_tensor(row_f[:, :], stat_b[:, :], ps[0][:, 0:NT], ADD))
            dve.tensor_copy(row_i[:, :], row_f[:, :]).then_inc(sem("row_starts"), 1)
            link(dve.tensor_scalar(stat_a[:, :], mask[:, :], -2.0 * EP, 2.0 * EP, MUL, ADD))
            link(dve.tensor_tensor(stat_a[:, :], stat_a[:, :], row_f[:, :], ADD))
            link(dve.tensor_copy(seed_i[:, :], stat_a[:, :]))
            dve.wait_ge(sem("nodes0"), 16 * NT)
            dve.tensor_tensor(nodes(C), nodes(C), bc(rcnt[:, :], D), MUL).then_inc(sem("agg"), 1)
            for n in range(14):
                dve.wait_ge(sem("mix_out"), n + 1)
                last = dve.bn_stats(bn_st[:, n, :], E[:, n * 448:min((n + 1) * 448, N_NODES)])
            link(last)
            link(dve.bn_aggr(bn[:, 0:2], bn_st[:, :, :].rearrange("p a b -> p (a b)")))
            link(dve.tensor_scalar(bn[:, 2:3], bn[:, 1:2], EPS, None, ADD))
            inv_sqrt(bn[:, 2:3])
            link(dve.tensor_scalar(bn[:, 2:3], bn[:, 2:3], cols[:, 2:3], None, MUL))
            for n in range(2):
                half = slice(n * NP // 2, (n + 1) * NP // 2)
                dve.tensor_scalar(E[:, half], E[:, half], bn[:, 0:1], bn[:, 2:3], SUB, MUL).then_inc(sem("bn_ready"), 1)
            for r in range(PTN):
                c = slice(r * T7 * P, (r + 1) * T7 * P)
                dve.wait_ge(sem("x1_ps"), r + 1)
                dve.tensor_tensor(X[:, c], X[:, c], pt[r % 2][:, 0:T7 * P], ADD).then_inc(sem("x1"), 1)
            dve.wait_ge(sem("x1"), PTN)
            dve.sem_inc(sem("x1_done"), 1)
            dve.wait_ge(sem("adj_zero"), 16 * 13)
            layernorm(X, A, sem("ln1"), tmp=C)
            w_rel = Db[:, 0:RELS * D].rearrange("p (r o) -> p r o", o=D)
            tmp = C[:, 0:RELS * D].rearrange("p (r o) -> p r o", o=D)
            dve.wait_ge(sem("bases_in"), 32)
            for b in range(BASES):
                link(dve.tensor_tensor(w_rel if b == 0 else tmp, bc(comp[:, :, b], D), row_bc(w_base[:, b, :], RELS), MUL))
                if b:
                    link(dve.tensor_tensor(w_rel, w_rel, tmp, ADD))
            dve.sem_inc(sem("rel_w"), 1)
            for n in range(NT):
                if n >= 2:
                    dve.wait_ge(sem(f"rel_stored{n % 2}"), 16 * (n // 2))
                for k in range(1, 8, 2):
                    dve.wait_ge(sem("rel_ps"), 8 * n + k + 1)
                    dve.tensor_copy((C, E)[n % 2][:, k * 512:(k + 1) * 512], ps[k % 4][:, :]).then_inc(sem("rel_dve"), 1)
            sweep(NG)
            dve.wait_ge(sem("nodes1"), 16 * NT)
            link(dve.tensor_tensor(nodes(C), nodes(C), bc(mask[:, :], D), MUL))
            link(dve.tensor_tensor(nodes(C), nodes(C), row_bc(rows[:, BIAS1, :], NT), ADD))
            link(dve.scalar_tensor_tensor(X[:, :], C[:, :], 0.0, X[:, :], MAX, ADD))
            layernorm(X, A, sem("ln2"), tmp=C)
            dve.wait_ge(sem("gat_rows"), PTN)
            for k, att in ((0, ATT_D), (1, ATT_S)):
                link(dve.tensor_tensor(nodes(Db), nodes(C), row_bc(rows[:, att, :], NT), MUL))
                link(dve.tensor_reduce(E[:, 0:NT * HEADS], Db.rearrange("p (t c) -> p t c", c=HC), AX.X, ADD))
                dve.tensor_copy(scores[:, :, k * HEADS:(k + 1) * HEADS],
                                E[:, 0:NT * HEADS].rearrange("p (t h) -> p t h", h=HEADS)
                                ).then_inc(sem("scores_ready"), 1)
                dve.wait_ge(sem("scores_ready"), k + 1)
            link(dve.tensor_copy(weight_e[:, :], src_i[:, :]))
            dve.memset(window_w[:, 2 * P:3 * P], 1.0)
            dve.memset(window_w[:, 0:P], 1.0 + EARLIER)
            link(dve.tensor_tensor(window_w[:, P:2 * P], tri[:, :], ident[:, :], SUB))
            link(dve.tensor_scalar(window_w[:, P:2 * P], window_w[:, P:2 * P], float(EARLIER), 1.0, MUL, ADD))
            with dve.Fori(0, NG // SLOTS) as j:
                for u in range(SLOTS):
                    q = j * SLOTS + u
                    dve.wait_ge(sem(f"window_in{u % 2}"), j * 64 + (32 + 32 * (u // 2)))
                    for k in range(GT):
                        here = slice(k * P, (k + 3) * P)
                        dve.scalar_tensor_tensor(same[:, k % 2, :], win[:, 0, u % 2, here],
                                                 dst_f[:, bass.ds(q * GT + k, 1)], window_w, ALU.is_equal, MUL
                                                 ).then_inc(sem("same_dst"), 1)
                        dve.wait_ge(sem("same_dst"), q * GT + k + 1)
                        a = dve.scalar_tensor_tensor(same[:, 2, :], win[:, 1, u % 2, here],
                                                     weight_e[:, bass.ds(q * GT + k, 1)], same[:, k % 2, :],
                                                     ALU.is_equal, MUL, accum_out=codes[:, bass.ds(q * GT + k, 1)])
                    a.then_inc(sem("searched"), 1)
            dve.wait_ge(sem("searched"), NG)
            dve.wait_ge(sem("spilled"), 32)
            e0, e1, e2, e3 = (A[:, k * ET:(k + 1) * ET].bitcast(I32) for k in range(4))
            f0, f1 = A[:, 4 * ET:5 * ET], A[:, 5 * ET:6 * ET]
            SHL, SHR, AND, OR = ALU.logical_shift_left, ALU.logical_shift_right, ALU.bitwise_and, ALU.bitwise_or
            link(dve.tensor_copy(e0, codes))
            link(dve.tensor_scalar(e1, e0, 10, None, SHR))
            link(dve.tensor_scalar(e0, e0, EARLIER - 1, None, AND))
            link(dve.tensor_copy(f0, e0))
            link(dve.tensor_scalar(f1, dst_f[:, 0:ET], float(NP), None, ALU.is_lt))
            link(dve.tensor_tensor(f0, f0, f1, MUL))
            dve.tensor_scalar(f1, f0, float(MOST), None, MIN)
            link(dve.tensor_reduce(end_col[:, 0:1], f0, AX.X, MAX))
            link(dve.tensor_copy(weight_e[:, 0:ET // 4].bitcast(F8), f1, saturate=False))
            link(dve.tensor_reduce(end_col[:, 1:2], cnt[:, :], AX.X, MAX))
            dve.scalar_tensor_tensor(end_col[:, 0:1], end_col[:, 1:2], float(MOST) / MOST_DEGREE, end_col[:, 0:1],
                                     MUL, MAX).then_inc(sem("worst"), 1)
            link(dve.tensor_copy(e2, dst_f[:, 0:ET]))
            link(dve.tensor_scalar(e3, e2, 7, 20, SHR, SHL))
            link(dve.tensor_scalar(e2, e2, P - 1, None, AND))
            link(dve.tensor_tensor(e3, e3, e2, OR))
            link(dve.tensor_scalar(e2, src_i[:, :], P - 1, 13, AND, SHL))
            link(dve.tensor_tensor(e3, e3, e2, OR))
            link(dve.tensor_scalar(e2, src_i[:, :], 7, 7, SHR, SHL))
            link(dve.tensor_tensor(e3, e3, e2, OR))
            link(dve.tensor_copy(f0, e1))
            link(dve.tensor_scalar(f0, f0, 1.0, None, MIN))
            link(dve.tensor_copy(e1, f0))
            link(dve.tensor_scalar(e1, e1, 26, None, SHL))
            link(dve.tensor_tensor(rel_i[:, :], e3, e1, OR))
            dve.wait_ge(sem("worst_ps"), 1)
            link(dve.tensor_reduce(in_col[0:1, 0:1], ps[0][0:1, 0:P], AX.X, MAX))
            link(dve.tensor_scalar(in_col[0:1, 0:1], in_col[0:1, 0:1], float(MOST), None, ALU.is_le))
            link(dve.tensor_copy(verdict[:, :], in_col[0:1, 0:1]))
            dve.sem_inc(sem("judged"), 1)
            dve.wait_ge(as_kept, NG + 4)
            dve.wait_ge(sem("spilled"), 32)
            by_place = lambda v: v[:, 0:NP].rearrange("p (j h c) -> p j h c", h=HEADS, c=CH)
            by_tile = lambda v: v[:, 0:NP].rearrange("p (c j h) -> p j h c", c=CH, h=HEADS)
            for k, (to, of) in enumerate(((A, E), (Dw, B), (X, C))):
                if k == 1:
                    dve.wait_ge(sem("seeds_in"), 32)
                dve.tensor_copy(by_place(to), by_tile(of)).then_inc(sem("permuted"), 1)
            dve.wait_ge(sem("to_heads"), 3 * PTN)
            dve.wait_ge(sem("dst_heads"), 16 * 2 * HEADS)
            link(dve.tensor_tensor(E[:, :], Bi, Ci, ALU.not_equal))
            link(dve.tensor_scalar(B[:, :], E[:, :], BIG, -BIG, MUL, ADD))
            link(dve.tensor_tensor(X[:, :], X[:, :], B[:, :], ADD))
            link(dve.tensor_tensor(B[:, :], A[:, :], X[:, :], MAX))
            link(dve.tensor_scalar(C[:, :], E[:, :], -BIG, None, MUL))
            link(dve.tensor_scalar(X[:, :], E[:, :], -1.0, 1.0, MUL, ADD))

            hc = lambda v: v.rearrange("p (h c) -> p h c", c=CH)
            state, through, through_01, result, starts = (chain_row[0:1, k, :] for k in (0, 1, 2, 3, 5))
            events = [0, 0]

            def flags(first_edges):
                link(dve.tensor_reduce(end_col[:, 0:1], first_edges[:, 0:NP], AX.X, MAX))
                dve.sem_inc(sem("ends"), 1)
                events[0] += 1
                dve.wait_ge(sem("ends_ps"), events[0])
                link(dve.tensor_scalar(through_01, ps[0][0:1, 0:P], -1.0, 1.0, MUL, ADD))

            def chain(scan, data, rev, largest):
                zero = -BIG if largest else 0.0
                if largest:
                    link(dve.tensor_scalar(through, through_01, BIG, -BIG, MUL, ADD))
                else:
                    link(dve.tensor_copy(through, through_01))
                at = slice(CH - 1, CH) if rev else slice(0, 1)
                link(dve.memset(hc(through)[:, :, at], zero))
                link(scan(zero))
                at = slice(0, 1) if rev else slice(CE - 1, CE)
                link(dve.tensor_copy(end_col[:, 0:1], data[:, at]))
                dve.sem_inc(sem("ends"), 1)
                events[0] += 1
                events[1] += 1
                dve.wait_ge(sem("ends_ps"), events[0])
                link(dve.tensor_copy(state, ps[0][0:1, 0:P]))
                way = (lambda v: v[:, ::-1]) if rev else (lambda v: v)
                link(dve.tensor_tensor_scan(way(result), way(through), way(state), zero,
                                            ADD if largest else MUL, MAX if largest else ADD))
                link(dve.memset(starts, zero))
                if rev:
                    link(dve.tensor_copy(hc(starts)[:, :, 0:CH - 1], hc(result)[:, :, 1:CH]))
                else:
                    link(dve.tensor_copy(hc(starts)[:, :, 1:CH], hc(result)[:, :, 0:CH - 1]))
                dve.sem_inc(sem("starts"), 1)
                dve.wait_ge(sem("starts_c"), events[1])
                link(dve.tensor_copy(in_col[:, :], ps[1][:, 0:1]))
                link(scan(in_col[:, 0:1]))

            flags(E)
            chain(lambda z: dve.tensor_tensor_scan(E[:, :], X[:, :], Db, z, MUL, ADD), E, False, False)
            chain(lambda z: dve.tensor_tensor_scan(Db, C[:, :], B[:, :], z, ADD, MAX), Db, False, True)
            dve.sem_inc(sem("fwd_done"), 1)
            dve.wait_ge(sem("dst_heads2"), 16 * 2 * HEADS)
            link(dve.tensor_tensor(B[:, :], Bi, Ci, ALU.not_equal))
            link(dve.tensor_scalar(C[:, :], B[:, :], -BIG, None, MUL))
            flags(B)
            chain(lambda z: dve.tensor_tensor_scan(X[:, ::-1], C[:, ::-1], Db[:, ::-1], z, ADD, MAX), X, True, True)
            link(dve.tensor_tensor(A[:, :], A[:, :], E[:, :], ADD))
            link(dve.scalar_tensor_tensor(A[:, :], A[:, :], SLOPE, A[:, :], MUL, MAX))
            link(dve.tensor_tensor(B[:, :], X[:, :], E[:, :], ADD))
            link(dve.scalar_tensor_tensor(B[:, :], B[:, :], SLOPE, B[:, :], MUL, MAX))
            dve.tensor_tensor(A[:, :], A[:, :], B[:, :], SUB).then_inc(sem("exponents"), 1)
            dve.wait_ge(sem("from_heads"), 2 * PTN)
            sweep(2 * NG, weights=True)
            dve.wait_ge(sem("nodes2"), 16 * NT)
            dve.wait_ge(sem("h2_back"), 16)
            dve.wait_ge(sem("gat_back"), 16)
            dve.wait_ge(sem("x_back"), 16)
            agg = Dw[:, :].rearrange("p (t f) -> p t f", f=WL2)
            K = NT * HEADS
            e0, e1, e2, e3 = (E[:, k * K:(k + 1) * K] for k in range(4))
            th = lambda v: v.rearrange("p (t h) -> p t h", h=HEADS)
            a_d, a_s = scores[:, :, 0:HEADS], scores[:, :, HEADS:]
            link(dve.tensor_scalar(stat_a[:, :], mask[:, :], BIG, -BIG, MUL, ADD))
            link(dve.tensor_tensor(th(e0), agg[:, :, D + HEADS:], bc(mask[:, :], HEADS), MUL))
            link(dve.tensor_tensor(th(e0), th(e0), bc(stat_a[:, :], HEADS), ADD))
            link(dve.tensor_tensor(th(e0), th(e0), a_s, MAX))
            link(dve.tensor_tensor(th(e1), th(e0), a_d, ADD))
            link(dve.scalar_tensor_tensor(e1, e1, SLOPE, e1, MUL, MAX))
            link(dve.tensor_tensor(th(e2), a_s, a_d, ADD))
            link(dve.scalar_tensor_tensor(e2, e2, SLOPE, e2, MUL, MAX))
            dve.tensor_tensor(self_w[:, :], e2, e1, SUB).then_inc(sem("self_exponents"), 1)
            dve.wait_ge(sem("self_w"), 1)
            link(dve.tensor_tensor(th(e3), agg[:, :, D:D + HEADS], bc(mask[:, :], HEADS), MUL))
            link(dve.tensor_tensor(e3, e3, self_w[:, :], ADD))
            link(dve.reciprocal(e3, e3))
            heads = lambda v: v[:, 0:NP].rearrange("p (k c) -> p k c", c=HC)
            link(dve.tensor_tensor(heads(B), heads(C), bc(self_w[:, :], HC), MUL))
            link(dve.tensor_tensor(nodes(C), agg[:, :, 0:D], bc(mask[:, :], D), MUL))
            link(dve.tensor_tensor(B[:, :], B[:, :], C[:, :], ADD))
            link(dve.tensor_tensor(heads(B), heads(B), bc(e3, HC), MUL))
            link(dve.tensor_tensor(nodes(B), nodes(B), row_bc(rows[:, B_GAT, :], NT), ADD))
            link(dve.tensor_tensor(B[:, :], B[:, :], A[:, :], ADD))
            layernorm(B, A, sem("ln_a"), relu=False, gain=G1, shift=BB1, tmp=C)
            for n in range(14):
                dve.wait_ge(sem("ff2_ps"), n + 1)
                dve.tensor_copy(Dw[:, n * 448:(n + 1) * 448], ps[2 + n % 2][:, 0:448]).then_inc(sem("ff2"), 1)
            for r in range(PTN):
                c = slice(r * T7 * P, (r + 1) * T7 * P)
                dve.wait_ge(sem("ffb_ps"), r + 1)
                dve.tensor_tensor(C[:, c], A[:, c], pt[r % 2][:, 0:T7 * P], ADD).then_inc(sem("ffb"), 1)
            dve.wait_ge(sem("ffb"), PTN)
            link(dve.tensor_tensor(nodes(C), nodes(C), row_bc(rows[:, B2, :], NT), ADD))
            layernorm(C, B, relu=False, gain=G2, shift=BB2, tmp=E)
            link(dve.tensor_tensor(X[:, :], X[:, :], B[:, :], ADD))
            layernorm(X, A, tmp=C)
            link(dve.tensor_scalar(stat_a[:, :], dinv[:, :], TELEPORT, None, MUL))
            link(dve.tensor_tensor(nodes(B), nodes(A), bc(stat_a[:, :], D), MUL))
            link(dve.tensor_tensor(sc_a[:, :], dinv[:, :], dinv[:, :], MUL))
            link(dve.tensor_scalar(sc_a[:, :], sc_a[:, :], 1.0 - TELEPORT, None, MUL))
            link(dve.tensor_tensor(sc_b[:, :], sc_a[:, :], mask[:, :], MUL))
            dve.tensor_tensor(nodes(C), nodes(A), bc(dinv[:, :], D), MUL).then_inc(sem("y_ready"), 1)
            dve.wait_ge(sem("y_ready"), 1)
            dense = dve.value_load(verdict[0:1, 0:1], min_val=0, max_val=1)
            with dve.If(dense == 1):
                link(dve.tensor_scalar(sc_b[:, :], sc_a[:, :], 1.0 / SCALE, None, MUL))
                dve.wait_ge(sem("upper"), 1)
                link(dve.scalar_tensor_tensor(halves(E)[:, :, D:2 * D], nodes(C), SCALE, halves(E)[:, :, 0:D], MUL, SUB))
                dve.sem_inc(sem("lower"), NT)
                dve.sem_inc(sem("y_tiles"), ADJ_SLOTS)
                banks = [ps[0][:, :], ps[1][:, :], ps[2][:, :], ps[3][:, :],
                         pt[0][:, 0:512], pt[0][:, 512:1024], pt[1][:, 0:512]]
                part_done = sem("part_done")
                with dve.Fori(0, STEPS // 2) as s2:
                    for half in range(2):
                        with dve.Fori(0, NT // ADJ_SLOTS) as a:
                            for u in range(ADJ_SLOTS):
                                n = s2 * (2 * NT) + a * ADJ_SLOTS + (half * NT + u)
                                tile = a * ADJ_SLOTS + u
                                yt = C[:, bass.ds(tile * P, P)]
                                w0, w1 = O[:, u % 2, 0, 0:D], O[:, u % 2, 1, 0:D]
                                dve.scalar_tensor_tensor(w0, yt, sc_a[:, bass.ds(tile, 1)], B[:, bass.ds(tile * P, P)],
                                                         MUL, ADD).then_inc(part_done, 1)
                                dve.wait_ge(part_done, n * 2 + 1)
                                dve.wait_ge(sem("multiplied"), n + 1)
                                dve.scalar_tensor_tensor(w1, banks[u][:, 0:D], sc_b[:, bass.ds(tile, 1)], w0, MUL, ADD
                                                         ).then_inc(part_done, 1)
                                dve.wait_ge(part_done, n * 2 + 2)
                                dve.scalar_tensor_tensor(yt, banks[u][:, D:2 * D], sc_b[:, bass.ds(tile, 1)], w1,
                                                         MUL, ADD).then_inc(sem("y_tiles"), 1)
                                dve.wait_ge(sem("upper"), n + 2)
                                new = halves((A, E)[half])
                                dve.scalar_tensor_tensor(new[:, bass.ds(tile, 1), D:2 * D],
                                                         nodes(C)[:, bass.ds(tile, 1), :], SCALE,
                                                         new[:, bass.ds(tile, 1), 0:D], MUL, SUB
                                                         ).then_inc(sem("lower"), 1)
                dve.wait_ge(sem("lower"), NT * (STEPS + 1))
            with dve.Else():
                with dve.Fori(0, STEPS) as s:
                    sweep((s + 3) * NG)
                    step = sem("step_link")
                    dve.tensor_tensor(nodes(E), nodes(C), bc(sc_a[:, :], D), MUL).then_inc(step, 1)
                    dve.wait_ge(step, s * 3 + 1)
                    dve.tensor_tensor(E[:, :], E[:, :], B[:, :], ADD).then_inc(step, 1)
                    dve.wait_ge(sem("nodes3"), s * (16 * NT) + 16 * NT)
                    dve.tensor_tensor(nodes(Db), nodes(Db), bc(sc_b[:, :], D), MUL).then_inc(step, 1)
                    dve.wait_ge(step, s * 3 + 3)
                    dve.wait_ge(sem("y_stored"), s * 16 + 16)
                    dve.tensor_tensor(C[:, :], E[:, :], Db, ADD).then_inc(sem("y_ready"), 1)
                    dve.wait_ge(sem("y_ready"), s + 2)
            link(dve.reciprocal(dinv[:, :], dinv[:, :]))
            link(dve.tensor_tensor(nodes(C), nodes(C), bc(dinv[:, :], D), MUL))
            dve.scalar_tensor_tensor(X[:, :], C[:, :], 0.0, X[:, :], MAX, ADD).then_inc(sem("out_ready"), 1)


def kernel(**inputs):
    import concourse.bacc as bacc
    from concourse.bass_utils import run_bass_kernel_spmd as run

    full = FULL * P
    k, n = np.arange(FREQ)[:, None], np.arange(D)[None, :]
    share = np.where((k == 0) | (k == D // 2), 1.0, 2.0) / D
    turn = 2 * np.pi * ((k * n) % D) / D
    cos, sin = np.cos(turn), np.where((k * n) % (D // 2) == 0, 0.0, np.sin(turn))
    fourier = np.stack([cos, sin, share * cos, share * sin], axis=1).astype(np.float32)

    def cols(a):
        return np.ascontiguousarray(np.asarray(a).reshape(-1)[:full].reshape(FULL, P).T)

    flat = {name: np.asarray(v) for name, v in inputs.items()}
    arrays = {
        "x": flat["x"], "src": flat["src"], "dst": flat["dst"], "etype": flat["edge_type_32"],
        "norm": flat["edge_weight1"].reshape(-1), "src_cols": cols(flat["src"]), "dst_cols": cols(flat["dst"]),
        "etype_cols": cols(flat["edge_type_32"]), "norm_cols": cols(flat["edge_weight1"]), "fourier": fourier,
        "w_fuse_t": np.ascontiguousarray(flat["L0_gnn_W_fuse"].T), "alpha": flat["L0_gnn_alpha"].reshape(1),
        "w_in": flat["L0_gnn_W_in"], "b_fuse": flat["L0_gnn_b_fuse"], "b_in": flat["L0_gnn_b_in"],
        "complex_weight": flat["L0_gnn_complex_weight"], "gamma": flat["L0_gnn_gamma"], "beta": flat["L0_gnn_beta"],
        "weight": flat["L1_gnn_weight"], "w_comp": flat["L1_gnn_w_comp"], "bias_param": flat["L1_gnn_bias_param"],
        "w_gat": flat["L2_gnn_W_gat"], "att_src": flat["L2_gnn_att_src"], "att_dst": flat["L2_gnn_att_dst"],
        "b_gat": flat["L2_gnn_b_gat"], "w1": flat["L2_gnn_W1"], "b1": np.ascontiguousarray(flat["L2_gnn_b1"].reshape(4, P).T),
        "w2": flat["L2_gnn_W2"], "b2": flat["L2_gnn_b2"], "ln1_g": flat["L2_gnn_ln1_g"], "ln1_b": flat["L2_gnn_ln1_b"],
        "ln2_g": flat["L2_gnn_ln2_g"], "ln2_b": flat["L2_gnn_ln2_b"],
    }
    nc = bacc.Bacc("TRN2", target_bir_lowering=False, num_devices=1)
    aps = {name: nc.dram_tensor(f"in_{name}", a.shape, mybir.dt.from_np(a.dtype), kind="ExternalInput").ap()
           for name, a in arrays.items()}
    out = nc.dram_tensor("out_x", (N_NODES, D), F32, kind="ExternalOutput").ap()
    build(nc, aps, out)
    r = run(nc, [{f"in_{name}": a for name, a in arrays.items()}], core_ids=[0])
    return r.results[0]["out_x"]
```

```python
from contextlib import ExitStack

import numpy as np

import concourse.bass as bass
from concourse import mybir

P = 128
N_NODES, N_EDGES, D = 6250, 100000, 128
NT = (N_NODES + P - 1) // P
NP = NT * P
GT = 4
SLOTS = 4
NG = 196
ET = NG * GT
EP = ET * P
GE_ROWS = GT * P
FULL = N_EDGES // P
REST = N_EDGES - FULL * P
FRONT = 2 * GE_ROWS
RELS, BASES, HEADS, HC, FF = 32, 8, 8, 16, 512
CH = 16
CE = EP // CH
CT = ET // CH
SEED_PARTS = 28
FREQ = D // 2 + 1
BIG = 1.0e30
EPS = 1e-5
STEPS, TELEPORT, SLOPE = 10, 0.1, 0.2
WL2 = D + 2 * HEADS

ADJ_SLOTS = 7
ADJ_PITCH = 1 << 13
MOST = 16
MOST_DEGREE = P
EARLIER = 1024
WIN = (GT + 2) * P
KEY_DST = 2048
KEY_SRC = 8192
SCALE = 1024.0

F32, I32, BF16 = mybir.dt.float32, mybir.dt.int32, mybir.dt.bfloat16
F16, F8, U8 = mybir.dt.float16, mybir.dt.float8e4, mybir.dt.uint8
ALU, ACT, AX = mybir.AluOpType, mybir.ActivationFunctionType, mybir.AxisListType
ADD, SUB, MUL, MAX, MIN = ALU.add, ALU.subtract, ALU.mult, ALU.max, ALU.min


def build(nc, t, out):
    ctx = ExitStack()
    with ctx:
        def sb(name, shape, dt=F32):
            return ctx.enter_context(nc.sbuf_tensor(name, shape, dt))

        def dram(name, shape, dt=F32):
            return nc.dram_tensor(name, shape, dt).ap()

        names = {}

        def sem(name):
            if name not in names:
                names[name] = ctx.enter_context(nc.semaphore(name))
            return names[name]

        dst_pad = dram("dst_pad", (FRONT + EP + P,), I32)
        key_pad = dram("key_pad", (P + EP + P,))
        adj = dram("adj", (NP, ADJ_PITCH), U8)
        table = dram("table", (NP, D))
        rel_table = dram("rel_table", (NP * RELS, D))
        gat_table = dram("gat_table", (NP, D + HEADS))
        x_spill = dram("x_spill", (NP, D))
        runs = dram("runs", (EP, D))
        runs2 = dram("runs2", (EP, WL2))
        edge_rows = dram("edge_rows", (EP, D))
        seeds = dram("seeds", (EP, 2 * HEADS))

        X, A, B, C, E = (sb(n, [P, NP]) for n in ("X", "A", "B", "C", "E"))
        arena = sb("arena", [P, NT * WL2 + SLOTS * GT * (D + HEADS) + 4 * GT * P + 2 * GE_ROWS])
        at = [0]

        def part(n):
            at[0] += n
            return arena[:, at[0] - n:at[0]]

        Dw = part(NT * WL2)
        Db = Dw[:, 0:NP]

        def nodes(v):
            return v[:, 0:NP].rearrange("p (t f) -> p t f", f=D)

        def halves(v):
            return v[:, 0:NP].bitcast(F16).rearrange("p (t f) -> p t f", f=2 * D)

        def bc(v, n):
            return v.unsqueeze(2).to_broadcast([v.shape[0], v.shape[1], n])

        def row_bc(v, n):
            return v.unsqueeze(1).to_broadcast([v.shape[0], n, v.shape[1]])

        src_i = sb("src_i", [P, ET], I32)
        rel_i = sb("rel_i", [P, ET], I32)
        dst_f = sb("dst_f", [P, ET + 1])
        weight_e = sb("weight_e", [P, ET])
        G = part(SLOTS * GT * (D + HEADS)).rearrange("p (s k f) -> p s k f", s=SLOTS, k=GT)
        idx = sb("idx", [P, 2, 2 * GT], I32)
        O = sb("O", [P, 2, GT, WL2])
        carry_rows = sb("carry_rows", [1, GT, D + HEADS])
        S = part(2 * GT * P).rearrange("p (s k e) -> p s k e", s=2, k=GT)
        carry_mask = part(2 * GT * P)[0:1, :].rearrange("p (s k e) -> p s k e", s=2, k=GT)
        dst_b = part(2 * GE_ROWS).bitcast(I32).rearrange("p (s e) -> p s e", s=2)
        adj_ring = arena[:, 0:ADJ_SLOTS * NP // 4].bitcast(F8).rearrange("p (s f) -> p s f", s=ADJ_SLOTS)
        vals = sb("vals", [P, 2, 2 * GT], U8)
        verdict = sb("verdict", [1, 1], I32)
        win = Dw[:, 0:2 * WIN].rearrange("p (s e) -> p s e", s=2)
        codes = Dw[:, 2 * WIN:2 * WIN + ET]
        window_w = Dw[:, 2 * WIN + ET:2 * WIN + ET + 3 * P]
        same = Dw[:, 2 * WIN + ET + 3 * P:2 * WIN + ET + (3 + 3 * GT) * P].rearrange("p (k e) -> p k e", k=GT)
        KEY_ROWS = 125
        KE = N_EDGES // KEY_ROWS
        key_parts = [Dw[0:KEY_ROWS, 2048 + k * KE:2048 + (k + 1) * KE].bitcast(I32) for k in range(2)]
        no_key = Dw[0:1, 4096:4096 + EP - N_EDGES + P]
        ident, tri = (sb(n, [P, P]) for n in ("ident", "tri"))
        ones, iota_f = Dw[:, NP:NP + P], Dw[:, NP + P:NP + 2 * P]
        iota_h = Dw[:, NP + 2 * P:NP + 2 * P + P // 2].bitcast(BF16)
        iota_i = A[:, 0:P].bitcast(I32)
        hot_lo = C[:, 0:GT * P].bitcast(BF16).rearrange("p (a k n) -> p a k n", a=2, k=GT)
        hot_hi = C[:, 1024:1024 + GT * NT].bitcast(BF16).rearrange("p (a k n) -> p a k n", a=2, k=GT)
        (cnt, mask, rcnt, dinv, row_f, stat_a, stat_b, sc_a, sc_b) = (
            sb(n, [P, NT]) for n in ("cnt", "mask", "rcnt", "dinv", "row_f", "stat_a", "stat_b", "sc_a", "sc_b"))
        row_i, seed_i = sb("row_i", [P, NT], I32), sb("seed_i", [P, NT], I32)
        scores = sb("scores", [P, NT, 2 * HEADS])
        wf = sb("wf", [P, 2, D])
        w_tot = sb("w_tot", [P, D])
        w_in, c_mat = Dw[:, 0:D], Dw[:, D:2 * D]
        cs = Dw[0:FREQ, 2 * D:6 * D].rearrange("p (a f) -> p a f", f=D)
        cs_w = Dw[0:FREQ, 6 * D:9 * D].rearrange("p (a f) -> p a f", f=D)
        cols = sb("cols", [P, 8])
        cw = sb("cw", [FREQ, 2])
        w_base = Dw[:, RELS * D:(RELS + BASES) * D].rearrange("p (b o) -> p b o", o=D)
        comp = Dw[:, (RELS + BASES) * D:(RELS + BASES) * D + RELS * BASES].rearrange("p (r b) -> p r b", b=BASES)
        rows = sb("rows", [P, 9, D])
        w_gat, w1, w2, b1 = sb("w_gat", [P, D]), sb("w1", [P, FF]), sb("w2", [P, 4, D]), sb("b1", [P, 4])
        bn_st, bn = sb("bn_st", [P, 14, 6]), sb("bn", [P, 4])
        end_col, in_col = sb("end_col", [P, 2]), sb("in_col", [P, 1])
        self_w = S.rearrange("p s k e -> p (s k e)")[:, 0:NT * HEADS]
        next_dst = bn[:, 0:1].bitcast(I32)
        chain_row = S[0:1, :, :, :].rearrange("p a k e -> p (a k) e")
        (BIAS1, ATT_S, ATT_D, B_GAT, G1, BB1, G2, BB2, B2) = range(9)

        ps = [ctx.enter_context(nc.psum_tensor(f"ps{k}", [P, 512], F32)) for k in range(4)]
        pt = [ctx.enter_context(nc.psum_tensor(f"pt{k}", [P, 1024], F32)) for k in range(2)]
        T7 = 7
        PTN = NT // T7

        gathered = [sem(f"gathered{k}") for k in range(SLOTS)]
        reloaded = [sem(f"reloaded{k}") for k in range(SLOTS)]
        dst_in = [sem(f"dst_in{k}") for k in range(2)]
        stored = [sem(f"stored{k}") for k in range(2)]
        kept = [sem(f"kept{k}") for k in range(SLOTS)]
        idx_set, summed, evacuated, selected = sem("idx_set"), sem("summed"), sem("evacuated"), sem("selected")
        tile_summed, carried = sem("tile_summed"), sem("carried")
        scaled, hist_ready, hist_used, as_kept, max_kept = (
            sem(n) for n in ("scaled", "hist_ready", "hist_used", "as_kept", "max_kept"))
        node_part = [sem(f"node_part{r}") for r in range(PTN)]
        CREDIT_SUM, CREDIT_EV = SLOTS * GT, 4

        def settle(eng):
            eng.sem_inc(sem("settled"), 1)

        table_v = table.rearrange("(t p) f -> p t f", p=P)
        spill_v = x_spill.rearrange("(t p) f -> p t f", p=P)
        gat_v = gat_table.rearrange("(t p) f -> p t f", p=P)
        out_full = (N_NODES // P) * P

        LOADS = []
        for k, n in enumerate(("b_fuse", "b_in", "gamma", "beta")):
            LOADS.append((cols[:, k:k + 1], t[n].rearrange("(p a) -> p a", a=1)))
        LOADS.append((cols[:, 6:7], t["b2"].rearrange("(p a) -> p a", a=1)))
        LOADS.append((cols[:, 4:5], t["alpha"].rearrange("(a b) -> a b", a=1).to_broadcast([P, 1])))
        LOADS.append((wf[:, :, :], t["w_fuse_t"].rearrange("(a p) o -> p a o", p=P)))
        LOADS.append((w_in[:, :], t["w_in"]))
        LOADS.append((cs[:, :, :], t["fourier"]))
        LOADS.append((cw[:, :], t["complex_weight"]))
        for k, n in enumerate(("bias_param", "att_src", "att_dst", "b_gat", "ln1_g", "ln1_b", "ln2_g", "ln2_b", "b2")):
            v = t[n] if len(t[n].shape) == 1 else t[n].rearrange("h c -> (h c)")
            LOADS.append((rows[:, k, :], v.rearrange("(a f) -> a f", a=1).to_broadcast([P, D])))
        LOADS.append((w_gat[:, :], t["w_gat"]))
        LOADS.append((w1[:, :], t["w1"]))
        LOADS.append((w2[:, :, :], t["w2"].rearrange("(c p) o -> p c o", p=P)))
        LOADS.append((b1[:, :], t["b1"]))
        EDGES = []
        for v, n in ((src_i, "src"), (rel_i, "etype"), (weight_e, "norm"), (B[:, :].bitcast(I32), "dst")):
            EDGES.append((v[:, 0:FULL], t[n + "_cols"]))
            EDGES.append((v[0:REST, FULL:FULL + 1], t[n][FULL * P:N_EDGES].rearrange("(p a) -> p a", a=1)))
        Bi, Ci, Ei = (v[:, :].bitcast(I32) for v in (B, C, E))

        block = ctx.enter_context(nc.Block())

        @block.sync
        def _(sp):
            def group_of(i):
                return NG - 1 - i

            def load_dst(slot, q):
                sp.dma_start(dst_b[:, slot, :],
                             dst_pad[bass.ds(q * GE_ROWS + FRONT, GE_ROWS)].rearrange("(a e) -> a e", a=1)
                             .to_broadcast([P, GE_ROWS])).then_inc(dst_in[slot], 16)

            def sweep(base, base_pairs, to, width, reload=False):
                def load_rows(slot, q):
                    sp.dma_start(G[:, slot, :, 0:D],
                                 edge_rows[bass.ds(q * GE_ROWS, GE_ROWS), :].rearrange("(t p) f -> p t f", p=P)
                                 ).then_inc(reloaded[slot], 16)
                to_v = to.rearrange("(t p) f -> p t f", p=P)

                def groups(j, last=False):
                    for u in range(SLOTS):
                        i = j * SLOTS + u
                        if not last or u < SLOTS - 1:
                            sp.wait_ge(selected, (i + base) * GT + 2 * GT)
                            settle(sp)
                            load_dst((u + 1) % 2, group_of(i) - 3)
                        sp.wait_ge(evacuated, (i + base) * GT + GT + CREDIT_EV)
                        if width == WL2:
                            settle(sp)
                            sp.wait_ge(max_kept, i + 1)
                        settle(sp)
                        sp.dma_start(to_v[:, bass.ds(group_of(i) * GT, GT), :],
                                     O[:, u % 2, :, 0:width]).then_inc(stored[u % 2], 16)
                        if reload and not last:
                            load_rows(u, group_of(i) - SLOTS)

                if reload:
                    for u in range(SLOTS):
                        load_rows(u, group_of(u))
                sp.wait_ge(selected, base * GT + GT)
                settle(sp)
                load_dst(0, group_of(0) - 2)
                with sp.Fori(0, NG // SLOTS - 1) as j:
                    groups(j)
                groups(NG // SLOTS - 1, last=True)

            sp.wait_ge(sem("padded"), 5)
            for dst_ap, src_ap in EDGES:
                sp.dma_start(dst_ap, src_ap).then_inc(sem("edges_in"), 16)
            full = N_NODES // P
            sp.dma_start(nodes(X)[:, 0:full, :], t["x"][0:full * P, :].rearrange("(t p) f -> p t f", p=P)
                         ).then_inc(sem("x_in"), 16)
            sp.dma_start(nodes(X)[0:N_NODES - full * P, full, :], t["x"][full * P:N_NODES, :]).then_inc(sem("x_in"), 16)
            tail = EP - N_EDGES
            for v, n in zip(key_parts, ("src", "dst")):
                sp.dma_start(v, t[n].rearrange("(p e) -> p e", p=KEY_ROWS)).then_inc(sem("key_parts_in"), 16)
            sp.dma_start(dst_pad[FRONT:FRONT + N_EDGES], t["dst"]).then_inc(sem("dst_padded"), 16)
            sp.dma_start(dst_pad[0:FRONT - tail], t["dst"][EP - FRONT:N_EDGES]).then_inc(sem("dst_padded"), 16)
            pad = Ei[0:1, 0:tail + P]
            sp.dma_start(dst_pad[FRONT - tail:FRONT], pad[:, 0:tail]).then_inc(sem("dst_padded"), 16)
            sp.dma_start(dst_pad[FRONT + N_EDGES:FRONT + EP + P], pad).then_inc(sem("dst_padded"), 16)
            sp.dma_start(key_pad[0:P], no_key[0:1, 0:P]).then_inc(sem("dst_padded"), 16)
            sp.dma_start(key_pad[P + N_EDGES:P + EP + P], no_key).then_inc(sem("dst_padded"), 16)
            for dst_ap, src_ap in LOADS:
                sp.dma_start(dst_ap, src_ap).then_inc(sem("weights_in"), 16)
            sz = 2 * HEADS * EP // P
            seeds_z = seeds.rearrange("(p a) f -> p (a f)", p=P)
            for k in range(2):
                sp.dma_start(seeds_z[:, k * (sz // 2):(k + 1) * (sz // 2)], C[:, 0:sz // 2]
                             ).then_inc(sem("seeds_zero"), 16)
            for k in range(2):
                sp.dma_start(runs[k * P:(k + 1) * P, :], C[:, 0:D]).then_inc(stored[k], 16)
            for k in range(SLOTS):
                sp.dma_start(edge_rows[k * P:(k + 1) * P, :], C[:, 0:D]).then_inc(kept[k], 16)
            sp.wait_ge(sem("dst_padded"), 96)
            load_dst(0, NG - 1)
            load_dst(1, NG - 2)
            sp.wait_ge(sem("keys"), 1)
            sp.dma_start(key_pad[P:P + N_EDGES].rearrange("(p e) -> p e", p=KEY_ROWS), key_parts[0].bitcast(F32)
                         ).then_inc(sem("keys_stored"), 16)
            sp.wait_ge(sem("normalized"), NT)
            sp.dma_start(table_v, nodes(A)).then_inc(sem("table0"), 16)
            sp.wait_ge(sem("w_tot"), 2)
            sp.wait_ge(sem("keys_stored"), 16)
            sp.dma_start(w_base, t["weight"].rearrange("b i o -> i b o")).then_inc(sem("bases_in"), 16)
            sp.dma_start(comp.rearrange("p r b -> p (r b)"),
                         t["w_comp"].rearrange("(a r) b -> a (r b)", a=1).to_broadcast([P, RELS * BASES])
                         ).then_inc(sem("bases_in"), 16)
            sweep(0, 0, runs, D)
            rel_v = rel_table.rearrange("(t p r) o -> t p (r o)", p=P, r=RELS)
            for n in range(NT):
                sp.wait_ge(sem("rel_act"), 4 * (n + 1))
                sp.wait_ge(sem("rel_dve"), 4 * (n + 1))
                sp.dma_start(rel_v[n], (C, E)[n % 2][:, 0:RELS * D]).then_inc(sem(f"rel_stored{n % 2}"), 16)
            sweep(NG, 0, runs, D)
            sp.wait_ge(sem("normalized"), 3 * NT)
            sp.dma_start(table_v, nodes(A)).then_inc(sem("spilled"), 16)
            sp.dma_start(spill_v, nodes(X)).then_inc(sem("spilled"), 16)
            sp.wait_ge(sem("gat_rows"), PTN)
            sp.dma_start(gat_v[:, :, 0:D], nodes(C)).then_inc(sem("gat_stored"), 16)
            sp.wait_ge(sem("scores_ready"), 2)
            sp.dma_start(gat_v[:, :, D:D + HEADS], scores[:, :, HEADS:]).then_inc(sem("gat_stored"), 16)
            rows_v = edge_rows.rearrange("(t p) f -> p t f", p=P)

            def load_window(slot, q):
                sp.dma_start(win[:, slot, :], key_pad[bass.ds(q * GE_ROWS, WIN)]
                             .rearrange("(a e) -> a e", a=1).to_broadcast([P, WIN])
                             ).then_inc(sem(f"window_in{slot}"), 16)

            def keep_groups(j, last=False):
                for u in range(SLOTS):
                    i = j * SLOTS + u
                    sp.wait_ge(gathered[u], (j + 1 + 2 * (NG // SLOTS)) * (16 * GT))
                    if not last:
                        settle(sp)
                    sp.dma_start(rows_v[:, bass.ds(i * GT, GT), :], G[:, u, :, 0:D]).then_inc(kept[u], 16)
                    if not last or u < SLOTS - 2:
                        sp.wait_ge(sem("searched"), i + 1)
                        if not last:
                            settle(sp)
                        load_window(u % 2, i + 2)

            sp.wait_ge(sem("scores_ready"), 2)
            for k in range(2):
                load_window(k, k)
            early = 4
            with sp.Fori(0, early) as j:
                keep_groups(j)
            sp.wait_ge(sem("seeded"), 16 * NT)
            sp.wait_ge(sem("spilled"), 32)
            sp.wait_ge(sem("gat_stored"), 32)
            seeds_v = seeds.rearrange("(t p) f -> p t f", p=P)
            W = ET // SEED_PARTS
            with sp.Fori(early, early + SEED_PARTS) as j:
                keep_groups(j)
                with nc.allow_non_contiguous_dma(reason="32-byte rows"):
                    for k, v in enumerate((B, C)):
                        sp.dma_start(v[:, bass.ds((j - early) * (W * HEADS), W * HEADS)]
                                     .rearrange("p (t h) -> p t h", h=HEADS),
                                     seeds_v[:, bass.ds((j - early) * W, W), k * HEADS:(k + 1) * HEADS]
                                     ).then_inc(sem("seeds_in"), 16)
            with sp.Fori(early + SEED_PARTS, NG // SLOTS - 1) as j:
                keep_groups(j)
            keep_groups(NG // SLOTS - 1, last=True)
            for k in range(SLOTS):
                sp.wait_ge(kept[k], 16 * (NG // SLOTS) + 16)
            def load_head_major(v, shift, name):
                for h in range(HEADS):
                    sp.dma_start(v[h * CH:(h + 1) * CH, :],
                                 dst_pad[FRONT + shift:FRONT + shift + EP].rearrange("(c e) -> c e", c=CH)
                                 ).then_inc(sem(name), 16)
            sp.wait_ge(sem("permuted"), 3)
            load_head_major(Bi, 0, "dst_heads")
            load_head_major(Ci, -1, "dst_heads")
            sp.wait_ge(sem("x_free"), 1)
            load_head_major(X[:, :].bitcast(I32), 0, "dst_heads2")
            with nc.allow_non_contiguous_dma(reason="a number for each chunk"):
                for h in range(HEADS):
                    sp.dma_start(next_dst[h * CH:(h + 1) * CH, :],
                                 dst_pad[FRONT + 1:FRONT + 1 + EP].rearrange("(c e) -> c e", c=CH)[:, CE - 1:CE]
                                 ).then_inc(sem("dst_heads2"), 16)
            sp.wait_ge(sem("from_heads"), 2 * PTN)
            sp.dma_start(nodes(A), table_v).then_inc(sem("h2_back"), 16)
            sp.dma_start(nodes(X), spill_v).then_inc(sem("x_back"), 16)
            sweep(2 * NG, 0, runs2, WL2, reload=True)
            sp.dma_start(nodes(C), gat_v[:, :, 0:D]).then_inc(sem("gat_back"), 16)
            sp.wait_ge(sem("judged"), 1)
            dense = sp.value_load(verdict[0:1, 0:1], min_val=0, max_val=1)
            adj_r = adj.rearrange("(j p) b -> p j b", p=P)
            ring_u8 = arena[:, 0:ADJ_SLOTS * NP // 4].bitcast(U8).rearrange("p (s f) -> p s f", s=ADJ_SLOTS)
            for k in range(2):
                sp.wait_ge(dst_in[k], 16 * (NG // 2) * 3 + 16)
                sp.wait_ge(stored[k], 16 * (NG // 2) * 3 + 16)
            with sp.If(dense == 1):
                def load_adj(u, j):
                    sp.dma_start(ring_u8[:, u:u + 1, :], adj_r[:, bass.ds(j, 1), 0:NP]).then_inc(sem(f"adj_in{u}"), 16)
                sp.wait_ge(sem("scattered_all"), 1)
                sp.wait_ge(sem("ffb"), PTN)
                for u in range(ADJ_SLOTS):
                    load_adj(u, u)
                with sp.Fori(0, STEPS) as s:
                    with sp.Fori(0, NT // ADJ_SLOTS - 1) as a:
                        for u in range(ADJ_SLOTS):
                            sp.wait_ge(sem("multiplied"), s * NT + a * ADJ_SLOTS + u + 1)
                            settle(sp)
                            load_adj(u, a * ADJ_SLOTS + (u + ADJ_SLOTS))
                    for u in range(ADJ_SLOTS):
                        sp.wait_ge(sem("multiplied"), s * NT + (NT - ADJ_SLOTS + u + 1))
                        settle(sp)
                        load_adj(u, u)
                for u in range(ADJ_SLOTS):
                    sp.wait_ge(sem(f"adj_in{u}"), 16 * (STEPS * NT // ADJ_SLOTS + 1))
            with sp.Else():
                with sp.Fori(0, STEPS) as s:
                    sp.wait_ge(sem("y_ready"), s + 1)
                    sp.dma_start(table_v, nodes(C)).then_inc(sem("y_stored"), 16)
                    sweep((s + 3) * NG, 0, runs, D)
                for k in range(2):
                    sp.wait_ge(stored[k], 16 * (NG // 2) * (3 + STEPS) + 16)
                    sp.wait_ge(dst_in[k], 16 * (NG // 2) * (3 + STEPS) + 16)
                sp.wait_ge(sem("y_stored"), 16 * STEPS)
            sp.wait_ge(sem("out_ready"), 1)
            sp.dma_start(out[0:full * P, :].rearrange("(t p) f -> p t f", p=P), nodes(X)[:, 0:full, :]
                         ).then_inc(sem("out_stored"), 16)
            sp.dma_start(out[full * P:N_NODES, :], nodes(X)[0:N_NODES - full * P, full, :]
                         ).then_inc(sem("out_stored"), 16)
            sp.wait_ge(sem("out_stored"), 32)

        @block.gpsimd
        def _(pool):
            pool.memset(nodes(X)[:, NT - 1, :], 0.0).then_inc(sem("padded"), 1)
            pool.memset(ident[:, :], 0.0).then_inc(sem("made"), 1)
            pool.memset(tri[:, :], 1.0).then_inc(sem("made"), 1)
            pool.memset(ones[:, :], 1.0).then_inc(sem("made"), 1)
            pool.iota(iota_i[:, :], pattern=[[1, P]], base=0, channel_multiplier=0).then_inc(sem("made"), 1)
            pool.wait_ge(sem("made"), 4)
            pool.affine_select(out=ident[:, :], in_=ident[:, :], compare_op=ALU.not_equal, fill=1.0, base=0,
                               pattern=[[-1, P]], channel_multiplier=1).then_inc(sem("made"), 1)
            pool.affine_select(out=tri[:, :], in_=tri[:, :], compare_op=ALU.is_ge, fill=0.0, base=0,
                               pattern=[[-1, P]], channel_multiplier=1).then_inc(sem("made"), 1)

            def sweep(p, rows_ap, indices, keep=False):
                w = rows_ap.shape[1]
                pairs = NG // 2

                def copy_pair(j, h):
                    i = j * SLOTS + 2 * h
                    q = i if keep else NG - 2 - i
                    pool.tensor_copy(idx[:, h, :], indices[:, bass.ds(q * GT, 2 * GT)]).then_inc(idx_set, 1)

                def groups(j, first=False, last=False):
                    for u in range(SLOTS):
                        i = j * SLOTS + u
                        if keep:
                            pool.wait_ge(kept[u], j * 16 + 16)
                            settle(pool)
                            pool.wait_ge(as_kept, i + 1)
                        else:
                            pool.wait_ge(summed, (p * NG + i) * GT + GT)
                        settle(pool)
                        h = u // 2
                        if u % 2 == 0:
                            pool.wait_ge(idx_set, j * 2 + p * pairs + (h + 1))
                            settle(pool)
                        at = (u % 2 if keep else 1 - u % 2) * GT
                        for k in range(GT):
                            pool.indirect_dma_start(
                                out=G[:, u, k, 0:w], out_offset=None, in_=rows_ap,
                                in_offset=bass.IndirectOffsetOnAxis(ap=idx[:, h, at + k:at + k + 1], axis=0)
                            ).then_inc(gathered[u], 16)
                        if u == 0:
                            if not first:
                                for v in (2, 3):
                                    pool.wait_ge(gathered[v], (p * (NG // SLOTS) + j) * (16 * GT))
                                settle(pool)
                            copy_pair(j, 1)
                        if u == 2 and not last:
                            for v in (0, 1):
                                pool.wait_ge(gathered[v], (p * (NG // SLOTS) + j + 1) * (16 * GT))
                            settle(pool)
                            copy_pair(j + 1, 0)

                copy_pair(0, 0)
                groups(0, first=isinstance(p, int) and p == 0)
                with pool.Fori(1, NG // SLOTS - 1) as j:
                    groups(j)
                groups(NG // SLOTS - 1, last=True)

            def node_rows(rows_ap, to_v, done=None):
                for n in range(NT):
                    pool.indirect_dma_start(
                        out=to_v[:, n, :], out_offset=None, in_=rows_ap,
                        in_offset=bass.IndirectOffsetOnAxis(ap=row_i[:, n:n + 1], axis=0)
                    ).then_inc(done or node_part[n // T7], 16)

            def wait_runs(passes):
                for k in range(2):
                    pool.wait_ge(stored[k], passes * (16 * (NG // 2)) + 16)
                    settle(pool)

            pool.wait_ge(sem("edge_numbers"), 1)
            pool.wait_ge(sem("table0"), 16)
            sweep(0, table, src_i)
            wait_runs(1)
            pool.wait_ge(sem("row_starts"), 1)
            node_rows(runs, nodes(C))
            for k in range(2):
                pool.wait_ge(sem(f"rel_stored{k}"), 16 * ((NT + 1 - k) // 2))
            sweep(1, rel_table, rel_i)
            wait_runs(2)
            node_rows(runs, nodes(C))
            pool.wait_ge(sem("seeds_zero"), 32)
            pool.wait_ge(sem("scores_ready"), 2)
            for n in range(NT):
                pool.indirect_dma_start(
                    out=seeds, out_offset=bass.IndirectOffsetOnAxis(ap=seed_i[:, n:n + 1], axis=0),
                    in_=scores[:, n, :], in_offset=None, bounds_check=EP - 1, oob_is_err=False
                ).then_inc(sem("seeded"), 16)
            pool.wait_ge(sem("gat_stored"), 32)
            pool.wait_ge(summed, 2 * NG * GT + CREDIT_SUM)
            sweep(2, gat_table, src_i, keep=True)
            pool.wait_ge(sem("judged"), 1)
            pool.wait_ge(sem("adj_zero"), 16 * NT)
            cells = adj.rearrange("r (b a) -> (r b) a", a=1)
            counts = weight_e[:, 0:ET // 4].bitcast(U8)

            def copy_cells(j, h):
                q = j * SLOTS + 2 * h
                pool.tensor_copy(idx[:, h, :], rel_i[:, bass.ds(q * GT, 2 * GT)]).then_inc(sem("cells_set"), 1)
                pool.tensor_copy(vals[:, h, :], counts[:, bass.ds(q * GT, 2 * GT)]).then_inc(sem("cells_set"), 1)

            def scatter_groups(j, first=False, last=False):
                for u in range(SLOTS):
                    h = u // 2
                    if u % 2 == 0:
                        pool.wait_ge(sem("cells_set"), j * 4 + (2 * h + 2))
                        settle(pool)
                    for k in range(u % 2 * GT, u % 2 * GT + GT):
                        pool.indirect_dma_start(
                            out=cells, out_offset=bass.IndirectOffsetOnAxis(ap=idx[:, h, k:k + 1], axis=0),
                            in_=vals[:, h, k:k + 1], in_offset=None, bounds_check=NP * ADJ_PITCH - 1,
                            oob_is_err=False).then_inc(sem(f"scattered{u}"), 16)
                    if u == 0:
                        if not first:
                            for v in (2, 3):
                                pool.wait_ge(sem(f"scattered{v}"), j * (16 * GT))
                            settle(pool)
                        copy_cells(j, 1)
                    if u == 2 and not last:
                        for v in (0, 1):
                            pool.wait_ge(sem(f"scattered{v}"), j * (16 * GT) + 16 * GT)
                        settle(pool)
                        copy_cells(j + 1, 0)

            for u in range(SLOTS):
                pool.wait_ge(gathered[u], 3 * (NG // SLOTS) * 16 * GT)
            few = pool.value_load(verdict[0:1, 0:1], min_val=0, max_val=1)
            with pool.If(few == 1):
                copy_cells(0, 0)
                scatter_groups(0, first=True)
                with pool.Fori(1, NG // SLOTS - 1) as j:
                    scatter_groups(j)
                scatter_groups(NG // SLOTS - 1, last=True)
                for u in range(SLOTS):
                    pool.wait_ge(sem(f"scattered{u}"), 16 * GT * (NG // SLOTS))
                pool.sem_inc(sem("scattered_all"), 1)
            wait_runs(3)
            node_rows(runs2, Dw[:, :].rearrange("p (t f) -> p t f", f=WL2))
            dense = pool.value_load(verdict[0:1, 0:1], min_val=0, max_val=1)
            with pool.If(dense == 0):
                with pool.Fori(0, STEPS) as s:
                    pool.wait_ge(sem("y_stored"), s * 16 + 16)
                    settle(pool)
                    sweep(s + 3, table, src_i)
                    wait_runs(s + 4)
                    node_rows(runs, nodes(Db), sem("nodes3"))

        @block.scalar
        def _(act):
            adj_v = adj.rearrange("(j p) b -> p j b", p=P)

            def sweep(base, width=D, scale=False, keep_max=False, zero_adj=False):
                def scale_rows(j, u, m):
                    k = GT - 1 - m
                    if m == 0:
                        act.wait_ge(gathered[u], (j + 1 + base // SLOTS) * (16 * GT))
                    act.activation(G[:, u, k, 0:D], G[:, u, k, 0:D], ACT.Copy,
                                   scale=weight_e[:, bass.ds((NG - 1 - (j * SLOTS + u)) * GT + k, 1)]
                                   ).then_inc(scaled, 1)

                def copy_weights(j, u):
                    act.activation(G[:, u, :, D:D + HEADS],
                                   B[:, bass.ds((NG - 1 - (j * SLOTS + u)) * (GT * HEADS), GT * HEADS)]
                                   .rearrange("p (k h) -> p k h", h=HEADS), ACT.Copy).then_inc(sem("beside"), 1)

                def groups(j, last=False):
                    if zero_adj:
                        act.dma_start(adj_v[:, bass.ds(j, 1), 0:NP],
                                      A[:, 0:NP // 4].bitcast(U8).rearrange("p (j b) -> p j b", j=1)
                                      ).then_inc(sem("adj_zero"), 16)
                    for u in range(SLOTS):
                        i = j * SLOTS + u
                        gi = i + base
                        act.wait_ge(stored[u % 2], (gi - u % 2) * 8 + 16)
                        if keep_max:
                            act.activation(O[:, u % 2, :, D + HEADS:WL2].rearrange("p k h -> p k h"),
                                           C[:, bass.ds((NG - 1 - i) * (GT * HEADS), GT * HEADS)]
                                           .rearrange("p (k h) -> p k h", h=HEADS), ACT.Copy).then_inc(max_kept, 1)
                        for m in range(GT):
                            act.wait_ge(summed, gi * GT + m + 1 + CREDIT_SUM)
                            act.activation(O[:, u % 2, GT - 1 - m, 0:width], ps[m][:, 0:width], ACT.Copy
                                           ).then_inc(evacuated, 1)
                            if keep_max and m == 0 and u < SLOTS - 1:
                                copy_weights(j, u + 1)
                            elif keep_max and m == 0 and not last:
                                copy_weights(j + 1, 0)
                            if scale and u < SLOTS - 1:
                                scale_rows(j, u + 1, m)
                            elif scale and not last:
                                scale_rows(j + 1, 0, m)

                if scale:
                    for m in range(GT):
                        scale_rows(0, 0, m)
                if keep_max:
                    copy_weights(0, 0)
                with act.Fori(0, NG // SLOTS - 1) as j:
                    groups(j)
                groups(NG // SLOTS - 1, last=True)

            def copy_pt(n, ready, done, to, before=0):
                for r in range(PTN):
                    act.wait_ge(ready, before + r + 1)
                    act.activation(to[:, r * T7 * P:(r + 1) * T7 * P], pt[r % 2][:, 0:T7 * P], ACT.Copy
                                   ).then_inc(done, 1)

            roots = [0]

            def root(v):
                roots[0] += 1
                act.wait_ge(sem("to_root"), roots[0])
                act.activation(v, v, ACT.Sqrt).then_inc(sem("rooted"), 1)

            norms = [0]

            def normalize(x, h, relu=True):
                root(stat_b[:, :])
                norms[0] += 1
                act.wait_ge(sem("norm_stats"), norms[0])
                for n in range(NT):
                    act.activation(nodes(h)[:, n, :], nodes(x)[:, n, :], ACT.Relu if relu else ACT.Identity,
                                   bias=stat_a[:, n:n + 1], scale=stat_b[:, n:n + 1]
                                   ).then_inc(sem("normalized"), 1)

            normalize(X, A)
            copy_pt(0, sem("hT_ps"), sem("hT"), B)
            act.wait_ge(sem("zeros"), 1)
            sweep(0, zero_adj=True)
            root(dinv[:, :])
            copy_pt(0, sem("aggT_ps"), sem("aggT"), Dw)
            act.wait_ge(sem("w_tot"), 2)
            for n in range(14):
                act.wait_ge(sem("mix_ps"), n + 1)
                act.activation(E[:, n * 448:(n + 1) * 448], ps[n % 4][:, 0:448], ACT.Identity, bias=cols[:, 5:6]
                               ).then_inc(sem("mix_out"), 1)
            root(bn[:, 2:3])
            for n in range(2):
                act.wait_ge(sem("bn_ready"), n + 1)
                half = slice(n * NP // 2, (n + 1) * NP // 2)
                act.activation(E[:, half], E[:, half], ACT.Gelu, bias=cols[:, 3:4]).then_inc(sem("gelu"), 1)
            normalize(X, Dw)
            copy_pt(0, sem("h1T_ps"), sem("h1T"), B)
            act.wait_ge(sem("x1_done"), 1)
            for n in range(NT):
                if n >= 2:
                    act.wait_ge(sem(f"rel_stored{n % 2}"), 16 * (n // 2))
                for k in range(0, 8, 2):
                    act.wait_ge(sem("rel_ps"), 8 * n + k + 1)
                    act.activation((C, E)[n % 2][:, k * 512:(k + 1) * 512], ps[k % 4][:, :], ACT.Copy
                                   ).then_inc(sem("rel_act"), 1)
            sweep(NG, scale=True)
            normalize(X, A)
            copy_pt(0, sem("h2T_ps"), sem("h2T"), B)
            copy_pt(0, sem("gat_ps"), sem("gat_rows"), C)
            with act.Fori(0, NG // SLOTS) as j:
                for u in range(SLOTS):
                    i = j * SLOTS + u
                    act.wait_ge(gathered[u], (j + 1 + 2 * (NG // SLOTS)) * (16 * GT))
                    act.activation(E[:, bass.ds(i * (GT * HEADS), GT * HEADS)].rearrange("p (k h) -> p k h", h=HEADS),
                                   G[:, u, :, D:D + HEADS], ACT.Copy).then_inc(as_kept, 1)
            for r in range(3 * PTN):
                to = (A, Dw, X)[r // PTN]
                act.wait_ge(sem("heads_ps"), r + 1)
                act.activation(to[:, (r % PTN) * T7 * P:(r % PTN + 1) * T7 * P], pt[r % 2][:, 0:T7 * P], ACT.Copy
                               ).then_inc(sem("to_heads"), 1)
            for r in range(2 * PTN):
                if r == PTN:
                    act.wait_ge(sem("exponents"), 1)
                    act.activation(A[:, :], A[:, :], ACT.Exp).then_inc(sem("edge_w"), 1)
                to = (C, B)[r // PTN][:, :].rearrange("p (c j h) -> p j h c", c=CH, h=HEADS)
                act.wait_ge(sem("edges_ps"), r + 1)
                for n in range(T7):
                    a = act.activation(to[:, (r % PTN) * T7 + n, :, :],
                                       pt[r % 2][:, n * P:(n + 1) * P].rearrange("p (h c) -> p h c", c=CH),
                                       ACT.Copy)
                a.then_inc(sem("from_heads"), 1)
            act.wait_ge(sem("from_heads"), 2 * PTN)
            sweep(2 * NG, width=D + HEADS, keep_max=True)
            for r in range(PTN):
                c = slice(r * T7 * HEADS, (r + 1) * T7 * HEADS)
                act.wait_ge(sem("self_exponents"), r + 1)
                act.activation(self_w[:, c], self_w[:, c], ACT.Exp).then_inc(sem("self_w"), 1)
            normalize(B, A, relu=False)
            copy_pt(0, sem("h3T_ps"), sem("h3T"), B)
            for n in range(14):
                for c in range(4):
                    act.wait_ge(sem("ff1_ps"), 4 * n + c + 1)
                    if n >= 2:
                        act.wait_ge(sem("ff2_ps"), n - 1)
                    act.activation(E[:, (n % 2) * 1792 + c * 448:(n % 2) * 1792 + (c + 1) * 448], ps[c % 2][:, 0:448],
                                   ACT.Relu, bias=b1[:, c:c + 1]).then_inc(sem("ff1"), 1)
            normalize(C, B, relu=False)
            normalize(X, A)
            act.wait_ge(sem("judged"), 1)
            dense = act.value_load(verdict[0:1, 0:1], min_val=0, max_val=1)
            with act.If(dense == 1):
                act.wait_ge(sem("y_ready"), 1)
                act.activation(halves(E)[:, :, 0:D], nodes(C), ACT.Copy, scale=SCALE).then_inc(sem("upper"), 1)
                with act.Fori(0, STEPS // 2) as s2:
                    for half in range(2):
                        with act.Fori(0, NT // ADJ_SLOTS) as a:
                            for u in range(ADJ_SLOTS):
                                n = s2 * (2 * NT) + a * ADJ_SLOTS + (half * NT + u)
                                act.wait_ge(sem("y_tiles"), n + 1 + ADJ_SLOTS)
                                act.activation(halves((A, E)[half])[:, bass.ds(a * ADJ_SLOTS + u, 1), 0:D],
                                               nodes(C)[:, bass.ds(a * ADJ_SLOTS + u, 1), :],
                                               ACT.Copy, scale=SCALE).then_inc(sem("upper"), 1)
            with act.Else():
                with act.Fori(0, STEPS) as s:
                    sweep((s + 3) * NG)

        @block.tensor
        def _(pe):
            def sweep(base, ready, width=D, hist=False):
                def within(j, u, m):
                    i = j * SLOTS + u
                    pe.wait_ge(selected, (i + base) * GT + m + 1)
                    ready(j, u, i, m)
                    pe.wait_ge(evacuated, (i + base) * GT + m + 1)
                    pe.matmul(ps[m][:, 0:width], S[:, u % 2, GT - 1 - m, :], G[:, u, GT - 1 - m, 0:width],
                              start=True, stop=True).then_inc(tile_summed, 1)

                def groups(j, last=False):
                    for u in range(SLOTS):
                        for m in range(GT):
                            if m < GT - 2:
                                within(j, u, m + 2)
                            elif u < SLOTS - 1:
                                within(j, u + 1, m + 2 - GT)
                            elif not last:
                                within(j + 1, 0, m + 2 - GT)
                            pe.wait_ge(carried, (j * SLOTS + u + base) * GT + m + 2)
                            pe.matmul(ps[m][:, 0:width], carry_mask[0:1, u % 2, GT - 1 - m, :],
                                      carry_rows[0:1, (m - 1) % GT, 0:width],
                                      start=False, stop=True, skip_group_check=True).then_inc(summed, 1)
                        if hist:
                            pe.wait_ge(hist_ready, j * SLOTS + u + 1)
                            for k in range(GT):
                                mm = pe.matmul(pt[0][:, 0:NT], hot_lo[:, u % 2, k, :], hot_hi[:, u % 2, k, :],
                                               start=False, stop=False, skip_group_check=True)
                            mm.then_inc(hist_used, 1)

                within(0, 0, 0)
                within(0, 0, 1)
                with pe.Fori(0, NG // SLOTS - 1) as j:
                    groups(j)
                groups(NG // SLOTS - 1, last=True)

            def transposes(src, done, free, before=0, norm=None, chunk=None):
                for r in range(PTN):
                    if norm is not None:
                        pe.wait_ge(sem("normalized"), norm * NT + (r + 1) * T7)
                    if chunk is not None:
                        pe.wait_ge(chunk, r + 1)
                    if r >= 2:
                        pe.wait_ge(free, before + r - 1)
                    for n in range(T7):
                        mm = pe.transpose(pt[r % 2][:, n * P:(n + 1) * P], src(r * T7 + n), ident[:, :])
                    mm.then_inc(done, 1)

            def tiles(v):
                return lambda n: v[:, n * P:(n + 1) * P]

            pe.sem_inc(summed, CREDIT_SUM)
            pe.wait_ge(sem("made"), 6)
            pe.wait_ge(sem("weights_in"), 16 * len(LOADS))
            pe.wait_ge(sem("filter"), 2)
            pe.matmul(ps[0][:, 0:D], cs[:, 0, :], cs_w[:, 0, :], start=True, stop=False)
            pe.matmul(ps[0][:, 0:D], cs[:, 1, :], cs_w[:, 1, :], start=False, stop=True).then_inc(sem("filter_ps"), 1)
            pe.wait_ge(sem("filter_c"), 1)
            pe.matmul(ps[1][:, 0:D], w_in[:, :], c_mat[:, :], start=True, stop=True).then_inc(sem("filter_ps"), 1)
            pe.matmul(ps[2][:, 0:1], c_mat[:, :], cols[:, 1:2], start=True, stop=True).then_inc(sem("filter_ps"), 1)
            transposes(tiles(A), sem("hT_ps"), sem("hT"), norm=0)
            pe.wait_ge(sem("hT"), PTN)
            pe.wait_ge(sem("w_tot"), 2)
            pe.wait_ge(sem("hist_zero"), 1)
            pe.matmul(pt[0][:, 0:NT], hot_lo[:, 0, 0, :], hot_hi[:, 0, 0, :], start=True, stop=False,
                      skip_group_check=True).then_inc(sem("hist_started"), 1)

            def rows_in(base):
                def ready(j, u, i, m):
                    if m == 0:
                        pe.wait_ge(gathered[u], (j + 1 + base) * (16 * GT))
                return ready
            per = NG // SLOTS
            sweep(0, rows_in(0), hist=True)
            pe.wait_ge(sem("counts"), 1)
            pe.wait_ge(evacuated, NG * GT + CREDIT_EV)
            pe.matmul(ps[0][:, 0:NT], iota_f[:, :], cnt[:, :], start=True, stop=True)
            pe.matmul(ps[1][:, 0:NT], ones[:, :], cnt[:, :], start=True, stop=True).then_inc(sem("starts_ps"), 1)
            transposes(tiles(C), sem("aggT_ps"), sem("aggT"), chunk=sem("agg"))
            pe.wait_ge(sem("aggT"), PTN)
            for n in range(14):
                if n >= 4:
                    pe.wait_ge(sem("mix_out"), n - 3)
                c = slice(n * 448, (n + 1) * 448)
                pe.matmul(ps[n % 4][:, 0:448], w_tot[:, :], B[:, c], start=True, stop=False)
                pe.matmul(ps[n % 4][:, 0:448], wf[:, 1, :], Dw[:, c], start=False, stop=True
                          ).then_inc(sem("mix_ps"), 1)
            pe.wait_ge(sem("gelu"), 2)
            transposes(tiles(E), sem("x1_ps"), sem("x1"))
            transposes(tiles(Dw), sem("h1T_ps"), sem("h1T"), norm=1)
            pe.wait_ge(sem("h1T"), PTN)
            pe.wait_ge(sem("rel_w"), 1)
            for n in range(NT):
                for k in range(8):
                    g = 8 * n + k
                    if g >= 4:
                        pe.wait_ge(sem("rel_dve" if k % 2 else "rel_act"), (g - 4) // 2 + 1)
                    pe.matmul(ps[k % 4][:, :], B[:, n * P:(n + 1) * P], A[:, k * 512:(k + 1) * 512],
                              start=True, stop=True).then_inc(sem("rel_ps"), 1)
            pe.wait_ge(sem("rel_act"), 4 * NT)
            pe.wait_ge(sem("rel_dve"), 4 * NT)

            def scaled_in(j, u, i, m):
                pe.wait_ge(scaled, i * GT + m + 1)
            sweep(NG, scaled_in)
            transposes(tiles(A), sem("h2T_ps"), sem("h2T"), norm=2)
            pe.wait_ge(sem("h2T"), PTN)
            for r in range(PTN):
                if r >= 2:
                    pe.wait_ge(sem("gat_rows"), r - 1)
                for n in range(T7):
                    mm = pe.matmul(pt[r % 2][:, n * P:(n + 1) * P], B[:, (r * T7 + n) * P:(r * T7 + n + 1) * P],
                                   w_gat[:, :], start=True, stop=True)
                mm.then_inc(sem("gat_ps"), 1)
            pe.wait_ge(sem("gat_rows"), PTN)

            pe.wait_ge(sem("worst"), 1)
            pe.transpose(ps[0][0:1, 0:P], end_col[:, 0:1], ident[:, :]).then_inc(sem("worst_ps"), 1)
            for k, v in enumerate((A, Dw, X)):
                pe.wait_ge(sem("permuted"), k + 1)
                for r in range(PTN):
                    g = k * PTN + r
                    if g >= 2:
                        pe.wait_ge(sem("to_heads"), g - 1)
                    for n in range(T7):
                        mm = pe.transpose(pt[g % 2][:, n * P:(n + 1) * P], tiles(v)(r * T7 + n), ident[:, :])
                    mm.then_inc(sem("heads_ps"), 1)
            pe.wait_ge(sem("to_heads"), 3 * PTN)
            chains = 0
            for n, back in enumerate((False, True, True, False, True)):
                pe.wait_ge(sem("ends"), n + 1)
                pe.transpose(ps[0][0:1, 0:P], end_col[:, 0:1], ident[:, :]).then_inc(sem("ends_ps"), 1)
                if back:
                    chains += 1
                    pe.wait_ge(sem("starts"), chains)
                    pe.matmul(ps[1][:, 0:1], chain_row[0:1, 5, :], ones[0:1, 0:1], start=True, stop=True
                              ).then_inc(sem("starts_c"), 1)
            for k, v in enumerate((X, A)):
                pe.wait_ge(sem("edge_w" if k else "maxima"), 1)
                for r in range(PTN):
                    g = k * PTN + r
                    if g >= 2:
                        pe.wait_ge(sem("from_heads"), g - 1)
                    for n in range(T7):
                        mm = pe.transpose(pt[g % 2][:, n * P:(n + 1) * P], v[:, (r * T7 + n) * P:(r * T7 + n + 1) * P],
                                          ident[:, :])
                    mm.then_inc(sem("edges_ps"), 1)
            pe.wait_ge(sem("from_heads"), 2 * PTN)

            def weighted_in(j, u, i, m):
                if m == 0:
                    pe.wait_ge(sem("beside"), i + 1)
                    settle(pe)
                pe.wait_ge(sem("weighted"), i * GT + m + 1)
            sweep(2 * NG, weighted_in, width=D + HEADS)
            transposes(tiles(A), sem("h3T_ps"), sem("h3T"), chunk=sem("ln_a"))
            pe.wait_ge(sem("h3T"), PTN)
            for n in range(14 + 1):
                if n < 14:
                    for c in range(4):
                        g = 4 * n + c
                        if g >= 2:
                            pe.wait_ge(sem("ff1"), g - 1)
                        pe.matmul(ps[c % 2][:, 0:448], w1[:, c * P:(c + 1) * P], B[:, n * 448:(n + 1) * 448],
                                  start=True, stop=True).then_inc(sem("ff1_ps"), 1)
                if n >= 1:
                    pe.wait_ge(sem("ff1"), 4 * n)
                    if n >= 3:
                        pe.wait_ge(sem("ff2"), n - 2)
                    base = ((n - 1) % 2) * 1792
                    for c in range(4):
                        mm = pe.matmul(ps[2 + (n - 1) % 2][:, 0:448], w2[:, c, :],
                                       E[:, base + c * 448:base + (c + 1) * 448], start=(c == 0), stop=(c == 3))
                    mm.then_inc(sem("ff2_ps"), 1)
            pe.wait_ge(sem("ff2"), 14)
            transposes(tiles(Dw), sem("ffb_ps"), sem("ffb"))
            pe.wait_ge(sem("ffb"), PTN)
            dense = pe.value_load(verdict[0:1, 0:1], min_val=0, max_val=1)
            banks = [ps[0][:, :], ps[1][:, :], ps[2][:, :], ps[3][:, :],
                     pt[0][:, 0:512], pt[0][:, 512:1024], pt[1][:, 0:512]]
            with pe.If(dense == 1):
                with pe.Fori(0, STEPS // 2) as s2:
                    for half in range(2):
                        y = halves((E, A)[half])
                        pe.wait_ge(sem("lower"), s2 * (2 * NT) + (half + 1) * NT)
                        settle(pe)
                        with pe.Fori(0, NT // ADJ_SLOTS) as a:
                            for u in range(ADJ_SLOTS):
                                n = s2 * (2 * NT) + a * ADJ_SLOTS + (half * NT + u)
                                pe.wait_ge(sem(f"adj_in{u}"), s2 * (2 * 16 * NT // ADJ_SLOTS) + a * 16
                                           + (half * 16 * NT // ADJ_SLOTS + 16))
                                settle(pe)
                                pe.wait_ge(sem("y_tiles"), n + 1)
                                settle(pe)
                                for i in range(NT):
                                    mm = pe.matmul(banks[u][:, 0:2 * D], adj_ring[:, u, i * P:(i + 1) * P],
                                                   y[:, i, :], start=(i == 0), stop=(i == NT - 1))
                                mm.then_inc(sem("multiplied"), 1)
            with pe.Else():
                with pe.Fori(0, STEPS) as s:
                    sweep((s + 3) * NG, rows_in((s + 3) * per))

        @block.vector
        def _(dve):
            links = [0]

            def link(ins):
                links[0] += 1
                ins.then_inc(sem("dve_link"), 1)
                dve.wait_ge(sem("dve_link"), links[0])

            def sweep(base, hist=False, weights=False):
                width = D + HEADS if weights else D

                def weight_rows(j, u, m):
                    k = GT - 1 - m
                    if m == 0:
                        dve.wait_ge(reloaded[u], j * 16 + 16)
                    g = G[:, u, k, 0:D].rearrange("p (h c) -> p h c", c=HC)
                    w = B[:, bass.ds(((NG - 1 - (j * SLOTS + u)) * GT + k) * HEADS, HEADS)]
                    dve.tensor_tensor(g, g, bc(w, HC), MUL).then_inc(sem("weighted"), 1)

                def select(j, u, m):
                    i = j * SLOTS + u
                    gi = i + base
                    t0 = (NG - 1 - i) * GT
                    k = GT - 1 - m
                    if m == 0:
                        dve.wait_ge(dst_in[u % 2], (gi - u % 2) * 8 + 16)
                        dve.wait_ge(summed, gi * GT + (CREDIT_SUM - GT))
                        settle(dve)
                        dve.tensor_tensor(carry_mask[0:1, u % 2, :, :],
                                          dst_b[0:1, u % 2, :].rearrange("p (k e) -> p k e", e=P),
                                          bc(dst_f[0:1, bass.ds(t0 + 1, GT)], P), ALU.is_equal)
                        if hist:
                            dve.wait_ge(hist_used, i + 1)
                            settle(dve)
                    dve.scalar_tensor_tensor(S[:, u % 2, k, :], dst_b[:, u % 2, k * P:(k + 1) * P],
                                             dst_f[:, bass.ds(t0 + k, 1)], tri[:, :], ALU.is_equal, MUL
                                             ).then_inc(selected, 1)
                    if hist:
                        dve.tensor_scalar(hot_lo[:, u % 2, k, :], iota_h,
                                          E[:, bass.ds(t0 + k, 1)], None, ALU.is_equal)
                        a = dve.tensor_scalar(hot_hi[:, u % 2, k, :], iota_h[:, 0:NT],
                                              E[:, bass.ds(t0 + k + ET, 1)], None, ALU.is_equal)
                        if m == GT - 1:
                            a.then_inc(hist_ready, 1)

                def groups(j, last=False):
                    for u in range(SLOTS):
                        gi = j * SLOTS + u + base
                        dve.wait_ge(selected, gi * GT + 1)
                        settle(dve)
                        for m in range(GT):
                            dve.wait_ge(tile_summed, gi * GT + m + 1)
                            dve.wait_ge(carried, gi * GT + m + 1)
                            settle(dve)
                            dve.scalar_tensor_tensor(carry_rows[0:1, m, 0:width],
                                                     carry_rows[0:1, (m - 1) % GT, 0:width],
                                                     carry_mask[0:1, u % 2, GT - 1 - m, 0:1],
                                                     ps[m % 4][0:1, 0:width], MUL, ADD).then_inc(carried, 1)
                            if last and u == SLOTS - 1:
                                continue
                            nj, nu = (j, u + 1) if u < SLOTS - 1 else (j + 1, 0)
                            if weights:
                                weight_rows(nj, nu, m)
                            if m:
                                select(nj, nu, m - 1)
                            if m == GT - 1:
                                select(nj, nu, m)

                for m in range(GT):
                    if weights:
                        weight_rows(0, 0, m)
                    select(0, 0, m)
                with dve.Fori(0, NG // SLOTS - 1) as j:
                    groups(j)
                groups(NG // SLOTS - 1, last=True)

            roots = [0]

            def inv_sqrt(v):
                roots[0] += 1
                dve.sem_inc(sem("to_root"), 1)
                dve.wait_ge(sem("rooted"), roots[0])
                link(dve.reciprocal(v, v))

            norms = [0]

            def layernorm(x, h, gain=None, shift=None, tmp=None, plus=None, done=None):
                st = tmp[:, 0:6 * NT].rearrange("p (t k) -> p t k", k=6)
                mv = tmp[:, 6 * NT:8 * NT].rearrange("p (t k) -> p t k", k=2)
                for n in range(NT):
                    a = dve.bn_stats(st[:, n, :], nodes(x)[:, n, :])
                link(a)
                for n in range(NT):
                    a = dve.bn_aggr(mv[:, n, :], st[:, n, :])
                link(a)
                link(dve.tensor_scalar(stat_b[:, :], mv[:, :, 1], EPS, None, ADD))
                inv_sqrt(stat_b[:, :])
                dve.scalar_tensor_tensor(stat_a[:, :], mv[:, :, 0], -1.0, stat_b[:, :], MUL, MUL
                                         ).then_inc(sem("norm_stats"), 1)
                norms[0] += 1
                if gain is None:
                    dve.wait_ge(sem("normalized"), norms[0] * NT)
                    return
                for r in range(PTN):
                    c = slice(r * T7, (r + 1) * T7)
                    dve.wait_ge(sem("normalized"), (norms[0] - 1) * NT + (r + 1) * T7)
                    link(dve.tensor_tensor(nodes(h)[:, c, :], nodes(h)[:, c, :], row_bc(rows[:, gain, :], T7), MUL))
                    a = dve.tensor_tensor(nodes(h)[:, c, :], nodes(h)[:, c, :], row_bc(rows[:, shift, :], T7), ADD)
                    if plus is not None:
                        link(a)
                        a = dve.tensor_tensor(nodes(plus)[:, c, :], nodes(plus)[:, c, :], nodes(h)[:, c, :], ADD)
                    if done is not None:
                        a.then_inc(done, 1)
                    else:
                        link(a)

            dve.memset(src_i[:, FULL:ET], 0)
            dve.memset(rel_i[:, FULL:ET], 0)
            dve.memset(weight_e[:, FULL:ET], 0.0)
            dve.memset(C[:, :], 0.0).then_inc(sem("padded"), 1)
            dve.memset(Ei[0:1, 0:EP - N_EDGES + P], NP).then_inc(sem("padded"), 1)
            dve.memset(Bi[:, FULL:ET], NP).then_inc(sem("padded"), 1)
            dve.memset(no_key, -1.0).then_inc(sem("padded"), 1)
            dve.memset(O[:, :, :, :], 0.0)
            dve.memset(carry_rows[:, :, :], 0.0).then_inc(carried, 1)
            dve.sem_inc(evacuated, CREDIT_EV)
            dve.sem_inc(as_kept, 4)
            dve.sem_inc(hist_used, 2)
            dve.memset(dst_f[:, ET:ET + 1], -1.0)
            dve.wait_ge(sem("edges_in"), 16 * len(EDGES))
            dve.wait_ge(sem("dst_padded"), 96)
            dve.tensor_copy(dst_f[:, 0:ET], Bi[:, 0:ET])
            dve.tensor_scalar(Bi[:, ET:2 * ET], Bi[:, 0:ET], 127, None, ALU.bitwise_and)
            link(dve.tensor_scalar(Bi[:, 2 * ET:3 * ET], Bi[:, 0:ET], 7, None, ALU.logical_shift_right))
            dve.tensor_copy(E[:, 0:2 * ET], Bi[:, ET:3 * ET])
            dve.scalar_tensor_tensor(rel_i[:, :], src_i[:, :], float(RELS), rel_i[:, :], MUL, ADD
                                     ).then_inc(sem("edge_numbers"), 1)
            dve.wait_ge(sem("key_parts_in"), 32)
            link(dve.tensor_scalar(key_parts[1], key_parts[1], KEY_DST - 1, 13, ALU.bitwise_and,
                                   ALU.logical_shift_left))
            link(dve.tensor_tensor(key_parts[1], key_parts[1], key_parts[0], ALU.bitwise_or))
            dve.tensor_copy(key_parts[0].bitcast(F32), key_parts[1]).then_inc(sem("keys"), 1)
            dve.wait_ge(sem("made"), 6)
            link(dve.tensor_copy(iota_h, iota_i[:, :]))
            dve.wait_ge(sem("weights_in"), 16 * len(LOADS))
            link(dve.tensor_scalar(cs_w[:, 2, :], cs[:, 3, :], cw[:, 1:2], None, MUL))
            dve.scalar_tensor_tensor(cs_w[:, 0, :], cs[:, 2, :], cw[:, 0:1], cs_w[:, 2, :], MUL, SUB
                                     ).then_inc(sem("filter"), 1)
            dve.wait_ge(sem("filter"), 1)
            link(dve.tensor_scalar(cs_w[:, 2, :], cs[:, 2, :], cw[:, 1:2], None, MUL))
            dve.scalar_tensor_tensor(cs_w[:, 1, :], cs[:, 3, :], cw[:, 0:1], cs_w[:, 2, :], MUL, ADD
                                     ).then_inc(sem("filter"), 1)
            dve.wait_ge(sem("filter_ps"), 1)
            dve.tensor_copy(c_mat[:, :], ps[0][:, 0:D]).then_inc(sem("filter_c"), 1)
            dve.wait_ge(sem("filter_ps"), 3)
            dve.scalar_tensor_tensor(w_tot[:, :], ps[1][:, 0:D], cols[:, 4:5], wf[:, 0, :], MUL, ADD
                                     ).then_inc(sem("w_tot"), 1)
            dve.scalar_tensor_tensor(cols[:, 5:6], ps[2][:, 0:1], cols[:, 4:5], cols[:, 0:1], MUL, ADD
                                     ).then_inc(sem("w_tot"), 1)
            dve.wait_ge(sem("x_in"), 32)
            dve.wait_ge(sem("seeds_zero"), 32)
            for k in range(SLOTS):
                dve.wait_ge(kept[k], 16)
            for k in range(2):
                dve.wait_ge(stored[k], 16)
            layernorm(X, A, tmp=C)
            dve.wait_ge(sem("hT"), PTN)
            dve.wait_ge(sem("table0"), 16)
            dve.memset(A[:, :], 0.0).then_inc(sem("zeros"), 1)
            dve.memset(hot_lo[:, 0, 0, :], 0.0)
            dve.memset(hot_hi[:, 0, 0, :], 0.0).then_inc(sem("hist_zero"), 1)
            dve.wait_ge(sem("hist_started"), 1)
            sweep(0, hist=True)
            dve.wait_ge(hist_used, NG + 2)
            dve.tensor_scalar(iota_f[:, :], tri[:, :], -1.0, 1.0, MUL, ADD)
            dve.tensor_copy(cnt[:, :], pt[0][:, 0:NT]).then_inc(sem("counts"), 1)
            dve.wait_ge(sem("counts"), 1)
            link(dve.tensor_scalar(mask[:, :], cnt[:, :], 1.0, None, MIN))
            link(dve.tensor_scalar(rcnt[:, :], cnt[:, :], 1.0, None, MAX))
            link(dve.reciprocal(rcnt[:, :], rcnt[:, :]))
            link(dve.tensor_tensor(rcnt[:, :], rcnt[:, :], mask[:, :], MUL))
            link(dve.tensor_scalar(dinv[:, :], cnt[:, :], 1.0, None, ADD))
            inv_sqrt(dinv[:, :])
            dve.wait_ge(sem("starts_ps"), 1)
            link(dve.tensor_copy(stat_a[:, :], ps[1][:, 0:NT]))
            link(dve.tensor_tensor_scan(stat_b[:, :], ones[:, 0:NT], stat_a[:, :], 0.0, MUL, ADD))
            link(dve.tensor_tensor(stat_b[:, :], stat_b[:, :], stat_a[:, :], SUB))
            link(dve.tensor_tensor(row_f[:, :], stat_b[:, :], ps[0][:, 0:NT], ADD))
            dve.tensor_copy(row_i[:, :], row_f[:, :]).then_inc(sem("row_starts"), 1)
            link(dve.tensor_scalar(stat_a[:, :], mask[:, :], -2.0 * EP, 2.0 * EP, MUL, ADD))
            link(dve.tensor_tensor(stat_a[:, :], stat_a[:, :], row_f[:, :], ADD))
            link(dve.tensor_copy(seed_i[:, :], stat_a[:, :]))
            dve.wait_ge(sem("adj_zero"), 16 * NT)
            w_rel = A[:, 0:RELS * D].rearrange("p (r o) -> p r o", o=D)
            tmp = Dw[:, 0:RELS * D].rearrange("p (r o) -> p r o", o=D)
            dve.wait_ge(sem("bases_in"), 32)
            for b in range(BASES):
                link(dve.tensor_tensor(w_rel if b == 0 else tmp, bc(comp[:, :, b], D), row_bc(w_base[:, b, :], RELS), MUL))
                if b:
                    link(dve.tensor_tensor(w_rel, w_rel, tmp, ADD))
            dve.sem_inc(sem("rel_w"), 1)
            for r in range(PTN):
                c = slice(r * T7, (r + 1) * T7)
                dve.wait_ge(node_part[r], 16 * T7)
                dve.tensor_tensor(nodes(C)[:, c, :], nodes(C)[:, c, :], bc(rcnt[:, c], D), MUL
                                  ).then_inc(sem("agg"), 1)
            for n in range(14):
                dve.wait_ge(sem("mix_out"), n + 1)
                last = dve.bn_stats(bn_st[:, n, :], E[:, n * 448:min((n + 1) * 448, N_NODES)])
            link(last)
            link(dve.bn_aggr(bn[:, 0:2], bn_st[:, :, :].rearrange("p a b -> p (a b)")))
            link(dve.tensor_scalar(bn[:, 2:3], bn[:, 1:2], EPS, None, ADD))
            inv_sqrt(bn[:, 2:3])
            link(dve.tensor_scalar(bn[:, 2:3], bn[:, 2:3], cols[:, 2:3], None, MUL))
            for n in range(2):
                half = slice(n * NP // 2, (n + 1) * NP // 2)
                dve.tensor_scalar(E[:, half], E[:, half], bn[:, 0:1], bn[:, 2:3], SUB, MUL).then_inc(sem("bn_ready"), 1)
            for r in range(PTN):
                c = slice(r * T7 * P, (r + 1) * T7 * P)
                dve.wait_ge(sem("x1_ps"), r + 1)
                dve.tensor_tensor(X[:, c], X[:, c], pt[r % 2][:, 0:T7 * P], ADD).then_inc(sem("x1"), 1)
            dve.wait_ge(sem("x1"), PTN)
            dve.sem_inc(sem("x1_done"), 1)
            layernorm(X, Db, tmp=C)
            for n in range(NT):
                if n >= 2:
                    dve.wait_ge(sem(f"rel_stored{n % 2}"), 16 * (n // 2))
                for k in range(1, 8, 2):
                    dve.wait_ge(sem("rel_ps"), 8 * n + k + 1)
                    dve.tensor_copy((C, E)[n % 2][:, k * 512:(k + 1) * 512], ps[k % 4][:, :]).then_inc(sem("rel_dve"), 1)
            sweep(NG)
            for r in range(PTN):
                c, cx = slice(r * T7, (r + 1) * T7), slice(r * T7 * D, (r + 1) * T7 * D)
                dve.wait_ge(node_part[r], 2 * 16 * T7)
                link(dve.tensor_tensor(nodes(C)[:, c, :], nodes(C)[:, c, :], bc(mask[:, c], D), MUL))
                link(dve.tensor_tensor(nodes(C)[:, c, :], nodes(C)[:, c, :], row_bc(rows[:, BIAS1, :], T7), ADD))
                link(dve.scalar_tensor_tensor(X[:, cx], C[:, cx], 0.0, X[:, cx], MAX, ADD))
            layernorm(X, A, tmp=C)
            dve.wait_ge(sem("gat_rows"), PTN)
            for k, att in ((0, ATT_D), (1, ATT_S)):
                link(dve.tensor_tensor(nodes(Db), nodes(C), row_bc(rows[:, att, :], NT), MUL))
                link(dve.tensor_reduce(E[:, 0:NT * HEADS], Db.rearrange("p (t c) -> p t c", c=HC), AX.X, ADD))
                dve.tensor_copy(scores[:, :, k * HEADS:(k + 1) * HEADS],
                                E[:, 0:NT * HEADS].rearrange("p (t h) -> p t h", h=HEADS)
                                ).then_inc(sem("scores_ready"), 1)
                dve.wait_ge(sem("scores_ready"), k + 1)
            key_i = same.rearrange("p k e -> p (k e)")[:, 0:ET].bitcast(I32)
            link(dve.tensor_copy(key_i, dst_f[:, 0:ET]))
            link(dve.tensor_scalar(key_i, key_i, KEY_DST - 1, 13, ALU.bitwise_and, ALU.logical_shift_left))
            link(dve.tensor_tensor(key_i, key_i, src_i[:, :], ALU.bitwise_or))
            link(dve.tensor_copy(weight_e[:, :], key_i))
            dve.memset(window_w[:, 2 * P:3 * P], 1.0)
            dve.memset(window_w[:, 0:P], 1.0 + EARLIER)
            link(dve.tensor_tensor(window_w[:, P:2 * P], tri[:, :], ident[:, :], SUB))
            link(dve.tensor_scalar(window_w[:, P:2 * P], window_w[:, P:2 * P], float(EARLIER), 1.0, MUL, ADD))
            with dve.Fori(0, NG // SLOTS) as j:
                for u in range(SLOTS):
                    q = j * SLOTS + u
                    dve.wait_ge(sem(f"window_in{u % 2}"), j * 32 + (16 + 16 * (u // 2)))
                    for k in range(GT):
                        a = dve.scalar_tensor_tensor(same[:, k, :], win[:, u % 2, k * P:(k + 3) * P],
                                                     weight_e[:, bass.ds(q * GT + k, 1)], window_w,
                                                     ALU.is_equal, MUL, accum_out=codes[:, bass.ds(q * GT + k, 1)])
                    a.then_inc(sem("searched"), 1)
                    dve.wait_ge(sem("searched"), q + 1)
                    settle(dve)
            dve.wait_ge(sem("searched"), NG)
            dve.wait_ge(sem("spilled"), 32)
            e0, e1, e2, e3 = (A[:, k * ET:(k + 1) * ET].bitcast(I32) for k in range(4))
            f0, f1 = A[:, 4 * ET:5 * ET], A[:, 5 * ET:6 * ET]
            SHL, SHR, AND, OR = ALU.logical_shift_left, ALU.logical_shift_right, ALU.bitwise_and, ALU.bitwise_or
            link(dve.tensor_copy(e0, codes))
            link(dve.tensor_scalar(e1, e0, 10, None, SHR))
            link(dve.tensor_scalar(e0, e0, EARLIER - 1, None, AND))
            link(dve.tensor_copy(f0, e0))
            link(dve.tensor_scalar(f1, dst_f[:, 0:ET], float(NP), None, ALU.is_lt))
            link(dve.tensor_tensor(f0, f0, f1, MUL))
            dve.tensor_scalar(f1, f0, float(MOST), None, MIN)
            link(dve.tensor_reduce(end_col[:, 0:1], f0, AX.X, MAX))
            link(dve.tensor_copy(weight_e[:, 0:ET // 4].bitcast(F8), f1, saturate=False))
            link(dve.tensor_reduce(end_col[:, 1:2], cnt[:, :], AX.X, MAX))
            dve.scalar_tensor_tensor(end_col[:, 0:1], end_col[:, 1:2], float(MOST) / MOST_DEGREE, end_col[:, 0:1],
                                     MUL, MAX).then_inc(sem("worst"), 1)
            link(dve.tensor_copy(e2, dst_f[:, 0:ET]))
            link(dve.tensor_scalar(e3, e2, 7, 20, SHR, SHL))
            link(dve.tensor_scalar(e2, e2, P - 1, None, AND))
            link(dve.tensor_tensor(e3, e3, e2, OR))
            link(dve.tensor_scalar(e2, src_i[:, :], P - 1, 13, AND, SHL))
            link(dve.tensor_tensor(e3, e3, e2, OR))
            link(dve.tensor_scalar(e2, src_i[:, :], 7, 7, SHR, SHL))
            link(dve.tensor_tensor(e3, e3, e2, OR))
            link(dve.tensor_copy(f0, e1))
            link(dve.tensor_scalar(f0, f0, 1.0, None, MIN))
            link(dve.tensor_copy(e1, f0))
            link(dve.tensor_scalar(e1, e1, 26, None, SHL))
            link(dve.tensor_tensor(rel_i[:, :], e3, e1, OR))
            dve.wait_ge(sem("worst_ps"), 1)
            link(dve.tensor_tensor(f0[0:1, 0:ET - 3], dst_f[0:1, 3:ET], dst_f[0:1, 0:ET - 3], SUB))
            link(dve.tensor_reduce(end_col[0:1, 1:2], f0[0:1, 0:ET - 3], AX.X, MAX))
            link(dve.tensor_scalar(end_col[0:1, 1:2], end_col[0:1, 1:2], float(KEY_DST), 2.0 * MOST, ALU.is_ge, MUL))
            link(dve.tensor_reduce(in_col[0:1, 0:1], ps[0][0:1, 0:P], AX.X, MAX))
            link(dve.tensor_tensor(in_col[0:1, 0:1], in_col[0:1, 0:1], end_col[0:1, 1:2], MAX))
            link(dve.tensor_scalar(in_col[0:1, 0:1], in_col[0:1, 0:1], float(MOST), None, ALU.is_le))
            link(dve.tensor_copy(verdict[:, :], in_col[0:1, 0:1]))
            dve.sem_inc(sem("judged"), 1)
            dve.wait_ge(as_kept, NG + 4)
            dve.wait_ge(sem("spilled"), 32)
            by_place = lambda v: v[:, 0:NP].rearrange("p (j h c) -> p j h c", h=HEADS, c=CH)
            by_tile = lambda v: v[:, 0:NP].rearrange("p (c j h) -> p j h c", c=CH, h=HEADS)
            for k, (to, of) in enumerate(((A, E), (Dw, B), (X, C))):
                if k == 1:
                    dve.wait_ge(sem("seeds_in"), 16 * 2 * SEED_PARTS)
                dve.tensor_copy(by_place(to), by_tile(of)).then_inc(sem("permuted"), 1)
            dve.wait_ge(sem("to_heads"), 3 * PTN)
            dve.wait_ge(sem("dst_heads"), 16 * 2 * HEADS)
            link(dve.tensor_tensor(E[:, :], Bi, Ci, ALU.not_equal))
            link(dve.tensor_scalar(B[:, :], E[:, :], BIG, -BIG, MUL, ADD))
            link(dve.tensor_tensor(X[:, :], X[:, :], B[:, :], ADD))
            link(dve.tensor_tensor(B[:, :], A[:, :], X[:, :], MAX))
            link(dve.tensor_scalar(C[:, :], E[:, :], -BIG, None, MUL))
            link(dve.tensor_scalar(X[:, :], E[:, :], -1.0, 1.0, MUL, ADD))

            hc = lambda v: v.rearrange("p (h c) -> p h c", c=CH)
            state, through, through_01, result, starts = (chain_row[0:1, k, :] for k in (0, 1, 2, 3, 5))
            events = [0, 0]

            def flags(first_edges):
                link(dve.tensor_reduce(end_col[:, 0:1], first_edges[:, 0:NP], AX.X, MAX))
                dve.sem_inc(sem("ends"), 1)
                events[0] += 1
                dve.wait_ge(sem("ends_ps"), events[0])
                link(dve.tensor_scalar(through_01, ps[0][0:1, 0:P], -1.0, 1.0, MUL, ADD))

            def chain(scan, data, rev, largest):
                zero = -BIG if largest else 0.0
                if largest:
                    link(dve.tensor_scalar(through, through_01, BIG, -BIG, MUL, ADD))
                else:
                    link(dve.tensor_copy(through, through_01))
                at = slice(CH - 1, CH) if rev else slice(0, 1)
                link(dve.memset(hc(through)[:, :, at], zero))
                link(scan(zero))
                at = slice(0, 1) if rev else slice(CE - 1, CE)
                link(dve.tensor_copy(end_col[:, 0:1], data[:, at]))
                dve.sem_inc(sem("ends"), 1)
                events[0] += 1
                events[1] += 1
                dve.wait_ge(sem("ends_ps"), events[0])
                link(dve.tensor_copy(state, ps[0][0:1, 0:P]))
                way = (lambda v: v[:, ::-1]) if rev else (lambda v: v)
                link(dve.tensor_tensor_scan(way(result), way(through), way(state), zero,
                                            ADD if largest else MUL, MAX if largest else ADD))
                link(dve.memset(starts, zero))
                if rev:
                    link(dve.tensor_copy(hc(starts)[:, :, 0:CH - 1], hc(result)[:, :, 1:CH]))
                else:
                    link(dve.tensor_copy(hc(starts)[:, :, 1:CH], hc(result)[:, :, 0:CH - 1]))
                dve.sem_inc(sem("starts"), 1)
                dve.wait_ge(sem("starts_c"), events[1])
                link(dve.tensor_copy(in_col[:, :], ps[1][:, 0:1]))
                link(scan(in_col[:, 0:1]))

            flags(E)
            chain(lambda z: dve.tensor_tensor_scan(E[:, :], X[:, :], Db, z, MUL, ADD), E, False, False)
            dve.sem_inc(sem("x_free"), 1)
            chain(lambda z: dve.tensor_tensor_scan(Db, C[:, :], B[:, :], z, ADD, MAX), Db, False, True)
            dve.wait_ge(sem("dst_heads2"), 16 * 2 * HEADS)
            Xi = X[:, :].bitcast(I32)
            dve.tensor_tensor(B[:, 0:CE - 1], Xi[:, 0:CE - 1], Xi[:, 1:CE], ALU.not_equal)
            link(dve.tensor_tensor(B[:, CE - 1:CE], Xi[:, CE - 1:CE], next_dst, ALU.not_equal))
            link(dve.tensor_scalar(C[:, :], B[:, :], -BIG, None, MUL))
            flags(B)
            chain(lambda z: dve.tensor_tensor_scan(X[:, ::-1], C[:, ::-1], Db[:, ::-1], z, ADD, MAX), X, True, True)
            dve.sem_inc(sem("maxima"), 1)
            link(dve.tensor_tensor(A[:, :], A[:, :], E[:, :], ADD))
            link(dve.scalar_tensor_tensor(A[:, :], A[:, :], SLOPE, A[:, :], MUL, MAX))
            link(dve.tensor_tensor(B[:, :], X[:, :], E[:, :], ADD))
            link(dve.scalar_tensor_tensor(B[:, :], B[:, :], SLOPE, B[:, :], MUL, MAX))
            dve.tensor_tensor(A[:, :], A[:, :], B[:, :], SUB).then_inc(sem("exponents"), 1)
            dve.wait_ge(sem("from_heads"), 2 * PTN)
            sweep(2 * NG, weights=True)
            dve.wait_ge(sem("h2_back"), 16)
            dve.wait_ge(sem("gat_back"), 16)
            dve.wait_ge(sem("x_back"), 16)
            agg = Dw[:, :].rearrange("p (t f) -> p t f", f=WL2)
            K = NT * HEADS
            th = lambda v: v.rearrange("p (t h) -> p t h", h=HEADS)
            heads = lambda v: v.rearrange("p (k c) -> p k c", c=HC)
            link(dve.tensor_scalar(stat_a[:, :], mask[:, :], BIG, -BIG, MUL, ADD))
            for r in range(PTN):
                dve.wait_ge(node_part[r], 3 * 16 * T7)
                c = slice(r * T7, (r + 1) * T7)
                ch, cf = slice(r * T7 * HEADS, (r + 1) * T7 * HEADS), slice(r * T7 * D, (r + 1) * T7 * D)
                e0, e1, e2, e3 = (E[:, k * K:(k + 1) * K][:, ch] for k in range(4))
                a_d, a_s = scores[:, c, 0:HEADS], scores[:, c, HEADS:]
                link(dve.tensor_tensor(th(e0), agg[:, c, D + HEADS:], bc(mask[:, c], HEADS), MUL))
                link(dve.tensor_tensor(th(e0), th(e0), bc(stat_a[:, c], HEADS), ADD))
                link(dve.tensor_tensor(th(e0), th(e0), a_s, MAX))
                link(dve.tensor_tensor(th(e1), th(e0), a_d, ADD))
                link(dve.scalar_tensor_tensor(e1, e1, SLOPE, e1, MUL, MAX))
                link(dve.tensor_tensor(th(e2), a_s, a_d, ADD))
                link(dve.scalar_tensor_tensor(e2, e2, SLOPE, e2, MUL, MAX))
                dve.tensor_tensor(self_w[:, ch], e2, e1, SUB).then_inc(sem("self_exponents"), 1)
                link(dve.tensor_tensor(agg[:, c, 0:D], agg[:, c, 0:D], bc(mask[:, c], D), MUL))
                dve.wait_ge(sem("self_w"), r + 1)
                link(dve.tensor_tensor(th(e3), agg[:, c, D:D + HEADS], bc(mask[:, c], HEADS), MUL))
                link(dve.tensor_tensor(e3, e3, self_w[:, ch], ADD))
                link(dve.reciprocal(e3, e3))
                link(dve.tensor_tensor(heads(B[:, cf]), heads(C[:, cf]), bc(self_w[:, ch], HC), MUL))
                link(dve.tensor_tensor(nodes(B)[:, c, :], nodes(B)[:, c, :], agg[:, c, 0:D], ADD))
                link(dve.tensor_tensor(heads(B[:, cf]), heads(B[:, cf]), bc(e3, HC), MUL))
                link(dve.tensor_tensor(nodes(B)[:, c, :], nodes(B)[:, c, :], row_bc(rows[:, B_GAT, :], T7), ADD))
                link(dve.tensor_tensor(B[:, cf], B[:, cf], A[:, cf], ADD))
            layernorm(B, A, gain=G1, shift=BB1, tmp=C, done=sem("ln_a"))
            for n in range(14):
                dve.wait_ge(sem("ff2_ps"), n + 1)
                dve.tensor_scalar(Dw[:, n * 448:(n + 1) * 448], ps[2 + n % 2][:, 0:448], cols[:, 6:7], None, ADD
                                  ).then_inc(sem("ff2"), 1)
            for r in range(PTN):
                c = slice(r * T7 * P, (r + 1) * T7 * P)
                dve.wait_ge(sem("ffb_ps"), r + 1)
                dve.tensor_tensor(C[:, c], A[:, c], pt[r % 2][:, 0:T7 * P], ADD).then_inc(sem("ffb"), 1)
            dve.wait_ge(sem("ffb"), PTN)
            layernorm(C, B, gain=G2, shift=BB2, tmp=E, plus=X)
            layernorm(X, A, tmp=C)
            dve.tensor_tensor(nodes(C), nodes(A), bc(dinv[:, :], D), MUL).then_inc(sem("y_ready"), 1)
            dve.wait_ge(sem("y_ready"), 1)
            link(dve.tensor_scalar(stat_a[:, :], dinv[:, :], TELEPORT, None, MUL))
            link(dve.tensor_tensor(nodes(B), nodes(A), bc(stat_a[:, :], D), MUL))
            link(dve.tensor_tensor(sc_a[:, :], dinv[:, :], dinv[:, :], MUL))
            link(dve.tensor_scalar(sc_a[:, :], sc_a[:, :], 1.0 - TELEPORT, None, MUL))
            link(dve.tensor_tensor(sc_b[:, :], sc_a[:, :], mask[:, :], MUL))
            dense = dve.value_load(verdict[0:1, 0:1], min_val=0, max_val=1)
            with dve.If(dense == 1):
                dve.tensor_scalar(sc_b[:, :], sc_a[:, :], 1.0 / SCALE, None, MUL)
                dve.wait_ge(sem("upper"), 1)
                dve.scalar_tensor_tensor(halves(E)[:, :, D:2 * D], nodes(C), SCALE, halves(E)[:, :, 0:D], MUL, SUB
                                         ).then_inc(sem("lower"), NT)
                dve.wait_ge(sem("lower"), NT)
                dve.sem_inc(sem("y_tiles"), ADJ_SLOTS)
                banks = [ps[0][:, :], ps[1][:, :], ps[2][:, :], ps[3][:, :],
                         pt[0][:, 0:512], pt[0][:, 512:1024], pt[1][:, 0:512]]
                part_done = sem("part_done")
                with dve.Fori(0, STEPS // 2) as s2:
                    for half in range(2):
                        with dve.Fori(0, NT // ADJ_SLOTS) as a:
                            for u in range(ADJ_SLOTS):
                                n = s2 * (2 * NT) + a * ADJ_SLOTS + (half * NT + u)
                                tile = a * ADJ_SLOTS + u
                                yt = C[:, bass.ds(tile * P, P)]
                                w0, w1 = O[:, u % 2, 0, 0:D], O[:, u % 2, 1, 0:D]
                                dve.scalar_tensor_tensor(w0, yt, sc_a[:, bass.ds(tile, 1)], B[:, bass.ds(tile * P, P)],
                                                         MUL, ADD).then_inc(part_done, 1)
                                dve.wait_ge(part_done, n * 2 + 1)
                                dve.wait_ge(sem("multiplied"), n + 1)
                                dve.scalar_tensor_tensor(w1, banks[u][:, 0:D], sc_b[:, bass.ds(tile, 1)], w0, MUL, ADD
                                                         ).then_inc(part_done, 1)
                                dve.wait_ge(part_done, n * 2 + 2)
                                dve.scalar_tensor_tensor(yt, banks[u][:, D:2 * D], sc_b[:, bass.ds(tile, 1)], w1,
                                                         MUL, ADD).then_inc(sem("y_tiles"), 1)
                                dve.wait_ge(sem("upper"), n + 2)
                                new = halves((A, E)[half])
                                dve.scalar_tensor_tensor(new[:, bass.ds(tile, 1), D:2 * D],
                                                         nodes(C)[:, bass.ds(tile, 1), :], SCALE,
                                                         new[:, bass.ds(tile, 1), 0:D], MUL, SUB
                                                         ).then_inc(sem("lower"), 1)
                dve.wait_ge(sem("lower"), NT * (STEPS + 1))
            with dve.Else():
                with dve.Fori(0, STEPS) as s:
                    sweep((s + 3) * NG)
                    step = sem("step_link")
                    dve.tensor_tensor(nodes(E), nodes(C), bc(sc_a[:, :], D), MUL).then_inc(step, 1)
                    dve.wait_ge(step, s * 3 + 1)
                    dve.tensor_tensor(E[:, :], E[:, :], B[:, :], ADD).then_inc(step, 1)
                    dve.wait_ge(sem("nodes3"), s * (16 * NT) + 16 * NT)
                    dve.tensor_tensor(nodes(Db), nodes(Db), bc(sc_b[:, :], D), MUL).then_inc(step, 1)
                    dve.wait_ge(step, s * 3 + 3)
                    dve.wait_ge(sem("y_stored"), s * 16 + 16)
                    dve.tensor_tensor(C[:, :], E[:, :], Db, ADD).then_inc(sem("y_ready"), 1)
                    dve.wait_ge(sem("y_ready"), s + 2)
            link(dve.reciprocal(dinv[:, :], dinv[:, :]))
            link(dve.tensor_tensor(nodes(C), nodes(C), bc(dinv[:, :], D), MUL))
            dve.scalar_tensor_tensor(X[:, :], C[:, :], 0.0, X[:, :], MAX, ADD).then_inc(sem("out_ready"), 1)


def kernel(**inputs):
    import concourse.bacc as bacc
    from concourse.bass_utils import run_bass_kernel_spmd as run

    full = FULL * P
    k, n = np.arange(FREQ)[:, None], np.arange(D)[None, :]
    share = np.where((k == 0) | (k == D // 2), 1.0, 2.0) / D
    turn = 2 * np.pi * ((k * n) % D) / D
    cos, sin = np.cos(turn), np.where((k * n) % (D // 2) == 0, 0.0, np.sin(turn))
    fourier = np.stack([cos, sin, share * cos, share * sin], axis=1).astype(np.float32)

    def cols(a):
        return np.ascontiguousarray(np.asarray(a).reshape(-1)[:full].reshape(FULL, P).T)

    flat = {name: np.asarray(v) for name, v in inputs.items()}
    arrays = {
        "x": flat["x"], "src": flat["src"], "dst": flat["dst"], "etype": flat["edge_type_32"],
        "norm": flat["edge_weight1"].reshape(-1), "src_cols": cols(flat["src"]), "dst_cols": cols(flat["dst"]),
        "etype_cols": cols(flat["edge_type_32"]), "norm_cols": cols(flat["edge_weight1"]), "fourier": fourier,
        "w_fuse_t": np.ascontiguousarray(flat["L0_gnn_W_fuse"].T), "alpha": flat["L0_gnn_alpha"].reshape(1),
        "w_in": flat["L0_gnn_W_in"], "b_fuse": flat["L0_gnn_b_fuse"], "b_in": flat["L0_gnn_b_in"],
        "complex_weight": flat["L0_gnn_complex_weight"], "gamma": flat["L0_gnn_gamma"], "beta": flat["L0_gnn_beta"],
        "weight": flat["L1_gnn_weight"], "w_comp": flat["L1_gnn_w_comp"], "bias_param": flat["L1_gnn_bias_param"],
        "w_gat": flat["L2_gnn_W_gat"], "att_src": flat["L2_gnn_att_src"], "att_dst": flat["L2_gnn_att_dst"],
        "b_gat": flat["L2_gnn_b_gat"], "w1": flat["L2_gnn_W1"], "b1": np.ascontiguousarray(flat["L2_gnn_b1"].reshape(4, P).T),
        "w2": flat["L2_gnn_W2"], "b2": flat["L2_gnn_b2"], "ln1_g": flat["L2_gnn_ln1_g"], "ln1_b": flat["L2_gnn_ln1_b"],
        "ln2_g": flat["L2_gnn_ln2_g"], "ln2_b": flat["L2_gnn_ln2_b"],
    }
    nc = bacc.Bacc("TRN2", target_bir_lowering=False, num_devices=1)
    aps = {name: nc.dram_tensor(f"in_{name}", a.shape, mybir.dt.from_np(a.dtype), kind="ExternalInput").ap()
           for name, a in arrays.items()}
    out = nc.dram_tensor("out_x", (N_NODES, D), F32, kind="ExternalOutput").ap()
    build(nc, aps, out)
    r = run(nc, [{f"in_{name}": a for name, a in arrays.items()}], core_ids=[0])
    return r.results[0]["out_x"]
```
